# Optimizing a Trainium2 kernel written in Bass

```python
import numpy as np
import jax
import jax.numpy as jnp

def _softmax(x, axis=-1):
    return jax.nn.softmax(x, axis=axis)

def _gelu(x):
    return jax.nn.gelu(x, approximate=True)

def _silu(x):
    return jax.nn.silu(x)

def _sigmoid(x):
    return jax.nn.sigmoid(x)

def _layernorm(x, axis=-1, eps=1e-05):
    m = jnp.mean(x, axis=axis, keepdims=True)
    v = jnp.var(x, axis=axis, keepdims=True)
    return (x - m) / jnp.sqrt(v + eps)

def _scatter_add(tgt, idx, src, axis=0):
    return tgt.at[idx].add(src)

def _segment_sum(src, seg, n):
    return jax.ops.segment_sum(src, seg, n)
kernel_name = 'mk_seq_postln_d2_jaxref_r8_13f19a'

def setup_inputs(seed: int=0):
    np.random.seed(seed)
    _w = jnp.asarray

    def _L0_attn_setup():
        import jax, jax.numpy as jnp
        import numpy as np
        D_MODEL, N_HEADS = (128, 16)
        D_H = D_MODEL // N_HEADS
        D_HR = D_H // 2
        D_LATENT = 32
        THETA = 10000.0

        def rope(x, theta=THETA):
            S, d = (x.shape[-2], x.shape[-1])
            inv = theta ** (-jnp.arange(0, d, 2, dtype=jnp.float32) / d)
            ang = jnp.arange(S, dtype=jnp.float32)[:, None] * inv
            cos, sin = (jnp.cos(ang), jnp.sin(ang))
            x1, x2 = (x[..., 0::2], x[..., 1::2])
            r1 = x1 * cos - x2 * sin
            r2 = x1 * sin + x2 * cos
            return jnp.stack([r1, r2], axis=-1).reshape(x.shape)
        key = jax.random.key(seed)
        ks = jax.random.split(key, 9)
        s = lambda fan_in: 1.0 / np.sqrt(fan_in)
        return {'x': jax.random.normal(ks[0], (4, 256, D_MODEL), jnp.float32), 'W_DQ': jax.random.normal(ks[1], (D_MODEL, D_LATENT), jnp.float32) * s(D_MODEL), 'W_UQ': jax.random.normal(ks[2], (D_LATENT, N_HEADS * D_H), jnp.float32) * s(D_LATENT), 'W_QR': jax.random.normal(ks[3], (D_LATENT, N_HEADS * D_HR), jnp.float32) * s(D_LATENT), 'W_DKV': jax.random.normal(ks[4], (D_MODEL, D_LATENT), jnp.float32) * s(D_MODEL), 'W_UK': jax.random.normal(ks[5], (D_LATENT, N_HEADS * D_H), jnp.float32) * s(D_LATENT), 'W_UV': jax.random.normal(ks[6], (D_LATENT, N_HEADS * D_H), jnp.float32) * s(D_LATENT), 'W_KR': jax.random.normal(ks[7], (D_MODEL, D_HR), jnp.float32) * s(D_MODEL), 'W_O': jax.random.normal(ks[8], (N_HEADS * D_H, D_MODEL), jnp.float32) * s(N_HEADS * D_H)}
    _L0_attn_in = _L0_attn_setup()

    def _L0_ffn_setup():
        import jax, jax.numpy as jnp
        import numpy as np
        BEST_K = 2

        def _expert(xf, w1, w3, w2):
            return jax.nn.silu(xf @ w1) * (xf @ w3) @ w2
        key = jax.random.key(seed)
        ks = jax.random.split(key, 9)
        E, S_sh, D, H = (8, 2, 128, 64)
        B, S = (2, 256)
        w = lambda k, shape: jax.random.normal(k, shape, dtype=jnp.float32) * 0.02
        return {'x': jax.random.normal(ks[0], (B, S, D), dtype=jnp.float32), 'router_w': w(ks[1], (D, E)), 'router_b': jnp.zeros((E,), dtype=jnp.float32), 'routed_w1': w(ks[2], (E, D, H)), 'routed_w3': w(ks[3], (E, D, H)), 'routed_w2': w(ks[4], (E, H, D)), 'shared_w1': w(ks[5], (S_sh, D, H)), 'shared_w3': w(ks[6], (S_sh, D, H)), 'shared_w2': w(ks[7], (S_sh, H, D))}
    _L0_ffn_in = _L0_ffn_setup()

    def _L1_attn_setup():
        import math
        import jax, jax.numpy as jnp
        import numpy as np
        N, T, C = (4, 256, 128)
        H, HS = (16, 64)
        LAYER_ID, N_LAYERS = (1, 12)
        _EPS = math.exp(-LAYER_ID / N_LAYERS)
        EPS_R = _EPS / 2.0
        EPS_K = _EPS + 0.3 * LAYER_ID / (N_LAYERS - 1)
        EPS_V = _EPS

        def _time_interp(x, eps):
            Tn = x.shape[1]
            curr = jnp.pad(x, ((0, 0), (1, 0), (0, 0)))[:, :Tn]
            prev = jnp.pad(x, ((0, 0), (0, 1), (0, 0)))[:, 1:]
            return eps * curr + (1.0 - eps) * prev
        key = jax.random.key(seed)
        ks = jax.random.split(key, 9)
        s = 1.0 / math.sqrt(C)
        return {'x': jax.random.normal(ks[0], (N, T, C), dtype=jnp.float32), 'Wr': jax.random.normal(ks[1], (H * HS, C), dtype=jnp.float32) * s, 'br': jax.random.normal(ks[2], (H * HS,), dtype=jnp.float32) * 0.01, 'Wk': jax.random.normal(ks[3], (H * HS, C), dtype=jnp.float32) * s, 'bk': jax.random.normal(ks[4], (H * HS,), dtype=jnp.float32) * 0.01, 'Wv': jax.random.normal(ks[5], (H * HS, C), dtype=jnp.float32) * s, 'bv': jax.random.normal(ks[6], (H * HS,), dtype=jnp.float32) * 0.01, 'Wo': jax.random.normal(ks[7], (C, H * HS), dtype=jnp.float32) * s, 'bo': jax.random.normal(ks[8], (C,), dtype=jnp.float32) * 0.01, 'time_decay': jnp.full((H * HS,), 0.1, dtype=jnp.float32), 'U': jnp.full((H * HS,), 0.1, dtype=jnp.float32)}
    _L1_attn_in = _L1_attn_setup()

    def _L1_ffn_setup():
        import jax, jax.numpy as jnp
        import numpy as np
        H = 128
        I = 512
        E = 8
        TOPK = 2
        key = jax.random.key(seed)
        ks = jax.random.split(key, 6)
        B, S = (4, 256)
        hidden_states = jax.random.normal(ks[0], (B, S, H), dtype=jnp.float32)
        gate_w = jax.random.normal(ks[1], (H, E), dtype=jnp.float32) * (1.0 / np.sqrt(H))
        W1 = jax.random.normal(ks[2], (E, H, I), dtype=jnp.float32) * np.sqrt(2.0 / (H + I))
        W3 = jax.random.normal(ks[3], (E, H, I), dtype=jnp.float32) * np.sqrt(2.0 / (H + I))
        W2 = jax.random.normal(ks[4], (E, I, H), dtype=jnp.float32) * np.sqrt(2.0 / (H + I))
        dom = jax.random.normal(ks[5], (E, H), dtype=jnp.float32) * 0.02
        return {'hidden_states': hidden_states, 'gate_w': gate_w, 'W1': W1, 'W2': W2, 'W3': W3, 'dom': dom}
    _L1_ffn_in = _L1_ffn_setup()
    _d = {'L0_attn_x': _L0_attn_in['x'], 'L0_attn_W_DQ': _L0_attn_in['W_DQ'], 'L0_attn_W_UQ': _L0_attn_in['W_UQ'], 'L0_attn_W_QR': _L0_attn_in['W_QR'], 'L0_attn_W_DKV': _L0_attn_in['W_DKV'], 'L0_attn_W_UK': _L0_attn_in['W_UK'], 'L0_attn_W_UV': _L0_attn_in['W_UV'], 'L0_attn_W_KR': _L0_attn_in['W_KR'], 'L0_attn_W_O': _L0_attn_in['W_O'], 'L0_ffn_router_w': _L0_ffn_in['router_w'], 'L0_ffn_router_b': _L0_ffn_in['router_b'], 'L0_ffn_routed_w1': _L0_ffn_in['routed_w1'], 'L0_ffn_routed_w3': _L0_ffn_in['routed_w3'], 'L0_ffn_routed_w2': _L0_ffn_in['routed_w2'], 'L0_ffn_shared_w1': _L0_ffn_in['shared_w1'], 'L0_ffn_shared_w3': _L0_ffn_in['shared_w3'], 'L0_ffn_shared_w2': _L0_ffn_in['shared_w2'], 'L1_attn_Wr': _L1_attn_in['Wr'], 'L1_attn_br': _L1_attn_in['br'], 'L1_attn_Wk': _L1_attn_in['Wk'], 'L1_attn_bk': _L1_attn_in['bk'], 'L1_attn_Wv': _L1_attn_in['Wv'], 'L1_attn_bv': _L1_attn_in['bv'], 'L1_attn_Wo': _L1_attn_in['Wo'], 'L1_attn_bo': _L1_attn_in['bo'], 'L1_attn_time_decay': _L1_attn_in['time_decay'], 'L1_attn_U': _L1_attn_in['U'], 'L1_ffn_gate_w': _L1_ffn_in['gate_w'], 'L1_ffn_W1': _L1_ffn_in['W1'], 'L1_ffn_W2': _L1_ffn_in['W2'], 'L1_ffn_W3': _L1_ffn_in['W3'], 'L1_ffn_dom': _L1_ffn_in['dom']}
    _x0 = _d['L0_attn_x']
    _d['L0_attn_x'] = jax.random.normal(jax.random.fold_in(jax.random.key(seed), 1), (4, 512, 128), dtype=_x0.dtype)
    del _x0
    return _d

def reference(L0_attn_x, L0_attn_W_DQ, L0_attn_W_UQ, L0_attn_W_QR, L0_attn_W_DKV, L0_attn_W_UK, L0_attn_W_UV, L0_attn_W_KR, L0_attn_W_O, L0_ffn_router_w, L0_ffn_router_b, L0_ffn_routed_w1, L0_ffn_routed_w3, L0_ffn_routed_w2, L0_ffn_shared_w1, L0_ffn_shared_w3, L0_ffn_shared_w2, L1_attn_Wr, L1_attn_br, L1_attn_Wk, L1_attn_bk, L1_attn_Wv, L1_attn_bv, L1_attn_Wo, L1_attn_bo, L1_attn_time_decay, L1_attn_U, L1_ffn_gate_w, L1_ffn_W1, L1_ffn_W2, L1_ffn_W3, L1_ffn_dom):

    def _L0_attn_ref(x, W_DQ, W_UQ, W_QR, W_DKV, W_UK, W_UV, W_KR, W_O):
        import jax, jax.numpy as jnp
        import numpy as np
        D_MODEL, N_HEADS = (128, 16)
        D_H = D_MODEL // N_HEADS
        D_HR = D_H // 2
        D_LATENT = 32
        THETA = 10000.0

        def rope(x, theta=THETA):
            S, d = (x.shape[-2], x.shape[-1])
            inv = theta ** (-jnp.arange(0, d, 2, dtype=jnp.float32) / d)
            ang = jnp.arange(S, dtype=jnp.float32)[:, None] * inv
            cos, sin = (jnp.cos(ang), jnp.sin(ang))
            x1, x2 = (x[..., 0::2], x[..., 1::2])
            r1 = x1 * cos - x2 * sin
            r2 = x1 * sin + x2 * cos
            return jnp.stack([r1, r2], axis=-1).reshape(x.shape)
        B, S, _ = x.shape
        d_qk = D_H + D_HR
        c_q = x @ W_DQ
        Qc = (c_q @ W_UQ).reshape(B, S, N_HEADS, D_H).transpose(0, 2, 1, 3)
        Qr = (c_q @ W_QR).reshape(B, S, N_HEADS, D_HR).transpose(0, 2, 1, 3)
        Qr = rope(Qr)
        c_kv = x @ W_DKV
        Kc = (c_kv @ W_UK).reshape(B, S, N_HEADS, D_H).transpose(0, 2, 1, 3)
        Kr = rope((x @ W_KR)[:, None, :, :])
        Kr = jnp.broadcast_to(Kr, (B, N_HEADS, S, D_HR))
        V = (c_kv @ W_UV).reshape(B, S, N_HEADS, D_H).transpose(0, 2, 1, 3)
        Q = jnp.concatenate([Qc, Qr], axis=-1)
        K = jnp.concatenate([Kc, Kr], axis=-1)
        scores = jnp.einsum('bhqd,bhkd->bhqk', Q, K)
        scores = jnp.clip(scores, -80.0, 80.0)
        causal = jnp.tril(jnp.ones((S, S), dtype=bool))
        scores = jnp.where(causal, scores, -jnp.inf)
        weights = jax.nn.softmax(scores / jnp.sqrt(jnp.float32(d_qk)), axis=-1)
        attn = jnp.einsum('bhqk,bhkd->bhqd', weights, V)
        attn = attn.transpose(0, 2, 1, 3).reshape(B, S, N_HEADS * D_H)
        return attn @ W_O

    def _L0_ffn_ref(x, router_w, router_b, routed_w1, routed_w3, routed_w2, shared_w1, shared_w3, shared_w2):
        import jax, jax.numpy as jnp
        import numpy as np
        BEST_K = 2

        def _expert(xf, w1, w3, w2):
            return jax.nn.silu(xf @ w1) * (xf @ w3) @ w2
        B, S, D = x.shape
        T = B * S
        xf = x.reshape(T, D)
        logits = xf @ router_w + router_b
        topk_vals, topk_idx = jax.lax.top_k(logits, BEST_K)
        sparse = jnp.full_like(logits, -jnp.inf)
        sparse = sparse.at[jnp.arange(T)[:, None], topk_idx].set(topk_vals)
        gates = jax.nn.softmax(sparse, axis=-1)
        routed = jax.vmap(_expert, in_axes=(None, 0, 0, 0))(xf, routed_w1, routed_w3, routed_w2)
        routed_out = jnp.einsum('etd,te->td', routed, gates)
        shared_out = jax.vmap(_expert, in_axes=(None, 0, 0, 0))(xf, shared_w1, shared_w3, shared_w2).sum(axis=0)
        return (routed_out + shared_out).reshape(B, S, D)

    def _L1_attn_ref(x, Wr, br, Wk, bk, Wv, bv, Wo, bo, time_decay, U):
        import math
        import jax, jax.numpy as jnp
        import numpy as np
        N, T, C = (4, 256, 128)
        H, HS = (16, 64)
        LAYER_ID, N_LAYERS = (1, 12)
        _EPS = math.exp(-LAYER_ID / N_LAYERS)
        EPS_R = _EPS / 2.0
        EPS_K = _EPS + 0.3 * LAYER_ID / (N_LAYERS - 1)
        EPS_V = _EPS

        def _time_interp(x, eps):
            Tn = x.shape[1]
            curr = jnp.pad(x, ((0, 0), (1, 0), (0, 0)))[:, :Tn]
            prev = jnp.pad(x, ((0, 0), (0, 1), (0, 0)))[:, 1:]
            return eps * curr + (1.0 - eps) * prev
        n, t, c = x.shape
        R = (_time_interp(x, EPS_R) @ Wr.T + br).reshape(n, t, H, HS)
        K = (_time_interp(x, EPS_K) @ Wk.T + bk).reshape(n, t, H, HS)
        V = (_time_interp(x, EPS_V) @ Wv.T + bv).reshape(n, t, H, HS)
        w = jax.nn.relu(time_decay).reshape(1, 1, H, HS)
        t_rem = (t - jnp.arange(1, t + 1, dtype=x.dtype)).reshape(1, t, 1, 1)
        W = -w * t_rem
        e = jnp.exp(jnp.clip(W + K, -20.0, 10.0))
        past_attention = jnp.cumsum(e * V, axis=1)
        past_energy = jnp.cumsum(e, axis=1)
        shift = lambda a: jnp.pad(a, ((0, 0), (1, 0), (0, 0), (0, 0)))[:, :t]
        eu = jnp.exp(jnp.clip(U.reshape(1, 1, H, HS) + K, -20.0, 10.0))
        A = shift(past_attention) + eu * V
        B = shift(past_energy) + eu
        WKV = A / B
        out = (jax.nn.sigmoid(R) * WKV).reshape(n, t, -1) @ Wo.T + bo
        return out

    def _L1_ffn_ref(hidden_states, gate_w, W1, W2, W3, dom):
        import jax, jax.numpy as jnp
        import numpy as np
        H = 128
        I = 512
        E = 8
        TOPK = 2
        B, S, Hd = hidden_states.shape
        x = hidden_states.reshape(-1, Hd)
        router_logits = x @ gate_w
        top_logits, top_idx = jax.lax.top_k(router_logits, TOPK)
        weights = jax.nn.softmax(top_logits, axis=-1)
        w_dense = jnp.einsum('tk,tke->te', weights, jax.nn.one_hot(top_idx, E, dtype=weights.dtype))
        out = jnp.zeros_like(x)
        for e in range(E):
            xe = x + dom[e]
            h = jax.nn.silu(xe @ W1[e]) * (xe @ W3[e])
            out = out + w_dense[:, e:e + 1] * (h @ W2[e])
        return out.reshape(B, S, Hd)
    x = L0_attn_x
    x = _layernorm(x + _L0_attn_ref(x, L0_attn_W_DQ, L0_attn_W_UQ, L0_attn_W_QR, L0_attn_W_DKV, L0_attn_W_UK, L0_attn_W_UV, L0_attn_W_KR, L0_attn_W_O), axis=-1)
    x = _layernorm(x + _L0_ffn_ref(x, L0_ffn_router_w, L0_ffn_router_b, L0_ffn_routed_w1, L0_ffn_routed_w3, L0_ffn_routed_w2, L0_ffn_shared_w1, L0_ffn_shared_w3, L0_ffn_shared_w2), axis=-1)
    x = _layernorm(x + _L1_attn_ref(x, L1_attn_Wr, L1_attn_br, L1_attn_Wk, L1_attn_bk, L1_attn_Wv, L1_attn_bv, L1_attn_Wo, L1_attn_bo, L1_attn_time_decay, L1_attn_U), axis=-1)
    x = _layernorm(x + _L1_ffn_ref(x, L1_ffn_gate_w, L1_ffn_W1, L1_ffn_W2, L1_ffn_W3, L1_ffn_dom), axis=-1)
    return x

_drawn_inputs = setup_inputs


def setup_inputs(seed=0):
    import zlib

    import numpy as np

    out = dict(_drawn_inputs(seed))
    spreads = {'L0_ffn_router_b': (0.0, 0.8),
     'L1_attn_time_decay': (0.10000000149011612, 0.2),
     'L1_attn_U': (0.10000000149011612, 0.6)}
    factors = {'L0_ffn_router_w': 6.415,
     'L0_ffn_routed_w1': 5.549,
     'L0_ffn_routed_w3': 6.345,
     'L0_ffn_routed_w2': 6.904,
     'L0_ffn_shared_w1': 4.337,
     'L0_ffn_shared_w3': 4.684,
     'L0_ffn_shared_w2': 4.417,
     'L1_attn_br': 6.386,
     'L1_attn_bk': 8.0,
     'L1_attn_bv': 3.107,
     'L1_attn_bo': 5.756,
     'L1_ffn_dom': 8.0}
    for name, (base, spread) in spreads.items():
        noise = np.random.default_rng([zlib.crc32(name.encode()), seed]).standard_normal(out[name].shape)
        drawn = base * np.exp(spread * noise) if base else spread * noise
        out[name] = jnp.asarray(drawn.astype(out[name].dtype))
    for name, factor in factors.items():
        out[name] = (out[name] * factor).astype(out[name].dtype)
    return out
```

```python
import math
from contextlib import ExitStack

import numpy as np

import concourse.bass as bass
from concourse import mybir

F32 = mybir.dt.float32
BF16 = mybir.dt.bfloat16
U32 = mybir.dt.uint32
ALU = mybir.AluOpType
ACT = mybir.ActivationFunctionType

B, S, D = 4, 512, 128
P = 128
TB = S // P
H, DH, DR, DL = 16, 8, 4, 32
DQK = DH + DR
E8 = 8
HID0, SH0 = 64, 2
PAIRS = (E8 + SH0) * HID0 // P
RP = E8 * HID0 // P
CH = 1024
CT = CH // P
HID1 = 512
FT = HID1 // P
LN_EPS = 1e-5
THETA = 10000.0

LAYER_ID, N_LAYERS = 1, 12
_EPS = math.exp(-LAYER_ID / N_LAYERS)
MIX = {"k": _EPS + 0.3 * LAYER_ID / (N_LAYERS - 1), "v": _EPS, "r": _EPS / 2.0}

QK_SCALE = 1.0 / math.sqrt(DQK)
P_MIN, P_MAX = math.exp(-80.0 * QK_SCALE), math.exp(80.0 * QK_SCALE)
E_MIN, E_MAX = math.exp(-20.0), math.exp(10.0)

Q_PART = (0, 1, 2, 0, 1, 0)
K_PART = (0, 0, 0, 1, 1, 2)
STACK = len(Q_PART) * DQK

def runs(order):
    out, at = [], 0
    while at < len(order):
        n = 1
        while at + n < len(order) and order[at + n] == order[at] + n:
            n += 1
        out.append((at, n))
        at += n
    return out


STACK_DMAS = len(runs(Q_PART)) + len(runs(K_PART))


KB_AT = (0, 512, 1024, 896)
KB_LEN = tuple(S - P * kb for kb in range(TB))
SC = 1280


class Steps:

    def __init__(self, eng, sem, first, total):
        self.eng, self.sem, self.first, self.total, self.n = eng, sem, first, total, 0

    def did(self, ins):
        ins.then_inc(self.sem, 1)
        self.n += 1

    def settle(self):
        self.eng.wait_ge(self.sem, self.first + self.n)

    def close(self):
        assert self.n == self.total, (self.n, self.total)


def network(nc, a, out):
    top = ExitStack()
    with top:
        def sb(name, shape, dt=F32, ctx=top):
            return ctx.enter_context(nc.sbuf_tensor(name, shape, dt))

        def sem(name):
            return top.enter_context(nc.semaphore(name))

        x_tok = sb("x_tok", [P, B * TB, D])
        x_feat = sb("x_feat", [P, B * S])
        x_pad = sb("x_pad", [P, B, S + 2])
        xn = sb("xn", [P, TB, D])
        x_sum = sb("x_sum", [P, TB, D])
        x_cur = sb("x_cur", [P, S])
        stats = sb("stats", [P, TB, 6])
        mv = sb("mv", [P, TB, 2])
        var_e = sb("var_e", [P, TB])
        rstd = sb("rstd", [P, TB])
        m_half = sb("m_half", [P, TB])
        ident = sb("ident", [P, P])
        iota8 = sb("iota8", [P, TB * E8])
        lg = sb("lg", [P, TB, E8])
        mx = sb("mx", [P, TB, 8])
        mi = sb("mi", [P, TB, 8], U32)
        mif = sb("mif", [P, 2, TB])
        mdiff = sb("mdiff", [P, TB])
        tg = sb("tg", [P, TB])
        g1 = sb("g1", [P, TB])
        g2 = sb("g2", [P, TB])
        oh1 = sb("oh1", [P, TB, E8])
        oh2 = sb("oh2", [P, TB, E8])
        gates = sb("gates", [P, TB, E8])
        w_o = sb("w_o", [P, D])
        r0_w = sb("r0_w", [P, E8])
        r0_b = sb("r0_b", [P, TB * E8])
        w1_0 = sb("w1_0", [P, PAIRS, P])
        w3_0 = sb("w3_0", [P, PAIRS, P])
        w2_0 = sb("w2_0", [P, PAIRS, D])
        pair_sel = sb("pair_sel", [E8, RP, P])
        w_rwkv = {q: sb(f"w_{q}", [P, CH]) for q in "kvr"}
        w_out = sb("w_out", [P, CT, D])
        cols = sb("cols", [P, 5, CT])
        bo = sb("bo", [P, TB, D])
        trem = sb("trem", [P, S])
        g_w = sb("g_w", [P, E8])
        dom = sb("dom", [P, E8])

        tail = top.enter_context(nc.psum_tensor("tail", [P, S], F32))
        pv = top.enter_context(nc.psum_tensor("pv", [P, S], F32))
        sc = [top.enter_context(nc.psum_tensor(f"sc{u}", [P, 3 * S], F32)) for u in range(2)]
        bank = [sc[k // 3][:, (k % 3) * S:(k % 3 + 1) * S] for k in range(6)]

        q_split = nc.dram_tensor("q_split", [B, 3, DQK * H, S], BF16).ap()
        k_split = nc.dram_tensor("k_split", [B, 3, DQK * H, S], BF16).ap()

        ld_attn, ld_x = sem("ld_attn"), sem("ld_x")
        ld_xf = [sem(f"ld_xf{b}") for b in range(B)]
        ld_ffn0, ld_rwkv, ld_ffn1 = sem("ld_ffn0"), sem("ld_rwkv"), sem("ld_ffn1")
        split_stored = [sem(f"split_stored{b}") for b in range(B)]
        stack_loaded = [sem(f"stack_loaded{u}") for u in range(2)]
        const_ready = sem("const_ready")
        v_const = sem("v_const")
        fold_mm, fold_ready = sem("fold_mm"), sem("fold_ready")
        qc_mm, kc_mm, rope_mm, v_mm = sem("qc_mm"), sem("kc_mm"), sem("rope_mm"), sem("v_mm")
        rope_ready, rot_ready = sem("rope_ready"), sem("rot_ready")
        part0_ready, res_ready = sem("part0_ready"), sem("res_ready")
        part1_ready, part2_ready = sem("part1_ready"), sem("part2_ready")
        v_stored = sem("v_stored")
        v_cur_ready = sem("v_cur_ready")
        scores_ready, exp_ready, probs_ready, pv_ready = (sem(n) for n in ("scores_ready", "exp_ready", "probs_ready", "pv_ready"))
        pv_read = sem("pv_read")
        tail_full = {n: sem(f"tail_full{n}") for n in range(1, 5)}
        tail_read = {n: sem(f"tail_read{n}") for n in range(1, 5)}
        step = {n: sem(f"dve_step{n}") for n in range(1, 5)}
        var_ready = {n: sem(f"var_ready{n}") for n in range(1, 5)}
        rstd_ready = {n: sem(f"rstd_ready{n}") for n in range(1, 5)}
        xn_ready = {n: sem(f"xn_ready{n}") for n in range(1, 5)}
        tok_stored = {n: sem(f"tok_stored{n}") for n in range(1, 5)}
        cur_ready = {n: sem(f"cur_ready{n}") for n in (2, 4)}
        diff_ready = {n: sem(f"diff_ready{n}") for n in (2, 4)}
        tanh_ready = {n: sem(f"tanh_ready{n}") for n in (2, 4)}
        gates_ready = {n: sem(f"gates_ready{n}") for n in (2, 4)}
        h1_ready = {n: sem(f"h1_ready{n}") for n in (2, 4)}
        h3_ready = {n: sem(f"h3_ready{n}") for n in (2, 4)}
        silu_ready = {n: sem(f"silu_ready{n}") for n in (2, 4)}
        hid_ready = {n: sem(f"hid_ready{n}") for n in (2, 4)}
        gt_ready, gb_ready, gs_ready = sem("gt_ready"), sem("gb_ready"), sem("gs_ready")
        down_ready = {n: sem(f"down_ready{n}") for n in (2, 4)}
        mix_ready, k_ready, v_ready, r_ready = (sem(n) for n in ("mix_ready", "k_ready", "v_ready", "r_ready"))
        karg_ready, eu0_ready, vb_ready, th_ready, e0_ready = (sem(n) for n in ("karg_ready", "eu0_ready", "vb_ready", "th_ready", "e0_ready"))
        eu_ready, euv_ready, den_ready, e_ready, ev_ready, sb_ready = (sem(n) for n in ("eu_ready", "euv_ready", "den_ready", "e_ready", "ev_ready", "sb_ready"))
        lnb_ready, inv_ready, y_ready, wtab_ready, wout_ready, num_ready, mixed, setup, gated_ready = (
            sem(n) for n in ("lnb_ready", "inv_ready", "y_ready", "wtab_ready", "wout_ready", "num_ready", "mixed", "setup", "gated_ready"))
        xe_ready, acc_ready = sem("xe_ready"), sem("acc_ready")
        out_stored = sem("out_stored")

        def wait_apart(eng, semaphore, count):
            count = eng.to_reg(count)
            eng.wait_ge(const_ready, 3)
            eng.wait_ge(semaphore, count)

        def residual_on_vector(dve, n, b, use):
            dve.wait_ge(tail_full[n], b * TAIL_USES[n] + use + 1)
            nc.vector.tensor_tensor(x_sum[:, :, :], tail[:, :].rearrange("p (t d) -> p t d", t=TB),
                                    x_tok[:, bass.ds(b * TB, TB), :], ALU.add).then_inc(tail_read[n], 1)
            dve.wait_ge(tail_read[n], b * TAIL_USES[n] + use + 1)

        def norm_on_vector(dve, n, b, steps):
            for t in range(TB):
                steps.did(nc.vector.bn_stats(stats[:, t, :], x_sum[:, t, :]))
            wait_apart(dve, steps.sem, steps.first + steps.n)
            for t in range(TB):
                steps.did(nc.vector.bn_aggr(mv[:, t, :], stats[:, t, :]))
            steps.settle()
            nc.vector.tensor_scalar(var_e[:, :], mv[:, :, 1], LN_EPS, None, ALU.add).then_inc(var_ready[n], 1)
            dve.wait_ge(rstd_ready[n], b + 1)
            if n < 4:
                dve.wait_ge(tail_full[n], b * TAIL_USES[n])
                dve.wait_ge(tok_stored[n], b)
            else:
                dve.wait_ge(out_stored, b * 16)
            for t in range(TB):
                ins = nc.vector.tensor_scalar(xn[:, t, :], x_sum[:, t, :], mv[:, t, 0:1], rstd[:, t:t + 1],
                                              ALU.subtract, ALU.mult)
                if t < TB - 1:
                    steps.did(ins)
            ins.then_inc(xn_ready[n], 1)
        NORM_STEPS = 2 * TB + (TB - 1)
        TAIL_USES = {1: TB + 3, 2: 4, 3: 2, 4: 1}

        def norm_on_pool(pool, n, b):
            pool.wait_ge(var_ready[n], b + 1)
            nc.gpsimd.tensor_tensor(rstd[:, :], var_e[:, :], m_half[:, :], ALU.pow).then_inc(rstd_ready[n], 1)
            if n < 4:
                pool.wait_ge(xn_ready[n], b + 1)
                nc.gpsimd.tensor_copy(x_tok[:, bass.ds(b * TB, TB), :], xn[:, :, :]).then_inc(tok_stored[n], 1)

        def turn_norm_on_tensor(pe, n, b, use):
            pe.wait_ge(xn_ready[n], b + 1)
            pe.wait_ge(tail_read[n], b * TAIL_USES[n] + use)
            for t in range(TB):
                ins = pe.transpose(tail[:, t * P:(t + 1) * P], xn[:, t, :], ident[:, :])
            ins.then_inc(tail_full[n], 1)

        def router_on_tensor(pe, n, b, w):
            pe.wait_ge(cur_ready[n], b + 1)
            pe.wait_ge(tail_read[n], b * TAIL_USES[n])
            for t in range(TB):
                ins = pe.matmul(tail[:, t * E8:(t + 1) * E8], x_cur[:, t * P:(t + 1) * P], w[:, :],
                                start=True, stop=True)
            ins.then_inc(tail_full[n], 1)

        def router_on_vector(dve, n, b, steps, bias):
            dve.wait_ge(tail_full[n], b * TAIL_USES[n] + 1)
            src = tail[:, 0:TB * E8]
            dst = lg[:, :, :].rearrange("p t e -> p (t e)")
            if bias is None:
                nc.vector.tensor_copy(dst, src).then_inc(tail_read[n], 1)
            else:
                nc.vector.tensor_tensor(dst, src, bias, ALU.add).then_inc(tail_read[n], 1)
            wait_apart(dve, tail_read[n], b * TAIL_USES[n] + 1)
            for t in range(TB):
                steps.did(nc.vector.max(mx[:, t, :], lg[:, t, :]))
            wait_apart(dve, steps.sem, steps.first + steps.n)
            for t in range(TB):
                steps.did(nc.vector.max_index(mi[:, t, :], mx[:, t, :], lg[:, t, :]))
            nc.vector.tensor_tensor(mdiff[:, :], mx[:, :, 0], mx[:, :, 1], ALU.subtract).then_inc(diff_ready[n], 1)
            steps.settle()
            steps.did(nc.vector.tensor_copy(mif[:, :, :].rearrange("p k t -> p t k"), mi[:, :, 0:2]))
            steps.settle()
            io = iota8[:, :].rearrange("p (t e) -> p t e", t=TB)
            for k, oh in enumerate((oh1, oh2)):
                steps.did(nc.vector.tensor_tensor(
                    oh[:, :, :], io, mif[:, k, :].unsqueeze(2).to_broadcast([P, TB, E8]), ALU.is_equal))
            dve.wait_ge(tanh_ready[n], b + 1)
            steps.did(nc.vector.tensor_scalar(g1[:, :], tg[:, :], 0.5, 0.5, ALU.mult, ALU.add))
            steps.did(nc.vector.tensor_scalar(g2[:, :], tg[:, :], -0.5, 0.5, ALU.mult, ALU.add))
            steps.settle()
            for oh, g in ((oh1, g1), (oh2, g2)):
                steps.did(nc.vector.tensor_tensor(oh[:, :, :], oh[:, :, :],
                                                  g[:, :].unsqueeze(2).to_broadcast([P, TB, E8]), ALU.mult))
            steps.settle()
            nc.vector.tensor_tensor(gates[:, :, :], oh1[:, :, :], oh2[:, :, :], ALU.add).then_inc(gates_ready[n], 1)
            dve.wait_ge(gates_ready[n], b + 1)
        ROUTER_STEPS = 2 * TB + 1 + 2 + 2 + 2

        def router_on_scalar(act, n, b):
            act.wait_ge(diff_ready[n], b + 1)
            nc.scalar.activation(tg[:, :], mdiff[:, :], ACT.Tanh, scale=0.5).then_inc(tanh_ready[n], 1)

        with ExitStack() as one:
            wdq = sb("wdq", [DL, D], ctx=one)
            wdkv = sb("wdkv", [DL, D], ctx=one)
            wuq = sb("wuq", [DL, 2 * P], ctx=one)
            wukv = sb("wukv", [DL, 2 * P], ctx=one)
            f_q = sb("f_q", [P, P], ctx=one)
            f_k = sb("f_k", [P, P], ctx=one)
            f_v = sb("f_v", [P, P], ctx=one)
            f_ra = sb("f_ra", [P, P], ctx=one)
            f_rb = sb("f_rb", [P, P], ctx=one)
            cos = sb("cos", [P, S], ctx=one)
            sin = sb("sin", [P, S], ctx=one)
            tri = sb("tri", [P, 2 * P], ctx=one)
            ra = sb("ra", [P, S], ctx=one)
            rb = sb("rb", [P, S], ctx=one)
            rot = sb("rot", [P, S], ctx=one)
            res = [sb(f"res{k}", [P, S], ctx=one) for k in range(3)]
            part = [[sb(f"part{u}{k}", [P, 3, S], BF16, ctx=one) for k in range(3)] for u in range(2)]
            v_all = sb("v_all", [P, B * TB, D], ctx=one)
            v_cur = sb("v_cur", [P, TB, H, 32], ctx=one)
            q_st = [sb(f"q_st{u}", [STACK, H, S], BF16, ctx=one) for u in range(2)]
            k_st = [sb(f"k_st{u}", [STACK, H, S], BF16, ctx=one) for u in range(2)]
            probs = [sb(f"probs{u}", [P, SC], ctx=one) for u in range(2)]
            o_feat = sb("o_feat", [P, S], ctx=one)
            rden = sb("rden", [P, TB, 4], ctx=one)
            o_tok = sb("o_tok", [P, TB, D], ctx=one)
            o_t = sb("o_t", [P, S], ctx=one)
            ATT_STEPS = 2 * H + 4 + NORM_STEPS

            block = one.enter_context(nc.Block())

            @block.sync
            def _(sp):
                attn_loads = ((wdq[:, :], a["wdq"]), (wdkv[:, :], a["wdkv"]), (wuq[:, :], a["wuq"]),
                              (wukv[:, :], a["wukv"]), (f_ra[:, P // 2:], a["wkr_a"]), (f_rb[:, P // 2:], a["wkr_b"]))
                for dst, src in attn_loads:
                    sp.dma_start(dst, src).then_inc(ld_attn, 16)
                for b in range(B):
                    sp.dma_start(x_feat[:, b * S:(b + 1) * S], a["x_feat"][:, b * S:(b + 1) * S]).then_inc(ld_xf[b], 16)
                    if b == 0:
                        sp.dma_start(cos[:, :], a["cos"]).then_inc(ld_attn, 16)
                        sp.dma_start(sin[:, :], a["sin"]).then_inc(ld_attn, 16)
                for dst, src in ((w_o[:, :], a["w_o"]), (ident[:, :], a["ident"]), (tri[:, :], a["tri"]),
                                 (iota8[:, :], a["iota8"])):
                    sp.dma_start(dst, src).then_inc(ld_x, 16)
                sp.dma_start(x_tok[:, :, :], a["x_tok"].rearrange("(n p) d -> p n d", p=P)).then_inc(ld_x, 16)
                for b in range(B):
                    u = b % 2
                    sp.wait_ge(part2_ready, 3 * b + 3)
                    sp.wait_ge(part1_ready, 3 * b + 3)
                    sp.wait_ge(part0_ready, 3 * b + 3)
                    c = DH * H
                    for dram, k, lo in ((q_split, 0, 0), (k_split, 1, P // 2)):
                        rows = dram[b].rearrange("s r c -> r s c")
                        sp.dma_start(rows[0:c], part[u][k][:, :, :]).then_inc(split_stored[b], 16)
                        sp.dma_start(rows[c:], part[u][2][lo:lo + P // 2, :, :]).then_inc(split_stored[b], 16)
                    sp.wait_ge(split_stored[b], 4 * 16)
                    if b >= 2:
                        sp.wait_ge(scores_ready, H * (b - 1))
                    for dst, dram, order in ((q_st[u], q_split, Q_PART), (k_st[u], k_split, K_PART)):
                        rows = dram[b].rearrange("s (k h) c -> (s k) h c", h=H)
                        for at, n in runs(order):
                            sp.dma_start(dst[at * DQK:(at + n) * DQK, :, :],
                                         rows[order[at] * DQK:(order[at] + n) * DQK]).then_inc(stack_loaded[u], 16)
                for dst, src in ((r0_w[:, :], a["r0_w"]), (r0_b[:, :], a["r0_b"]), (w1_0[:, :, :], a["w1_0"]),
                                 (w3_0[:, :, :], a["w3_0"]), (w2_0[:, :, :], a["w2_0"]), (pair_sel[:, :, :], a["pair_sel"])):
                    sp.dma_start(dst, src).then_inc(ld_ffn0, 16)
                for dst, src in ((w_rwkv["k"][:, :], a["wk"]), (w_rwkv["v"][:, :], a["wv"]), (w_rwkv["r"][:, :], a["wr"]),
                                 (w_out[:, :, :], a["w_out"]), (cols[:, :, :], a["cols"]), (bo[:, :, :], a["bo"]),
                                 (trem[:, :], a["trem"])):
                    sp.dma_start(dst, src).then_inc(ld_rwkv, 16)
                for dst, src in ((g_w[:, :], a["g_w"]), (dom[:, :], a["dom"])):
                    sp.dma_start(dst, src).then_inc(ld_ffn1, 16)

            @block.gpsimd
            def _(pool):
                nc.gpsimd.memset(v_cur[:, :, :, :], 0.0).then_inc(v_const, 1)
                pool.wait_ge(v_const, 1)
                nc.gpsimd.memset(v_cur[:, :, :, DH:DH + 1], 1.0).then_inc(v_const, 1)
                nc.gpsimd.memset(m_half[:, :], -0.5).then_inc(const_ready, 1)
                nc.gpsimd.memset(x_pad[:, :, 0:1], 0.0).then_inc(const_ready, 1)
                nc.gpsimd.memset(x_pad[:, :, S + 1:S + 2], 0.0).then_inc(const_ready, 1)
                for b in range(B):
                    u = b % 2
                    pool.wait_ge(rope_ready, 2 * b + 2)
                    pool.wait_ge(res_ready, 3 * b)
                    pool.wait_ge(part0_ready, 3 * b)
                    nc.gpsimd.tensor_tensor(rot[:, :], ra[:, :], rb[:, :], ALU.add).then_inc(rot_ready, 1)
                    for k in range(3):
                        pool.wait_ge(part1_ready, 3 * b + k + 1)
                        nc.gpsimd.tensor_tensor(part[u][k][:, 2, :], res[k][:, :], part[u][k][:, 1, :], ALU.subtract)\
                            .then_inc(part2_ready, 1)
                pool.wait_ge(const_ready, 3)
                with pool.Fori(0, B // 2) as pair:
                    for u in range(2):
                        b = pair * 2 + u
                        pool.wait_ge(v_stored, B)
                        pool.wait_ge(v_const, 2)
                        pool.wait_ge(pv_ready, b * H)
                        nc.gpsimd.tensor_copy(v_cur[:, :, :, 0:DH],
                                              v_all[:, bass.ds(b * TB, TB), :].rearrange("p t (h d) -> p t h d", h=H))\
                            .then_inc(v_cur_ready, 1)
                        norm_on_pool(pool, 1, b)

            @block.tensor
            def _(pe):
                pe.wait_ge(ld_attn, 8 * 16)
                pe.matmul(bank[0][:, 0:2 * P], wdq[:, :], wuq[:, :], start=True, stop=True).then_inc(fold_mm, 1)
                pe.matmul(bank[1][:, 0:2 * P], wdkv[:, :], wukv[:, :], start=True, stop=True).then_inc(fold_mm, 1)
                pe.wait_ge(fold_ready, 5)
                for b in range(B):
                    x = x_feat[:, b * S:(b + 1) * S]
                    pe.wait_ge(ld_xf[b], 16)
                    pe.wait_ge(res_ready, 3 * b)
                    pe.matmul(bank[0], f_q[:, :], x, start=True, stop=True).then_inc(qc_mm, 1)
                    pe.matmul(bank[1], f_k[:, :], x, start=True, stop=True).then_inc(kc_mm, 1)
                    pe.wait_ge(rope_ready, 2 * b)
                    pe.matmul(bank[2], f_ra[:, :], x, start=True, stop=True).then_inc(rope_mm, 1)
                    pe.matmul(bank[3], f_rb[:, :], x, start=True, stop=True).then_inc(rope_mm, 1)
                    pe.wait_ge(v_stored, b)
                    for t in range(TB):
                        ins = pe.matmul(bank[4][:, t * P:(t + 1) * P], x[:, t * P:(t + 1) * P], f_v[:, :],
                                        start=True, stop=True)
                    ins.then_inc(v_mm, 1)
                pe.wait_ge(part0_ready, 3 * B)
                pe.wait_ge(rope_ready, 2 * B)
                pe.wait_ge(res_ready, 3 * B)
                pe.wait_ge(v_stored, B)
                pe.wait_ge(ld_x, 5 * 16)

                with pe.Fori(0, B // 2) as pair:
                    for u in range(2):
                        b = pair * 2 + u
                        tails = b * TAIL_USES[1]

                        def scores(h):
                            w = h % 2
                            pe.wait_ge(exp_ready, b * H + max(h - 1, 0))
                            for kb in range(TB):
                                ins = pe.matmul(sc[w][:, KB_AT[kb]:KB_AT[kb] + KB_LEN[kb]],
                                                k_st[u][:, h, kb * P:(kb + 1) * P], q_st[u][:, h, kb * P:S],
                                                start=True, stop=True)
                            ins.then_inc(scores_ready, 1)

                        def values(h):
                            j = h % 4
                            pe.wait_ge(probs_ready, b * H + h + 1)
                            if j == 0:
                                pe.wait_ge(pv_read, b * 4 + h // 4)
                            for kb in range(TB):
                                ins = pe.matmul(pv[32 * j:32 * j + 32, kb * P:S], v_cur[:, kb, h, :],
                                                probs[h % 2][:, KB_AT[kb]:KB_AT[kb] + KB_LEN[kb]],
                                                start=(kb == 0), stop=(kb == TB - 1))
                            ins.then_inc(pv_ready, 1)

                        def turn_group(g):
                            pe.wait_ge(pv_read, b * 4 + g + 1)
                            pe.wait_ge(tail_read[1], tails + g)
                            for t in range(TB):
                                ins = pe.transpose(tail[:, t * P:(t + 1) * P], o_feat[:, t * P:(t + 1) * P], ident[:, :])
                            ins.then_inc(tail_full[1], 1)

                        pe.wait_ge(stack_loaded[u], (pair + 1) * (16 * STACK_DMAS))
                        pe.wait_ge(v_cur_ready, b + 1)
                        scores(0)
                        for h in range(1, H + 1):
                            if h < H:
                                scores(h)
                            if h > 4 and h % 4 == 1:
                                turn_group(h // 4 - 1)
                            values(h - 1)
                        turn_group(3)
                        pe.wait_ge(tail_read[1], tails + 4)
                        for t in range(TB):
                            ins = pe.transpose(tail[:, t * P:(t + 1) * P], o_tok[:, t, :], ident[:, :])
                        ins.then_inc(tail_full[1], 1)
                        pe.wait_ge(tail_read[1], tails + 5)
                        for t in range(TB):
                            ins = pe.matmul(tail[:, t * P:(t + 1) * P], o_t[:, t * P:(t + 1) * P], w_o[:, :],
                                            start=True, stop=True)
                        ins.then_inc(tail_full[1], 1)
                        turn_norm_on_tensor(pe, 1, b, 6)

            @block.scalar
            def _(act):
                act.wait_ge(fold_mm, 2)
                half = P // 2
                for dst, src in ((f_q[:, :], bank[0][:, 0:P]), (f_ra[:, 0:half], bank[0][:, P:P + half]),
                                 (f_rb[:, 0:half], bank[0][:, P + half:2 * P]), (f_k[:, :], bank[1][:, 0:P]),
                                 (f_v[:, :], bank[1][:, P:2 * P])):
                    nc.scalar.copy(dst, src).then_inc(fold_ready, 1)
                for b in range(B):
                    u = b % 2
                    if b >= 2:
                        act.wait_ge(split_stored[b - 2], 4 * 16)
                    for k, ready, src in ((0, qc_mm, bank[0]), (1, kc_mm, bank[1]), (2, rot_ready, rot[:, :])):
                        act.wait_ge(ready, b + 1)
                        nc.scalar.copy(part[u][k][:, 0, :], src).then_inc(part0_ready, 1)
                    act.wait_ge(v_mm, b + 1)
                    nc.scalar.copy(v_all[:, b * TB:(b + 1) * TB, :], bank[4].rearrange("p (t d) -> p t d", t=TB))\
                        .then_inc(v_stored, 1)
                    for k in range(3):
                        act.wait_ge(res_ready, 3 * b + k + 1)
                        nc.scalar.copy(part[u][k][:, 1, :], res[k][:, :]).then_inc(part1_ready, 1)

                with act.Fori(0, B // 2) as pair:
                    for u in range(2):
                        b = pair * 2 + u
                        tails = b * TAIL_USES[1]
                        for h in range(H + 1):
                            if h < H:
                                act.wait_ge(scores_ready, b * H + h + 1)
                                act.wait_ge(pv_ready, b * H + max(h - 1, 0))
                                nc.scalar.activation(probs[h % 2][:, :], sc[h % 2][:, 0:SC], ACT.Exp, scale=QK_SCALE)\
                                    .then_inc(exp_ready, 1)
                            if h > 0 and h % 4 == 0:
                                g = h // 4 - 1
                                act.wait_ge(pv_ready, b * H + h)
                                act.wait_ge(tail_full[1], tails + g)
                                nc.scalar.copy(o_feat[:, :], pv[:, :]).then_inc(pv_read, 1)
                        act.wait_ge(tail_full[1], tails + 5)
                        nc.scalar.copy(o_t[:, :], tail[:, :]).then_inc(tail_read[1], 1)
                        act.wait_ge(tail_full[1], tails + 7)
                        nc.scalar.copy(x_feat[:, bass.ds(b * S, S)], tail[:, :]).then_inc(tail_read[1], 1)

            @block.vector
            def _(dve):
                for b in range(B):
                    u = b % 2
                    dve.wait_ge(rot_ready, b)
                    dve.wait_ge(rope_mm, 2 * b + 1)
                    dve.wait_ge(ld_attn, 8 * 16)
                    nc.vector.tensor_tensor(ra[:, :], bank[2], cos[:, :], ALU.mult).then_inc(rope_ready, 1)
                    dve.wait_ge(rope_mm, 2 * b + 2)
                    nc.vector.tensor_tensor(rb[:, :], bank[3], sin[:, :], ALU.mult).then_inc(rope_ready, 1)
                    dve.wait_ge(part2_ready, 3 * b)
                    for k, src in enumerate((bank[0], bank[1], rot[:, :])):
                        dve.wait_ge(part0_ready, 3 * b + k + 1)
                        nc.vector.tensor_tensor(res[k][:, :], src, part[u][k][:, 0, :], ALU.subtract)\
                            .then_inc(res_ready, 1)
                dve.wait_ge(ld_x, 5 * 16)

                with dve.Fori(0, B // 2) as pair:
                    for u in range(2):
                        b = pair * 2 + u
                        tails = b * TAIL_USES[1]
                        steps = Steps(dve, step[1], b * ATT_STEPS, ATT_STEPS)

                        def clip_and_mask(h):
                            p = probs[h % 2]
                            dve.wait_ge(exp_ready, b * H + h + 1)
                            steps.did(nc.vector.tensor_scalar(p[:, :], p[:, :], P_MIN, P_MAX, ALU.max, ALU.min))
                            steps.settle()
                            diag = p[:, 0:2 * S].rearrange("p (k c) -> p k c", c=S)[:, :, 0:P]
                            steps.did(nc.vector.tensor_tensor(
                                diag, diag, tri[:, :].rearrange("p (k c) -> p k c", c=P), ALU.mult))
                            pair_23 = p[:, KB_AT[3]:KB_AT[2] + P]
                            nc.vector.tensor_tensor(pair_23, pair_23, tri[:, :], ALU.mult).then_inc(probs_ready, 1)

                        def normalise(g):
                            dve.wait_ge(tail_full[1], tails + g + 1)
                            t4 = tail[:, :].rearrange("p (t j c) -> p t j c", t=TB, j=4)
                            steps.did(nc.vector.reciprocal(rden[:, :, :], t4[:, :, :, DH]))
                            steps.settle()
                            ov = o_tok[:, :, :].rearrange("p t (h d) -> p t h d", d=DH)[:, :, 4 * g:4 * g + 4, :]
                            nc.vector.tensor_tensor(ov, t4[:, :, :, 0:DH],
                                                    rden[:, :, :].unsqueeze(3).to_broadcast([P, TB, 4, DH]), ALU.mult)\
                                .then_inc(tail_read[1], 1)

                        for h in range(H):
                            clip_and_mask(h)
                            if h >= 6 and h % 4 == 2:
                                normalise(h // 4 - 1)
                        normalise(3)
                        residual_on_vector(dve, 1, b, 5)
                        norm_on_vector(dve, 1, b, steps)
                        steps.close()

        with ExitStack() as two:
            sil = [sb(f"sil{u}", [P, S], ctx=two) for u in range(2)]
            sg = [sb(f"sg{u}", [P, S], ctx=two) for u in range(2)]
            hid = sb("hid", [P, PAIRS, S], ctx=two)
            g_t = sb("g_t", [E8, S], ctx=two)
            FFN0_STEPS = ROUTER_STEPS + NORM_STEPS
            h1, h3, gb = (bank[0], bank[1]), (bank[2], bank[3]), (bank[4], bank[5])

            block = two.enter_context(nc.Block())

            @block.gpsimd
            def _(pool):
                with pool.Fori(0, B) as b:
                    norm_on_pool(pool, 2, b)

            @block.tensor
            def _(pe):
                pe.wait_ge(ld_ffn0, 6 * 16)
                with pe.Fori(0, B) as b:
                    tails = b * TAIL_USES[2]
                    router_on_tensor(pe, 2, b, r0_w)

                    def up(m):
                        w = m % 2
                        n = b * PAIRS + m
                        pe.wait_ge(silu_ready[2], b * PAIRS + max(m - 1, 0))
                        pe.matmul(h1[w], w1_0[:, m, :], x_cur[:, :], start=True, stop=True).then_inc(h1_ready[2], 1)
                        pe.wait_ge(hid_ready[2], b * PAIRS + max(m - 1, 0))
                        pe.matmul(h3[w], w3_0[:, m, :], x_cur[:, :], start=True, stop=True).then_inc(h3_ready[2], 1)

                    def spread_gates(m):
                        pe.wait_ge(gs_ready, b * RP + max(m - 1, 0))
                        pe.matmul(gb[m % 2], pair_sel[:, m, :], g_t[:, :], start=True, stop=True).then_inc(gb_ready, 1)

                    up(0)
                    up(1)
                    pe.wait_ge(gates_ready[2], b + 1)
                    pe.wait_ge(tail_read[2], tails + 1)
                    for t in range(TB):
                        ins = pe.transpose(tail[0:E8, t * P:(t + 1) * P], gates[:, t, :], ident[:, :])
                    ins.then_inc(tail_full[2], 1)
                    pe.wait_ge(gt_ready, b + 1)
                    for m in range(PAIRS):
                        if m >= 2:
                            up(m)
                        if m < RP:
                            spread_gates(m)
                    pe.wait_ge(hid_ready[2], (b + 1) * PAIRS)
                    for t in range(TB):
                        for m in range(PAIRS):
                            ins = pe.matmul(tail[:, t * P:(t + 1) * P], hid[:, m, t * P:(t + 1) * P], w2_0[:, m, :],
                                            start=(m == 0), stop=(m == PAIRS - 1))
                    ins.then_inc(tail_full[2], 1)
                    turn_norm_on_tensor(pe, 2, b, 3)

            @block.scalar
            def _(act):
                with act.Fori(0, B) as b:
                    tails = b * TAIL_USES[2]
                    act.wait_ge(h3_ready[2], b * PAIRS)
                    nc.scalar.copy(x_cur[:, :], x_feat[:, bass.ds(b * S, S)]).then_inc(cur_ready[2], 1)
                    for m in range(PAIRS):
                        act.wait_ge(h1_ready[2], b * PAIRS + m + 1)
                        act.wait_ge(hid_ready[2], b * PAIRS + max(m - 1, 0))
                        nc.scalar.activation(sil[m % 2][:, :], h1[m % 2], ACT.Silu).then_inc(silu_ready[2], 1)
                        if m == 0:
                            router_on_scalar(act, 2, b)
                        if m == 1:
                            act.wait_ge(tail_full[2], tails + 2)
                            act.wait_ge(gb_ready, b * RP)
                            nc.scalar.copy(g_t[:, :], tail[0:E8, :]).then_inc(gt_ready, 1)
                            act.wait_ge(gt_ready, b + 1)
                            nc.scalar.copy(tg[0:1, 0:1], tg[0:1, 0:1]).then_inc(tail_read[2], 1)
                    act.wait_ge(tail_full[2], tails + 4)
                    nc.scalar.copy(x_pad[:, bass.ds(b, 1), 1:S + 1], tail[:, :].unsqueeze(1)).then_inc(tail_read[2], 1)

            @block.vector
            def _(dve):
                dve.wait_ge(ld_ffn0, 6 * 16)
                with dve.Fori(0, B) as b:
                    steps = Steps(dve, step[2], b * FFN0_STEPS, FFN0_STEPS)
                    router_on_vector(dve, 2, b, steps, r0_b[:, :])
                    for m in range(PAIRS):
                        w = m % 2
                        dve.wait_ge(silu_ready[2], b * PAIRS + m + 1)
                        src = sil[w][:, :]
                        if m == 0:
                            dve.wait_ge(tail_full[2], b * TAIL_USES[2])
                        if m < RP:
                            dve.wait_ge(gb_ready, b * RP + m + 1)
                            nc.vector.tensor_tensor(sg[w][:, :], src, gb[w], ALU.mult).then_inc(gs_ready, 1)
                            dve.wait_ge(gs_ready, b * RP + m + 1)
                            src = sg[w][:, :]
                        dve.wait_ge(h3_ready[2], b * PAIRS + m + 1)
                        nc.vector.tensor_tensor(hid[:, m, :], src, h3[w], ALU.mult).then_inc(hid_ready[2], 1)
                    residual_on_vector(dve, 2, b, 2)
                    norm_on_vector(dve, 2, b, steps)
                    steps.close()

        w1_1 = sb("w1_1", [P, E8, HID1])
        w3_1 = sb("w3_1", [P, E8, HID1])
        w2_1 = sb("w2_1", [P, E8, FT, D])
        with ExitStack() as three:
            mix = {q: sb(f"mix_{q}", [P, S], ctx=three) for q in "kvr"}
            mtmp = sb("mtmp", [P, S], ctx=three)
            wtab = sb("wtab", [P, CT, S], ctx=three)
            ubk = sb("ubk", [P, CT], ctx=three)
            wneg = sb("wneg", [P, CT], ctx=three)
            brh = sb("brh", [P, CT], ctx=three)
            ones = sb("ones", [P, S], ctx=three)
            w_half = w_out
            karg = [sb(f"karg{u}", [P, S], ctx=three) for u in range(2)]
            e_w = [sb(f"e_w{u}", [P, S], ctx=three) for u in range(2)]
            e_u = [sb(f"e_u{u}", [P, S], ctx=three) for u in range(2)]
            val = [sb(f"val{u}", [P, S], ctx=three) for u in range(2)]
            ev = [sb(f"ev{u}", [P, S], ctx=three) for u in range(2)]
            euv = [sb(f"euv{u}", [P, S], ctx=three) for u in range(2)]
            sum_e = [sb(f"sum_e{u}", [P, S], ctx=three) for u in range(2)]
            sum_ev = [sb(f"sum_ev{u}", [P, S], ctx=three) for u in range(2)]
            th = [sb(f"th{u}", [P, S], ctx=three) for u in range(2)]
            num = sb("num", [P, CT, S], ctx=three)
            den = sb("den", [P, CT, S], ctx=three)
            RWKV_STEPS = 3 + CT + NORM_STEPS + 1
            kb_, vb_, rb_ = (bank[0], bank[1]), (bank[2], bank[3]), (bank[4], bank[5])
            COLS = {"bk": 0, "bv": 1, "br": 2, "td": 3, "u": 4}

            def col(name, c):
                return cols[:, COLS[name], c:c + 1]

            block = three.enter_context(nc.Block())

            @block.sync
            def _(sp):
                for dst, src in ((w1_1, "w1_1"), (w3_1, "w3_1")):
                    sp.dma_start(dst[:, :, :], a[src].rearrange("e d h -> d e h")).then_inc(ld_ffn1, 16)
                sp.dma_start(w2_1[:, :, :, :], a["w2_1"].rearrange("e (f p) d -> p e f d", p=P)).then_inc(ld_ffn1, 16)

            @block.gpsimd
            def _(pool):
                with pool.Fori(0, B) as b:
                    for c in range(CT):
                        w, n = c % 2, b * CT + c
                        wait_apart(pool, eu0_ready, n + 1)
                        nc.gpsimd.tensor_scalar(e_u[w][:, :], e_u[w][:, :], E_MAX, E_MIN, ALU.min, ALU.max)\
                            .then_inc(eu_ready, 1)
                        pool.wait_ge(vb_ready, n + 1)
                        pool.wait_ge(eu_ready, n + 1)
                        pool.wait_ge(num_ready, b * CT + max(c - 1, 0))
                        nc.gpsimd.tensor_tensor(euv[w][:, :], e_u[w][:, :], val[w][:, :], ALU.mult).then_inc(euv_ready, 1)
                        pool.wait_ge(sb_ready, n + 1)
                        pool.wait_ge(y_ready, b * CT)
                        nc.gpsimd.tensor_tensor(den[:, c, :], sum_e[w][:, :], e_u[w][:, :], ALU.add).then_inc(den_ready, 1)
                    norm_on_pool(pool, 3, b)

            @block.tensor
            def _(pe):
                pe.wait_ge(ld_rwkv, 7 * 16)
                pe.wait_ge(wout_ready, 1)
                with pe.Fori(0, B) as b:
                    pe.wait_ge(mix_ready, b + 1)
                    for c in range(CT):
                        w = c % 2
                        before = b * CT + max(c - 1, 0)
                        cs = slice(c * P, (c + 1) * P)
                        pe.wait_ge(karg_ready, before)
                        pe.wait_ge(eu0_ready, before)
                        pe.matmul(kb_[w], w_rwkv["k"][:, cs], mix["k"][:, :], start=True, stop=True).then_inc(k_ready, 1)
                        pe.wait_ge(vb_ready, before)
                        pe.matmul(vb_[w], w_rwkv["v"][:, cs], mix["v"][:, :], start=True, stop=True).then_inc(v_ready, 1)
                        pe.wait_ge(th_ready, before)
                        pe.matmul(rb_[w], w_rwkv["r"][:, cs], mix["r"][:, :], start=True, stop=True).then_inc(r_ready, 1)
                    pe.wait_ge(tail_read[3], b * TAIL_USES[3])
                    for c in range(CT):
                        pe.wait_ge(y_ready, b * CT + c + 1)
                        for t in range(TB):
                            ins = pe.matmul(tail[:, t * P:(t + 1) * P], num[:, c, t * P:(t + 1) * P], w_half[:, c, :],
                                            start=(c == 0 and t == 0), stop=(c == CT - 1), skip_group_check=True)
                    ins.then_inc(tail_full[3], 1)
                    turn_norm_on_tensor(pe, 3, b, 1)

            @block.scalar
            def _(act):
                act.wait_ge(ld_rwkv, 7 * 16)
                nc.scalar.mul(w_half[:, :, :], w_out[:, :, :], 0.5).then_inc(wout_ready, 1)
                act.wait_ge(wtab_ready, 1)
                with act.Fori(0, B) as b:
                    for c in range(CT):
                        w, n = c % 2, b * CT + c
                        before = b * CT + max(c - 1, 0)
                        act.wait_ge(karg_ready, n + 1)
                        act.wait_ge(den_ready, before)
                        nc.scalar.activation(e_u[w][:, :], kb_[w], ACT.Exp, bias=ubk[:, c:c + 1]).then_inc(eu0_ready, 1)
                        act.wait_ge(sb_ready, before)
                        act.wait_ge(ev_ready, before)
                        nc.scalar.activation(e_w[w][:, :], karg[w][:, :], ACT.Exp).then_inc(e0_ready, 1)
                        act.wait_ge(v_ready, n + 1)
                        act.wait_ge(euv_ready, before)
                        nc.scalar.activation(val[w][:, :], vb_[w], ACT.Identity, bias=col("bv", c)).then_inc(vb_ready, 1)
                        act.wait_ge(r_ready, n + 1)
                        act.wait_ge(gated_ready, before)
                        nc.scalar.activation(th[w][:, :], rb_[w], ACT.Tanh, bias=brh[:, c:c + 1], scale=0.5)\
                            .then_inc(th_ready, 1)
                    for half in range(2):
                        hs = slice(half * CT // 2, (half + 1) * CT // 2)
                        act.wait_ge(den_ready, b * CT + (half + 1) * CT // 2)
                        nc.scalar.activation(den[:, hs, :], den[:, hs, :], ACT.Ln).then_inc(lnb_ready, 1)
                    for half in range(2):
                        hs = slice(half * CT // 2, (half + 1) * CT // 2)
                        act.wait_ge(lnb_ready, b * 2 + half + 1)
                        nc.scalar.activation(den[:, hs, :], den[:, hs, :], ACT.Exp, scale=-1.0).then_inc(inv_ready, 1)
                    act.wait_ge(tail_full[3], b * TAIL_USES[3] + 2)
                    nc.scalar.copy(x_feat[:, bass.ds(b * S, S)], tail[:, :]).then_inc(tail_read[3], 1)

            @block.vector
            def _(dve):
                dve.wait_ge(ld_rwkv, 7 * 16)
                dve.wait_ge(const_ready, 3)
                nc.vector.memset(ones[:, :], 1.0).then_inc(setup, 1)
                for w in range(2):
                    nc.vector.memset(sum_e[w][:, 0:1], 0.0).then_inc(setup, 1)
                    nc.vector.memset(sum_ev[w][:, 0:1], 0.0).then_inc(setup, 1)
                nc.vector.tensor_scalar(wneg[:, :], cols[:, COLS["td"], :], 0.0, -1.0, ALU.max, ALU.mult).then_inc(setup, 1)
                nc.vector.tensor_tensor(ubk[:, :], cols[:, COLS["u"], :], cols[:, COLS["bk"], :], ALU.add).then_inc(setup, 1)
                nc.vector.tensor_scalar(brh[:, :], cols[:, COLS["br"], :], 0.5, None, ALU.mult).then_inc(setup, 1)
                dve.wait_ge(setup, 8)
                for c in range(CT):
                    ins = nc.vector.tensor_scalar(wtab[:, c, :], trem[:, :], wneg[:, c:c + 1], col("bk", c), ALU.mult, ALU.add)
                ins.then_inc(wtab_ready, 1)
                dve.wait_ge(wtab_ready, 1)
                with dve.Fori(0, B) as b:
                    steps = Steps(dve, step[3], b * RWKV_STEPS, RWKV_STEPS)
                    dve.wait_ge(r_ready, b * CT)
                    for q in "kvr":
                        eps = MIX[q]
                        steps.did(nc.vector.tensor_scalar(mtmp[:, :], x_pad[:, bass.ds(b, 1), 2:S + 2].rearrange("p o s -> p (o s)"),
                                                          1.0 - eps, None, ALU.mult))
                        steps.settle()
                        ins = nc.vector.scalar_tensor_tensor(mix[q][:, :], x_pad[:, bass.ds(b, 1), 0:S].rearrange("p o s -> p (o s)"),
                                                             eps, mtmp[:, :], ALU.mult, ALU.add)
                        if q == "r":
                            ins.then_inc(mix_ready, 1)
                        else:
                            ins.then_inc(mixed, 1)
                            dve.wait_ge(mixed, b * 2 + "kvr".index(q) + 1)
                    for c in range(CT):
                        w, n = c % 2, b * CT + c
                        dve.wait_ge(k_ready, n + 1)
                        dve.wait_ge(e0_ready, b * CT + max(c - 1, 0))
                        nc.vector.tensor_tensor(karg[w][:, :], kb_[w], wtab[:, c, :], ALU.add).then_inc(karg_ready, 1)
                        dve.wait_ge(e0_ready, n + 1)
                        nc.vector.tensor_scalar(e_w[w][:, :], e_w[w][:, :], E_MAX, E_MIN, ALU.min, ALU.max).then_inc(e_ready, 1)
                        dve.wait_ge(e_ready, n + 1)
                        dve.wait_ge(den_ready, b * CT + max(c - 1, 0))
                        nc.vector.tensor_tensor_scan(sum_e[w][:, 1:S], ones[:, 0:S - 1], e_w[w][:, 0:S - 1], 0.0,
                                                     ALU.mult, ALU.add).then_inc(sb_ready, 1)
                        dve.wait_ge(vb_ready, n + 1)
                        nc.vector.tensor_tensor(ev[w][:, :], e_w[w][:, :], val[w][:, :], ALU.mult).then_inc(ev_ready, 1)
                        dve.wait_ge(ev_ready, n + 1)
                        steps.did(nc.vector.tensor_tensor_scan(sum_ev[w][:, 1:S], ones[:, 0:S - 1], ev[w][:, 0:S - 1], 0.0,
                                                               ALU.mult, ALU.add))
                        steps.settle()
                        dve.wait_ge(euv_ready, n + 1)
                        if c == 0:
                            dve.wait_ge(tail_full[3], b * TAIL_USES[3])
                        nc.vector.tensor_tensor(num[:, c, :], sum_ev[w][:, :], euv[w][:, :], ALU.add).then_inc(num_ready, 1)
                        dve.wait_ge(num_ready, n + 1)
                        dve.wait_ge(th_ready, n + 1)
                        nc.vector.scalar_tensor_tensor(num[:, c, :], th[w][:, :], 1.0, num[:, c, :], ALU.add, ALU.mult)\
                            .then_inc(gated_ready, 1)
                    dve.wait_ge(gated_ready, (b + 1) * CT)
                    for c in range(CT):
                        dve.wait_ge(inv_ready, b * 2 + c // (CT // 2) + 1)
                        nc.vector.tensor_tensor(num[:, c, :], num[:, c, :], den[:, c, :], ALU.mult).then_inc(y_ready, 1)
                    residual_on_vector(dve, 3, b, 0)
                    steps.did(nc.vector.tensor_tensor(x_sum[:, :, :], x_sum[:, :, :], bo[:, :, :], ALU.add))
                    steps.settle()
                    norm_on_vector(dve, 3, b, steps)
                    steps.close()

        with ExitStack() as four:
            xe = [sb(f"xe{u}", [P, S], ctx=four) for u in range(2)]
            sil = [sb(f"sil1{u}", [P, S], ctx=four) for u in range(2)]
            hid = [sb(f"hid1{u}", [P, FT, S], ctx=four) for u in range(2)]
            FFN1_STEPS = ROUTER_STEPS + NORM_STEPS
            h1, h3 = (bank[0], bank[1]), (bank[2], bank[3])
            down = (bank[4], bank[5])
            block = four.enter_context(nc.Block())

            @block.sync
            def _(sp):
                with sp.Fori(0, B) as b:
                    sp.wait_ge(xn_ready[4], b + 1)
                    sp.dma_start(out.rearrange("b (t p) d -> b p t d", p=P)[bass.ds(b, 1)].rearrange("o p t d -> (o p) t d"),
                                 xn[:, :, :]).then_inc(out_stored, 16)
                sp.wait_ge(out_stored, B * 16)

            @block.gpsimd
            def _(pool):
                with pool.Fori(0, B) as b:
                    norm_on_pool(pool, 4, b)

            @block.tensor
            def _(pe):
                pe.wait_ge(ld_ffn1, 5 * 16)
                with pe.Fori(0, B) as b:
                    router_on_tensor(pe, 4, b, g_w)

                    def up(e):
                        pe.wait_ge(xe_ready, b * E8 + e + 1)
                        for f in range(FT):
                            w, fs = f % 2, slice(f * P, (f + 1) * P)
                            before = (b * E8 + e) * FT + f
                            before = before - 1 if e or f else before
                            pe.wait_ge(silu_ready[4], before)
                            pe.matmul(h1[w], w1_1[:, e, fs], xe[e % 2][:, :], start=True, stop=True).then_inc(h1_ready[4], 1)
                            pe.wait_ge(hid_ready[4], before)
                            pe.matmul(h3[w], w3_1[:, e, fs], xe[e % 2][:, :], start=True, stop=True).then_inc(h3_ready[4], 1)

                    def go_down(e):
                        pe.wait_ge(hid_ready[4], (b * E8 + e + 1) * FT)
                        pe.wait_ge(acc_ready, (b * E8 + (e - 1 if e else 0)) * TB)
                        for t in range(TB):
                            for f in range(FT):
                                ins = pe.matmul(down[e % 2][:, t * P:(t + 1) * P], hid[e % 2][:, f, t * P:(t + 1) * P],
                                                w2_1[:, e, f, :], start=(f == 0), stop=(f == FT - 1))
                        ins.then_inc(down_ready[4], 1)

                    for e in range(E8):
                        up(e)
                        if e:
                            go_down(e - 1)
                    go_down(E8 - 1)

            @block.scalar
            def _(act):
                with act.Fori(0, B) as b:
                    act.wait_ge(xe_ready, b * E8)
                    act.wait_ge(tail_full[4], b)
                    nc.scalar.copy(x_cur[:, :], x_feat[:, bass.ds(b * S, S)]).then_inc(cur_ready[4], 1)
                    for e in range(E8):
                        for f in range(FT):
                            n = (b * E8 + e) * FT + f
                            act.wait_ge(h1_ready[4], n + 1)
                            act.wait_ge(hid_ready[4], n - 1 if e or f else n)
                            nc.scalar.activation(sil[f % 2][:, :], h1[f % 2], ACT.Silu).then_inc(silu_ready[4], 1)
                            if e == 0 and f == 1:
                                router_on_scalar(act, 4, b)

            @block.vector
            def _(dve):
                dve.wait_ge(ld_ffn1, 5 * 16)
                with dve.Fori(0, B) as b:
                    steps = Steps(dve, step[4], b * FFN1_STEPS, FFN1_STEPS)

                    def shift_input(e):
                        dve.wait_ge(cur_ready[4], b + 1)
                        dve.wait_ge(h3_ready[4], (b * E8 + max(e - 1, 0)) * FT)
                        nc.vector.tensor_scalar(xe[e % 2][:, :], x_cur[:, :], dom[:, e:e + 1], None, ALU.add)\
                            .then_inc(xe_ready, 1)

                    def hidden(e):
                        dve.wait_ge(down_ready[4], b * E8 + (e - 1 if e else 0))
                        for f in range(FT):
                            n = (b * E8 + e) * FT + f
                            dve.wait_ge(silu_ready[4], n + 1)
                            dve.wait_ge(h3_ready[4], n + 1)
                            nc.vector.tensor_tensor(hid[e % 2][:, f, :], sil[f % 2][:, :], h3[f % 2], ALU.mult)\
                                .then_inc(hid_ready[4], 1)

                    def gated_sum(e):
                        dve.wait_ge(down_ready[4], b * E8 + e + 1)
                        dve.wait_ge(acc_ready, (b * E8 + e) * TB)
                        for t in range(TB):
                            before = x_sum[:, t, :] if e else x_tok[:, bass.ds(b * TB + t, 1), :].rearrange("p o d -> p (o d)")
                            nc.vector.scalar_tensor_tensor(x_sum[:, t, :], down[e % 2][:, t * P:(t + 1) * P],
                                                           gates[:, t, e:e + 1], before, ALU.mult, ALU.add)\
                                .then_inc(acc_ready, 1)

                    shift_input(0)
                    shift_input(1)
                    router_on_vector(dve, 4, b, steps, None)
                    for e in range(E8):
                        hidden(e)
                        if e + 2 < E8:
                            shift_input(e + 2)
                        if e:
                            gated_sum(e - 1)
                    gated_sum(E8 - 1)
                    dve.wait_ge(acc_ready, (b + 1) * E8 * TB)
                    norm_on_vector(dve, 4, b, steps)
                    steps.close()


def _constants():
    inv = np.float32(THETA) ** (-np.arange(0, DR, 2, dtype=np.float32) / np.float32(DR))
    ang = np.arange(S, dtype=np.float32)[:, None] * inv.astype(np.float32)
    row = np.arange(P) // H % DR
    cos = np.cos(ang).astype(np.float32).T[row // 2]
    sin = np.sin(ang).astype(np.float32).T[row // 2] * np.where(row % 2 == 0, -1, 1).astype(np.float32)[:, None]
    tri = np.triu(np.ones((P, P), np.float32))
    pair_sel = np.zeros((E8, RP, P), np.float32)
    for e in range(E8):
        pair_sel[e, e // 2, HID0 * (e % 2):HID0 * (e % 2 + 1)] = 1
    return {
        "cos": cos, "sin": sin, "ident": np.eye(P, dtype=np.float32), "tri": np.tile(tri, (1, 2)),
        "iota8": np.tile(np.arange(E8, dtype=np.float32), (P, TB)), "pair_sel": pair_sel,
        "trem": np.tile(np.float32(S) - np.arange(1, S + 1, dtype=np.float32), (P, 1)),
    }


def _lay_out(i):
    x = i["L0_attn_x"].reshape(B * S, D)
    swap = np.arange(DR) ^ 1
    qr = i["L0_attn_W_QR"].reshape(DL, H, DR)
    kr = i["L0_attn_W_KR"]

    def feature_major(w, width):
        return w.reshape(w.shape[0], H, width).transpose(0, 2, 1).reshape(w.shape[0], H * width)

    def pairs_up(routed, shared):
        w = np.concatenate([routed, shared])
        return w.transpose(1, 0, 2).reshape(D, PAIRS, P)

    w2 = np.concatenate([i["L0_ffn_routed_w2"], i["L0_ffn_shared_w2"]])
    return {
        "x_tok": x, "x_feat": x.T,
        "wdq": i["L0_attn_W_DQ"].T, "wdkv": i["L0_attn_W_DKV"].T,
        "wuq": np.concatenate([feature_major(i["L0_attn_W_UQ"], DH), feature_major(i["L0_attn_W_QR"], DR),
                               feature_major(qr[:, :, swap].reshape(DL, H * DR), DR)], axis=1),
        "wukv": np.concatenate([feature_major(i["L0_attn_W_UK"], DH), i["L0_attn_W_UV"]], axis=1),
        "wkr_a": np.repeat(kr, H, axis=1), "wkr_b": np.repeat(kr[:, swap], H, axis=1),
        "w_o": i["L0_attn_W_O"],
        "r0_w": i["L0_ffn_router_w"], "r0_b": np.tile(i["L0_ffn_router_b"], (P, TB)),
        "w1_0": pairs_up(i["L0_ffn_routed_w1"], i["L0_ffn_shared_w1"]),
        "w3_0": pairs_up(i["L0_ffn_routed_w3"], i["L0_ffn_shared_w3"]),
        "w2_0": w2.reshape(PAIRS, P, D).transpose(1, 0, 2),
        "wk": i["L1_attn_Wk"].T, "wv": i["L1_attn_Wv"].T, "wr": i["L1_attn_Wr"].T,
        "w_out": i["L1_attn_Wo"].T.reshape(CT, P, D).transpose(1, 0, 2),
        "cols": np.stack([i[n].reshape(CT, P).T for n in
                          ("L1_attn_bk", "L1_attn_bv", "L1_attn_br", "L1_attn_time_decay", "L1_attn_U")], axis=1),
        "bo": np.tile(i["L1_attn_bo"], (P, TB, 1)),
        "g_w": i["L1_ffn_gate_w"], "dom": i["L1_ffn_dom"].T,
        "w1_1": i["L1_ffn_W1"], "w3_1": i["L1_ffn_W3"], "w2_1": i["L1_ffn_W2"],
    }


def kernel(**inputs):
    import concourse.bacc as bacc
    from concourse.bass_utils import run_bass_kernel_spmd as run

    arrays = _lay_out({k: np.asarray(v) for k, v in inputs.items()})
    arrays.update(_constants())
    nc = bacc.Bacc("TRN2", target_bir_lowering=False, num_devices=1)
    feed, aps = {}, {}
    for name, value in arrays.items():
        value = np.ascontiguousarray(value)
        feed["in_" + name] = value
        aps[name] = nc.dram_tensor("in_" + name, value.shape, mybir.dt.from_np(value.dtype), kind="ExternalInput").ap()
    out = nc.dram_tensor("out", (B, S, D), F32, kind="ExternalOutput").ap()
    network(nc, aps, out)
    return run(nc, [feed], core_ids=[0]).results[0]["out"]
```

```python
import math
from contextlib import ExitStack

import numpy as np

import concourse.bass as bass
from concourse import mybir

F32 = mybir.dt.float32
BF16 = mybir.dt.bfloat16
U32 = mybir.dt.uint32
I32 = mybir.dt.int32
ALU = mybir.AluOpType
ACT = mybir.ActivationFunctionType

B, S, D = 4, 512, 128
P = 128
TB = S // P
H, DH, DR, DL = 16, 8, 4, 32
DQK = DH + DR
E8 = 8
HID0, SH0 = 64, 2
PAIRS = (E8 + SH0) * HID0 // P
RP = E8 * HID0 // P
CH = 1024
CT = CH // P
HID1 = 512
TILES = B * S * 2 // P + E8
SLOTS = TILES * P
UNROLL = 4
ZW = 320
FT = HID1 // P
LN_EPS = 1e-5
THETA = 10000.0

LAYER_ID, N_LAYERS = 1, 12
_EPS = math.exp(-LAYER_ID / N_LAYERS)
MIX = {"k": _EPS + 0.3 * LAYER_ID / (N_LAYERS - 1), "v": _EPS, "r": _EPS / 2.0}

QK_SCALE = 1.0 / math.sqrt(DQK)
P_MIN, P_MAX = math.exp(-80.0 * QK_SCALE), math.exp(80.0 * QK_SCALE)
E_MIN, E_MAX = math.exp(-20.0), math.exp(10.0)

Q_PART = (0, 1, 2, 0, 1, 0)
K_PART = (0, 0, 0, 1, 1, 2)
STACK = len(Q_PART) * DQK

def runs(order):
    out, at = [], 0
    while at < len(order):
        n = 1
        while at + n < len(order) and order[at + n] == order[at] + n:
            n += 1
        out.append((at, n))
        at += n
    return out


STACK_DMAS = len(runs(Q_PART)) + len(runs(K_PART))


KB_AT = (0, 512, 1024, 896)
KB_LEN = tuple(S - P * kb for kb in range(TB))
SC = 1280


class Steps:

    def __init__(self, eng, sem, first, total):
        self.eng, self.sem, self.first, self.total, self.n = eng, sem, first, total, 0

    def did(self, ins):
        ins.then_inc(self.sem, 1)
        self.n += 1

    def settle(self):
        self.eng.wait_ge(self.sem, self.first + self.n)

    def close(self):
        assert self.n == self.total, (self.n, self.total)


def network(nc, a, out):
    top = ExitStack()
    with top:
        def sb(name, shape, dt=F32, ctx=top):
            return ctx.enter_context(nc.sbuf_tensor(name, shape, dt))

        def sem(name):
            return top.enter_context(nc.semaphore(name))

        x_tok = sb("x_tok", [P, B * TB, D])
        x_feat = sb("x_feat", [P, B * S])
        x_pad = sb("x_pad", [P, B, S + 2])
        xn = sb("xn", [P, TB, D])
        x_sum = sb("x_sum", [P, TB, D])
        x_cur = sb("x_cur", [P, S])
        stats = sb("stats", [P, TB, 6])
        mv = sb("mv", [P, TB, 2])
        var_e = sb("var_e", [P, TB])
        rstd = sb("rstd", [P, TB])
        m_half = sb("m_half", [P, TB])
        ident = sb("ident", [P, P])
        iota8 = sb("iota8", [P, TB * E8])
        lg = sb("lg", [P, TB, E8])
        mx = sb("mx", [P, TB, 8])
        mi = sb("mi", [P, TB, 8], U32)
        mif = sb("mif", [P, 2, TB])
        mdiff = sb("mdiff", [P, TB])
        tg = sb("tg", [P, TB])
        g1 = sb("g1", [P, TB])
        g2 = sb("g2", [P, TB])
        oh1 = sb("oh1", [P, TB, E8])
        oh2 = sb("oh2", [P, TB, E8])
        gates = sb("gates", [P, TB, E8])
        w_o = sb("w_o", [P, D])
        r0_w = sb("r0_w", [P, E8])
        r0_b = sb("r0_b", [P, TB * E8])
        w1_0 = sb("w1_0", [P, PAIRS, P])
        w3_0 = sb("w3_0", [P, PAIRS, P])
        w2_0 = sb("w2_0", [P, PAIRS, D])
        pair_sel = sb("pair_sel", [E8, RP, P])
        w_rwkv = {q: sb(f"w_{q}", [P, CH]) for q in "kvr"}
        w_out = sb("w_out", [P, CT, D])
        cols = sb("cols", [P, 5, CT])
        bo = sb("bo", [P, TB, D])
        trem = sb("trem", [P, S])
        zeros = sb("zeros", [P, ZW])
        g_w = sb("g_w", [P, E8])
        dom = sb("dom", [P, E8])

        tail = top.enter_context(nc.psum_tensor("tail", [P, S], F32))
        pv = top.enter_context(nc.psum_tensor("pv", [P, S], F32))
        sc = [top.enter_context(nc.psum_tensor(f"sc{u}", [P, 3 * S], F32)) for u in range(2)]
        bank = [sc[k // 3][:, (k % 3) * S:(k % 3 + 1) * S] for k in range(6)]

        q_split = nc.dram_tensor("q_split", [B, 3, DQK * H, S], BF16).ap()
        k_split = nc.dram_tensor("k_split", [B, 3, DQK * H, S], BF16).ap()
        x_sorted = nc.dram_tensor("x_sorted", [SLOTS, D], F32).ap()
        y_sorted = nc.dram_tensor("y_sorted", [SLOTS, D], F32).ap()

        ld_attn, ld_x = sem("ld_attn"), sem("ld_x")
        ld_xf = [sem(f"ld_xf{b}") for b in range(B)]
        ld_ffn0, ld_rwkv, ld_ffn1 = sem("ld_ffn0"), sem("ld_rwkv"), sem("ld_ffn1")
        split_stored = [sem(f"split_stored{b}") for b in range(B)]
        stack_loaded = [sem(f"stack_loaded{u}") for u in range(2)]
        const_ready = sem("const_ready")
        v_const = sem("v_const")
        fold_mm, fold_ready = sem("fold_mm"), sem("fold_ready")
        qc_mm, kc_mm, rope_mm, v_mm = sem("qc_mm"), sem("kc_mm"), sem("rope_mm"), sem("v_mm")
        rope_ready, rot_ready = sem("rope_ready"), sem("rot_ready")
        part0_ready, res_ready = sem("part0_ready"), sem("res_ready")
        part1_ready, part2_ready = sem("part1_ready"), sem("part2_ready")
        v_stored, rden_ready, clipped, masked = (sem(n) for n in ("v_stored", "rden_ready", "clipped", "masked"))
        v_cur_ready = sem("v_cur_ready")
        scores_ready, exp_ready, probs_ready, pv_ready = (sem(n) for n in ("scores_ready", "exp_ready", "probs_ready", "pv_ready"))
        pv_read = sem("pv_read")
        tail_full = {n: sem(f"tail_full{n}") for n in range(1, 5)}
        tail_read = {n: sem(f"tail_read{n}") for n in range(1, 5)}
        step = {n: sem(f"dve_step{n}") for n in range(1, 5)}
        var_ready = {n: sem(f"var_ready{n}") for n in range(1, 5)}
        rstd_ready = {n: sem(f"rstd_ready{n}") for n in range(1, 5)}
        xn_ready = {n: sem(f"xn_ready{n}") for n in range(1, 5)}
        tok_stored = {n: sem(f"tok_stored{n}") for n in range(1, 5)}
        cur_ready = {n: sem(f"cur_ready{n}") for n in (2, 4)}
        diff_ready = {n: sem(f"diff_ready{n}") for n in (2, 4)}
        tanh_ready = {n: sem(f"tanh_ready{n}") for n in (2, 4)}
        gates_ready = {n: sem(f"gates_ready{n}") for n in (2, 4)}
        h1_ready = {n: sem(f"h1_ready{n}") for n in (2, 4)}
        h3_ready = {n: sem(f"h3_ready{n}") for n in (2, 4)}
        silu_ready = {n: sem(f"silu_ready{n}") for n in (2, 4)}
        hid_ready = {n: sem(f"hid_ready{n}") for n in (2, 4)}
        gt_ready, gb_ready, gs_ready = sem("gt_ready"), sem("gb_ready"), sem("gs_ready")
        down_ready = {n: sem(f"down_ready{n}") for n in (2, 4)}
        mix_ready, k_ready, v_ready, r_ready = (sem(n) for n in ("mix_ready", "k_ready", "v_ready", "r_ready"))
        karg_ready, eu0_ready, vb_ready, th_ready, e0_ready = (sem(n) for n in ("karg_ready", "eu0_ready", "vb_ready", "th_ready", "e0_ready"))
        euv_ready, den_ready, e_ready, ev_ready, sb_ready = (sem(n) for n in ("euv_ready", "den_ready", "e_ready", "ev_ready", "sb_ready"))
        lnb_ready, inv_ready, y_ready, wtab_ready, wout_ready, num_ready, mixed, setup, gated_ready = (
            sem(n) for n in ("lnb_ready", "inv_ready", "y_ready", "wtab_ready", "wout_ready", "num_ready", "mixed", "setup", "gated_ready"))
        after_scaled, sum_ev_ready, half_out = sem("after_scaled"), sem("sum_ev_ready"), sem("half_out")
        xe_ready, acc_ready = sem("xe_ready"), sem("acc_ready")
        ld_gate = sem("ld_gate")
        cleared, scattered, ld_route, logits_ready, chosen_ready, ranks_ready, slot_ready, owner_ready, route_step = (
            sem(n) for n in ("cleared", "scattered", "ld_route", "logits_ready", "chosen_ready", "ranks_ready",
                             "slot_ready", "owner_ready", "route_step"))
        x_loaded, y_stored = [sem(f"x_loaded{w}") for w in range(2)], [sem(f"y_stored{w}") for w in range(2)]
        xt_full, ht_full, ht_done, y_done = (sem(n) for n in ("xt_full", "ht_full", "ht_done", "y_done"))
        gathered = [sem(f"gathered{b}") for b in range(B)]
        out_stored = sem("out_stored")

        def wait_apart(eng, semaphore, count):
            count = eng.to_reg(count)
            eng.wait_ge(const_ready, 4)
            eng.wait_ge(semaphore, count)

        def residual_on_vector(dve, n, b, use):
            dve.wait_ge(tail_full[n], b * TAIL_USES[n] + use + 1)
            nc.vector.tensor_tensor(x_sum[:, :, :], tail[:, :].rearrange("p (t d) -> p t d", t=TB),
                                    x_tok[:, bass.ds(b * TB, TB), :], ALU.add).then_inc(tail_read[n], 1)
            dve.wait_ge(tail_read[n], b * TAIL_USES[n] + use + 1)

        def norm_on_vector(dve, n, b, steps):
            for t in range(TB):
                steps.did(nc.vector.bn_stats(stats[:, t, :], x_sum[:, t, :]))
            wait_apart(dve, steps.sem, steps.first + steps.n)
            for t in range(TB):
                steps.did(nc.vector.bn_aggr(mv[:, t, :], stats[:, t, :]))
            steps.settle()
            nc.vector.tensor_scalar(var_e[:, :], mv[:, :, 1], LN_EPS, None, ALU.add).then_inc(var_ready[n], 1)
            dve.wait_ge(rstd_ready[n], b + 1)
            if n < 4:
                dve.wait_ge(tail_full[n], b * TAIL_USES[n])
                dve.wait_ge(tok_stored[n], b)
            else:
                dve.wait_ge(out_stored, b * 16)
            for t in range(TB):
                ins = nc.vector.tensor_scalar(xn[:, t, :], x_sum[:, t, :], mv[:, t, 0:1], rstd[:, t:t + 1],
                                              ALU.subtract, ALU.mult)
                if t < TB - 1:
                    steps.did(ins)
            ins.then_inc(xn_ready[n], 1)
        NORM_STEPS = 2 * TB + (TB - 1)
        TAIL_USES = {1: H // 4 + 3, 2: 4, 3: 2, 4: 1}

        def norm_on_pool(pool, n, b):
            pool.wait_ge(var_ready[n], b + 1)
            nc.gpsimd.tensor_tensor(rstd[:, :], var_e[:, :], m_half[:, :], ALU.pow).then_inc(rstd_ready[n], 1)
            if n < 4:
                pool.wait_ge(xn_ready[n], b + 1)
                nc.gpsimd.tensor_copy(x_tok[:, bass.ds(b * TB, TB), :], xn[:, :, :]).then_inc(tok_stored[n], 1)

        def turn_norm_on_tensor(pe, n, b, use):
            pe.wait_ge(xn_ready[n], b + 1)
            pe.wait_ge(tail_read[n], b * TAIL_USES[n] + use)
            for t in range(TB):
                ins = pe.transpose(tail[:, t * P:(t + 1) * P], xn[:, t, :], ident[:, :])
            ins.then_inc(tail_full[n], 1)

        def router_on_tensor(pe, n, b, w):
            pe.wait_ge(cur_ready[n], b + 1)
            pe.wait_ge(tail_read[n], b * TAIL_USES[n])
            for t in range(TB):
                ins = pe.matmul(tail[:, t * E8:(t + 1) * E8], x_cur[:, t * P:(t + 1) * P], w[:, :],
                                start=True, stop=True)
            ins.then_inc(tail_full[n], 1)

        def router_on_vector(dve, n, b, steps, bias):
            dve.wait_ge(tail_full[n], b * TAIL_USES[n] + 1)
            src = tail[:, 0:TB * E8]
            dst = lg[:, :, :].rearrange("p t e -> p (t e)")
            if bias is None:
                nc.vector.tensor_copy(dst, src).then_inc(tail_read[n], 1)
            else:
                nc.vector.tensor_tensor(dst, src, bias, ALU.add).then_inc(tail_read[n], 1)
            wait_apart(dve, tail_read[n], b * TAIL_USES[n] + 1)
            for t in range(TB):
                steps.did(nc.vector.max(mx[:, t, :], lg[:, t, :]))
            wait_apart(dve, steps.sem, steps.first + steps.n)
            for t in range(TB):
                steps.did(nc.vector.max_index(mi[:, t, :], mx[:, t, :], lg[:, t, :]))
            nc.vector.tensor_tensor(mdiff[:, :], mx[:, :, 0], mx[:, :, 1], ALU.subtract).then_inc(diff_ready[n], 1)
            steps.settle()
            steps.did(nc.vector.tensor_copy(mif[:, :, :].rearrange("p k t -> p t k"), mi[:, :, 0:2]))
            steps.settle()
            io = iota8[:, :].rearrange("p (t e) -> p t e", t=TB)
            for k, oh in enumerate((oh1, oh2)):
                steps.did(nc.vector.tensor_tensor(
                    oh[:, :, :], io, mif[:, k, :].unsqueeze(2).to_broadcast([P, TB, E8]), ALU.is_equal))
            dve.wait_ge(tanh_ready[n], b + 1)
            steps.did(nc.vector.tensor_scalar(g1[:, :], tg[:, :], 0.5, 0.5, ALU.mult, ALU.add))
            steps.did(nc.vector.tensor_scalar(g2[:, :], tg[:, :], -0.5, 0.5, ALU.mult, ALU.add))
            steps.settle()
            for oh, g in ((oh1, g1), (oh2, g2)):
                steps.did(nc.vector.tensor_tensor(oh[:, :, :], oh[:, :, :],
                                                  g[:, :].unsqueeze(2).to_broadcast([P, TB, E8]), ALU.mult))
            steps.settle()
            nc.vector.tensor_tensor(gates[:, :, :], oh1[:, :, :], oh2[:, :, :], ALU.add).then_inc(gates_ready[n], 1)
            dve.wait_ge(gates_ready[n], b + 1)
        ROUTER_STEPS = 2 * TB + 1 + 2 + 2 + 2

        def router_on_scalar(act, n, b):
            act.wait_ge(diff_ready[n], b + 1)
            nc.scalar.activation(tg[:, :], mdiff[:, :], ACT.Tanh, scale=0.5).then_inc(tanh_ready[n], 1)

        with ExitStack() as one:
            wdq = sb("wdq", [DL, D], ctx=one)
            wdkv = sb("wdkv", [DL, D], ctx=one)
            wuq = sb("wuq", [DL, 2 * P], ctx=one)
            wukv = sb("wukv", [DL, 2 * P], ctx=one)
            f_q = sb("f_q", [P, P], ctx=one)
            f_k = sb("f_k", [P, P], ctx=one)
            f_v = sb("f_v", [P, P], ctx=one)
            f_ra = sb("f_ra", [P, P], ctx=one)
            f_rb = sb("f_rb", [P, P], ctx=one)
            cos = sb("cos", [P, S], ctx=one)
            sin = sb("sin", [P, S], ctx=one)
            tri = sb("tri", [P, 2 * P], ctx=one)
            ra = sb("ra", [P, S], ctx=one)
            rb = sb("rb", [P, S], ctx=one)
            rot = sb("rot", [P, S], ctx=one)
            res = [sb(f"res{k}", [P, S], ctx=one) for k in range(3)]
            part = [[sb(f"part{u}{k}", [P, 3, S], BF16, ctx=one) for k in range(3)] for u in range(2)]
            v_all = sb("v_all", [P, B * TB, D], ctx=one)
            DV = DH + 1
            v_cur = [sb(f"v_cur{u}", [P, TB, H * DV + 32 - DV], ctx=one) for u in range(2)]
            q_st = [sb(f"q_st{u}", [STACK, H, S], BF16, ctx=one) for u in range(2)]
            k_st = [sb(f"k_st{u}", [STACK, H, S], BF16, ctx=one) for u in range(2)]
            probs = [sb(f"probs{u}", [P, SC], ctx=one) for u in range(4)]
            o_feat = sb("o_feat", [P, S], ctx=one)
            rden = sb("rden", [P, TB, 4], ctx=one)
            o_tok = sb("o_tok", [P, TB, D], ctx=one)
            o_t = sb("o_t", [P, S], ctx=one)
            HH, GROUPS = 2 * H, 2 * H // 4
            TURN_OUT, PROJECT, TURN_NORM = H + 5, H + 6, H + 9

            TAIL_ORDER = [("group", g) for g in range(4)] + [("out", 0), ("project", 0), ("group", 4), ("norm", 0)] \
                + [("group", g) for g in range(5, 8)] + [("out", 1), ("project", 1), ("norm", 1)]

            def tails_before(pair, what, k):
                return pair * len(TAIL_ORDER) + TAIL_ORDER.index((what, k))

            def use_of_batch(what, u):
                return TAIL_ORDER.index((what, u)) - u * TAIL_USES[1]

            block = one.enter_context(nc.Block())

            @block.sync
            def _(sp):
                attn_loads = ((wdq[:, :], a["wdq"]), (wdkv[:, :], a["wdkv"]), (wuq[:, :], a["wuq"]),
                              (wukv[:, :], a["wukv"]), (f_ra[:, P // 2:], a["wkr_a"]), (f_rb[:, P // 2:], a["wkr_b"]))
                for dst, src in attn_loads:
                    sp.dma_start(dst, src).then_inc(ld_attn, 16)
                for b in range(B):
                    sp.dma_start(x_feat[:, b * S:(b + 1) * S], a["x_feat"][:, b * S:(b + 1) * S]).then_inc(ld_xf[b], 16)
                    if b == 0:
                        sp.dma_start(cos[:, :], a["cos"]).then_inc(ld_attn, 16)
                        sp.dma_start(sin[:, :], a["sin"]).then_inc(ld_attn, 16)
                for dst, src in ((w_o[:, :], a["w_o"]), (ident[:, :], a["ident"]), (tri[:, :], a["tri"]),
                                 (iota8[:, :], a["iota8"])):
                    sp.dma_start(dst, src).then_inc(ld_x, 16)
                sp.dma_start(x_tok[:, :, :], a["x_tok"].rearrange("(n p) d -> p n d", p=P)).then_inc(ld_x, 16)
                for b in range(B):
                    u = b % 2
                    sp.wait_ge(part2_ready, 3 * b + 3)
                    sp.wait_ge(part1_ready, 3 * b + 3)
                    sp.wait_ge(part0_ready, 3 * b + 3)
                    c = DH * H
                    for dram, k, lo in ((q_split, 0, 0), (k_split, 1, P // 2)):
                        rows = dram[b].rearrange("s r c -> r s c")
                        sp.dma_start(rows[0:c], part[u][k][:, :, :]).then_inc(split_stored[b], 16)
                        sp.dma_start(rows[c:], part[u][2][lo:lo + P // 2, :, :]).then_inc(split_stored[b], 16)
                    sp.wait_ge(split_stored[b], 4 * 16)
                    if b >= 2:
                        sp.wait_ge(scores_ready, H * (b - 1))
                    for dst, dram, order in ((q_st[u], q_split, Q_PART), (k_st[u], k_split, K_PART)):
                        rows = dram[b].rearrange("s (k h) c -> (s k) h c", h=H)
                        for at, n in runs(order):
                            sp.dma_start(dst[at * DQK:(at + n) * DQK, :, :],
                                         rows[order[at] * DQK:(order[at] + n) * DQK]).then_inc(stack_loaded[u], 16)
                for dst, src in ((r0_w[:, :], a["r0_w"]), (r0_b[:, :], a["r0_b"]), (w1_0[:, :, :], a["w1_0"]),
                                 (w3_0[:, :, :], a["w3_0"]), (w2_0[:, :, :], a["w2_0"]), (pair_sel[:, :, :], a["pair_sel"])):
                    sp.dma_start(dst, src).then_inc(ld_ffn0, 16)
                for dst, src in ((w_rwkv["k"][:, :], a["wk"]), (w_rwkv["v"][:, :], a["wv"]), (w_rwkv["r"][:, :], a["wr"]),
                                 (w_out[:, :, :], a["w_out"]), (cols[:, :, :], a["cols"]), (bo[:, :, :], a["bo"]),
                                 (trem[:, :], a["trem"])):
                    sp.dma_start(dst, src).then_inc(ld_rwkv, 16)
                for dst, src in ((g_w[:, :], a["g_w"]), (dom[:, :], a["dom"])):
                    sp.dma_start(dst, src).then_inc(ld_gate, 16)

            @block.gpsimd
            def _(pool):
                for u in range(2):
                    nc.gpsimd.memset(v_cur[u][:, :, :], 1.0).then_inc(v_const, 1)
                nc.gpsimd.memset(m_half[:, :], -0.5).then_inc(const_ready, 1)
                nc.gpsimd.memset(zeros[:, :], 0.0).then_inc(const_ready, 1)
                nc.gpsimd.memset(x_pad[:, :, 0:1], 0.0).then_inc(const_ready, 1)
                nc.gpsimd.memset(x_pad[:, :, S + 1:S + 2], 0.0).then_inc(const_ready, 1)
                for b in range(B):
                    u = b % 2
                    pool.wait_ge(rope_ready, 2 * b + 2)
                    pool.wait_ge(res_ready, 3 * b)
                    pool.wait_ge(part0_ready, 3 * b)
                    nc.gpsimd.tensor_tensor(rot[:, :], ra[:, :], rb[:, :], ALU.add).then_inc(rot_ready, 1)
                    for k in range(3):
                        pool.wait_ge(part1_ready, 3 * b + k + 1)
                        nc.gpsimd.tensor_tensor(part[u][k][:, 2, :], res[k][:, :], part[u][k][:, 1, :], ALU.subtract)\
                            .then_inc(part2_ready, 1)
                pool.wait_ge(const_ready, 4)
                pool.wait_ge(v_stored, B)
                pool.wait_ge(v_const, 2)
                with pool.Fori(0, B // 2) as pair:
                    pool.wait_ge(pv_ready, pair * HH)
                    for u in range(2):
                        nc.gpsimd.tensor_copy(v_cur[u][:, :, 0:H * DV].rearrange("p t (h d) -> p t h d", d=DV)[:, :, :, 0:DH],
                                              v_all[:, bass.ds((pair * 2 + u) * TB, TB), :].rearrange("p t (h d) -> p t h d", h=H))\
                            .then_inc(v_cur_ready, 1)
                    for u in range(2):
                        norm_on_pool(pool, 1, pair * 2 + u)

            @block.tensor
            def _(pe):
                pe.wait_ge(ld_attn, 8 * 16)
                pe.matmul(bank[0][:, 0:2 * P], wdq[:, :], wuq[:, :], start=True, stop=True).then_inc(fold_mm, 1)
                pe.matmul(bank[1][:, 0:2 * P], wdkv[:, :], wukv[:, :], start=True, stop=True).then_inc(fold_mm, 1)
                pe.wait_ge(fold_ready, 5)
                for b in range(B):
                    x = x_feat[:, b * S:(b + 1) * S]
                    pe.wait_ge(ld_xf[b], 16)
                    pe.wait_ge(res_ready, 3 * b)
                    pe.matmul(bank[0], f_q[:, :], x, start=True, stop=True).then_inc(qc_mm, 1)
                    pe.matmul(bank[1], f_k[:, :], x, start=True, stop=True).then_inc(kc_mm, 1)
                    pe.wait_ge(rope_ready, 2 * b)
                    pe.matmul(bank[2], f_ra[:, :], x, start=True, stop=True).then_inc(rope_mm, 1)
                    pe.matmul(bank[3], f_rb[:, :], x, start=True, stop=True).then_inc(rope_mm, 1)
                    pe.wait_ge(v_stored, b)
                    for t in range(TB):
                        ins = pe.matmul(bank[4][:, t * P:(t + 1) * P], x[:, t * P:(t + 1) * P], f_v[:, :],
                                        start=True, stop=True)
                    ins.then_inc(v_mm, 1)
                pe.wait_ge(part0_ready, 3 * B)
                pe.wait_ge(rope_ready, 2 * B)
                pe.wait_ge(res_ready, 3 * B)
                pe.wait_ge(v_stored, B)
                pe.wait_ge(ld_x, 5 * 16)

                with pe.Fori(0, B // 2) as pair:
                    def scores(m):
                        u, h = m // H, m % H
                        if h == 0:
                            pe.wait_ge(stack_loaded[u], (pair + 1) * (16 * STACK_DMAS))
                        pe.wait_ge(exp_ready, pair * HH + max(m - 1, 0))
                        for kb in range(TB):
                            ins = pe.matmul(sc[m % 2][:, KB_AT[kb]:KB_AT[kb] + KB_LEN[kb]],
                                            k_st[u][:, h, kb * P:(kb + 1) * P], q_st[u][:, h, kb * P:S],
                                            start=True, stop=True)
                        ins.then_inc(scores_ready, 1)

                    def values(m):
                        u, h, j = m // H, m % H, m % 4
                        if h == 0:
                            pe.wait_ge(v_cur_ready, pair * 2 + u + 1)
                        pe.wait_ge(probs_ready, pair * HH + (m + 1))
                        pe.wait_ge(pv_read, pair * HH + max(m - 3, 0))
                        for kb in range(TB):
                            ins = pe.matmul(pv[32 * j:32 * j + 32, kb * P:S], v_cur[u][:, kb, h * DV:h * DV + 32],
                                            probs[j][:, KB_AT[kb]:KB_AT[kb] + KB_LEN[kb]],
                                            start=(kb == 0), stop=(kb == TB - 1))
                        ins.then_inc(pv_ready, 1)

                    def turn_group(g):
                        pe.wait_ge(pv_read, pair * HH + 4 * (g + 1))
                        pe.wait_ge(tail_read[1], tails_before(pair, "group", g))
                        for t in range(TB):
                            ins = pe.transpose(tail[:, t * P:(t + 1) * P], o_feat[:, t * P:(t + 1) * P], ident[:, :])
                        ins.then_inc(tail_full[1], 1)

                    def turn_out(u):
                        pe.wait_ge(tail_read[1], tails_before(pair, "out", u))
                        for t in range(TB):
                            ins = pe.transpose(tail[:, t * P:(t + 1) * P], o_tok[:, t, :], ident[:, :])
                        ins.then_inc(tail_full[1], 1)

                    def project(u):
                        pe.wait_ge(tail_read[1], tails_before(pair, "project", u))
                        for t in range(TB):
                            ins = pe.matmul(tail[:, t * P:(t + 1) * P], o_t[:, t * P:(t + 1) * P], w_o[:, :],
                                            start=True, stop=True)
                        ins.then_inc(tail_full[1], 1)

                    for m in range(HH + 2):
                        if m < HH:
                            scores(m)
                        if m > 4 and m % 4 == 3:
                            turn_group(m // 4 - 1)
                        if m == TURN_OUT:
                            turn_out(0)
                        if m == PROJECT:
                            project(0)
                        if m == TURN_NORM:
                            turn_norm_on_tensor(pe, 1, pair * 2, use_of_batch("norm", 0))
                        if m >= 2:
                            values(m - 2)
                    turn_group(GROUPS - 1)
                    turn_out(1)
                    project(1)
                    turn_norm_on_tensor(pe, 1, pair * 2 + 1, use_of_batch("norm", 1))

            @block.scalar
            def _(act):
                act.wait_ge(fold_mm, 2)
                half = P // 2
                for dst, src in ((f_q[:, :], bank[0][:, 0:P]), (f_ra[:, 0:half], bank[0][:, P:P + half]),
                                 (f_rb[:, 0:half], bank[0][:, P + half:2 * P]), (f_k[:, :], bank[1][:, 0:P]),
                                 (f_v[:, :], bank[1][:, P:2 * P])):
                    nc.scalar.copy(dst, src).then_inc(fold_ready, 1)
                for b in range(B):
                    u = b % 2
                    if b >= 2:
                        act.wait_ge(split_stored[b - 2], 4 * 16)
                    for k, ready, src in ((0, qc_mm, bank[0]), (1, kc_mm, bank[1]), (2, rot_ready, rot[:, :])):
                        act.wait_ge(ready, b + 1)
                        nc.scalar.copy(part[u][k][:, 0, :], src).then_inc(part0_ready, 1)
                    act.wait_ge(v_mm, b + 1)
                    nc.scalar.copy(v_all[:, b * TB:(b + 1) * TB, :], bank[4].rearrange("p (t d) -> p t d", t=TB))\
                        .then_inc(v_stored, 1)
                    for k in range(3):
                        act.wait_ge(res_ready, 3 * b + k + 1)
                        nc.scalar.copy(part[u][k][:, 1, :], res[k][:, :]).then_inc(part1_ready, 1)

                with act.Fori(0, B // 2) as pair:
                    def keep_sums(m):
                        rows = slice(32 * (m % 4), 32 * (m % 4) + 32)
                        act.wait_ge(pv_ready, pair * HH + (m + 1))
                        act.wait_ge(tail_full[1], tails_before(pair, "group", m // 4 - 1) + 1 if m >= 4 else pair * len(TAIL_ORDER))
                        nc.scalar.copy(o_feat[rows, :], pv[rows, :]).then_inc(pv_read, 1)

                    def keep_turned(u):
                        act.wait_ge(tail_full[1], tails_before(pair, "out", u) + 1)
                        nc.scalar.copy(o_t[:, :], tail[:, :]).then_inc(tail_read[1], 1)

                    def keep_features(u):
                        act.wait_ge(tail_full[1], tails_before(pair, "norm", u) + 1)
                        nc.scalar.copy(x_feat[:, bass.ds((pair * 2 + u) * S, S)], tail[:, :]).then_inc(tail_read[1], 1)

                    for m in range(HH + 3):
                        if m < HH:
                            act.wait_ge(scores_ready, pair * HH + (m + 1))
                            act.wait_ge(pv_ready, pair * HH + max(m - 3, 0))
                            nc.scalar.activation(probs[m % 4][:, :], sc[m % 2][:, 0:SC], ACT.Exp, scale=QK_SCALE)\
                                .then_inc(exp_ready, 1)
                        if m >= 3:
                            keep_sums(m - 3)
                        if m == TURN_OUT:
                            keep_turned(0)
                        if m == TURN_NORM:
                            keep_features(0)
                    keep_turned(1)
                    keep_features(1)

            @block.vector
            def _(dve):
                for b in range(B):
                    u = b % 2
                    dve.wait_ge(rot_ready, b)
                    dve.wait_ge(rope_mm, 2 * b + 1)
                    dve.wait_ge(ld_attn, 8 * 16)
                    nc.vector.tensor_tensor(ra[:, :], bank[2], cos[:, :], ALU.mult).then_inc(rope_ready, 1)
                    dve.wait_ge(rope_mm, 2 * b + 2)
                    nc.vector.tensor_tensor(rb[:, :], bank[3], sin[:, :], ALU.mult).then_inc(rope_ready, 1)
                    dve.wait_ge(part2_ready, 3 * b)
                    for k, src in enumerate((bank[0], bank[1], rot[:, :])):
                        dve.wait_ge(part0_ready, 3 * b + k + 1)
                        nc.vector.tensor_tensor(res[k][:, :], src, part[u][k][:, 0, :], ALU.subtract)\
                            .then_inc(res_ready, 1)
                dve.wait_ge(ld_x, 5 * 16)

                with dve.Fori(0, B // 2) as pair:
                    steps = [Steps(dve, step[1], (pair * 2 + u) * NORM_STEPS, NORM_STEPS) for u in range(2)]

                    def clip_and_mask(m):
                        p = probs[m % 4]
                        dve.wait_ge(exp_ready, pair * HH + (m + 1))
                        nc.vector.tensor_scalar(p[:, :], p[:, :], P_MIN, P_MAX, ALU.max, ALU.min).then_inc(clipped, 1)
                        dve.wait_ge(clipped, pair * HH + (m + 1))
                        diag = p[:, 0:2 * S].rearrange("p (k c) -> p k c", c=S)[:, :, 0:P]
                        nc.vector.tensor_tensor(
                            diag, diag, tri[:, :].rearrange("p (k c) -> p k c", c=P), ALU.mult).then_inc(masked, 1)
                        pair_23 = p[:, KB_AT[3]:KB_AT[2] + P]
                        nc.vector.tensor_tensor(pair_23, pair_23, tri[:, :], ALU.mult).then_inc(probs_ready, 1)

                    def normalise(g):
                        gh = g % (H // 4)
                        dve.wait_ge(tail_full[1], tails_before(pair, "group", g) + 1)
                        t4 = tail[:, :].rearrange("p (t j c) -> p t j c", t=TB, j=4)
                        nc.vector.reciprocal(rden[:, :, :], t4[:, :, :, DH]).then_inc(rden_ready, 1)
                        dve.wait_ge(rden_ready, pair * GROUPS + (g + 1))
                        ov = o_tok[:, :, :].rearrange("p t (h d) -> p t h d", d=DH)[:, :, 4 * gh:4 * gh + 4, :]
                        nc.vector.tensor_tensor(ov, t4[:, :, :, 0:DH],
                                                rden[:, :, :].unsqueeze(3).to_broadcast([P, TB, 4, DH]), ALU.mult)\
                            .then_inc(tail_read[1], 1)

                    def add_and_norm(u):
                        residual_on_vector(dve, 1, pair * 2 + u, use_of_batch("project", u))
                        norm_on_vector(dve, 1, pair * 2 + u, steps[u])
                        steps[u].close()

                    for m in range(HH):
                        clip_and_mask(m)
                        if m > 4 and m % 4 == 3:
                            normalise(m // 4 - 1)
                        if m == PROJECT:
                            add_and_norm(0)
                    normalise(GROUPS - 1)
                    add_and_norm(1)

        with ExitStack() as two:
            sil = [sb(f"sil{u}", [P, S], ctx=two) for u in range(2)]
            sg = [sb(f"sg{u}", [P, S], ctx=two) for u in range(2)]
            hid = sb("hid", [P, PAIRS, S], ctx=two)
            g_t = sb("g_t", [E8, S], ctx=two)
            FFN0_STEPS = ROUTER_STEPS + NORM_STEPS
            h1, h3, gb = (bank[0], bank[1]), (bank[2], bank[3]), (bank[4], bank[5])

            block = two.enter_context(nc.Block())

            @block.gpsimd
            def _(pool):
                with pool.Fori(0, B) as b:
                    norm_on_pool(pool, 2, b)

            @block.tensor
            def _(pe):
                pe.wait_ge(ld_ffn0, 6 * 16)
                with pe.Fori(0, B) as b:
                    tails = b * TAIL_USES[2]
                    router_on_tensor(pe, 2, b, r0_w)

                    def up(m):
                        w = m % 2
                        n = b * PAIRS + m
                        pe.wait_ge(silu_ready[2], b * PAIRS + max(m - 1, 0))
                        pe.matmul(h1[w], w1_0[:, m, :], x_cur[:, :], start=True, stop=True).then_inc(h1_ready[2], 1)
                        pe.wait_ge(hid_ready[2], b * PAIRS + max(m - 1, 0))
                        pe.matmul(h3[w], w3_0[:, m, :], x_cur[:, :], start=True, stop=True).then_inc(h3_ready[2], 1)

                    def spread_gates(m):
                        pe.wait_ge(gs_ready, b * RP + max(m - 1, 0))
                        pe.matmul(gb[m % 2], pair_sel[:, m, :], g_t[:, :], start=True, stop=True).then_inc(gb_ready, 1)

                    up(0)
                    up(1)
                    pe.wait_ge(gates_ready[2], b + 1)
                    pe.wait_ge(tail_read[2], tails + 1)
                    for t in range(TB):
                        ins = pe.transpose(tail[0:E8, t * P:(t + 1) * P], gates[:, t, :], ident[:, :])
                    ins.then_inc(tail_full[2], 1)
                    pe.wait_ge(gt_ready, b + 1)
                    for m in range(PAIRS):
                        if m >= 2:
                            up(m)
                        if m < RP:
                            spread_gates(m)
                    pe.wait_ge(hid_ready[2], (b + 1) * PAIRS)
                    for t in range(TB):
                        for m in range(PAIRS):
                            ins = pe.matmul(tail[:, t * P:(t + 1) * P], hid[:, m, t * P:(t + 1) * P], w2_0[:, m, :],
                                            start=(m == 0), stop=(m == PAIRS - 1))
                    ins.then_inc(tail_full[2], 1)
                    turn_norm_on_tensor(pe, 2, b, 3)

            @block.scalar
            def _(act):
                with act.Fori(0, B) as b:
                    tails = b * TAIL_USES[2]
                    act.wait_ge(h3_ready[2], b * PAIRS)
                    nc.scalar.copy(x_cur[:, :], x_feat[:, bass.ds(b * S, S)]).then_inc(cur_ready[2], 1)
                    for m in range(PAIRS):
                        act.wait_ge(h1_ready[2], b * PAIRS + m + 1)
                        act.wait_ge(hid_ready[2], b * PAIRS + max(m - 1, 0))
                        nc.scalar.activation(sil[m % 2][:, :], h1[m % 2], ACT.Silu).then_inc(silu_ready[2], 1)
                        if m == 0:
                            router_on_scalar(act, 2, b)
                        if m == 1:
                            act.wait_ge(tail_full[2], tails + 2)
                            act.wait_ge(gb_ready, b * RP)
                            nc.scalar.copy(g_t[:, :], tail[0:E8, :]).then_inc(gt_ready, 1)
                            act.wait_ge(gt_ready, b + 1)
                            nc.scalar.copy(tg[0:1, 0:1], tg[0:1, 0:1]).then_inc(tail_read[2], 1)
                    act.wait_ge(tail_full[2], tails + 4)
                    nc.scalar.copy(x_pad[:, bass.ds(b, 1), 1:S + 1], tail[:, :].unsqueeze(1)).then_inc(tail_read[2], 1)

            @block.vector
            def _(dve):
                dve.wait_ge(ld_ffn0, 6 * 16)
                with dve.Fori(0, B) as b:
                    steps = Steps(dve, step[2], b * FFN0_STEPS, FFN0_STEPS)
                    router_on_vector(dve, 2, b, steps, r0_b[:, :])
                    for m in range(PAIRS):
                        w = m % 2
                        dve.wait_ge(silu_ready[2], b * PAIRS + m + 1)
                        src = sil[w][:, :]
                        if m == 0:
                            dve.wait_ge(tail_full[2], b * TAIL_USES[2])
                        if m < RP:
                            dve.wait_ge(gb_ready, b * RP + m + 1)
                            nc.vector.tensor_tensor(sg[w][:, :], src, gb[w], ALU.mult).then_inc(gs_ready, 1)
                            dve.wait_ge(gs_ready, b * RP + m + 1)
                            src = sg[w][:, :]
                        dve.wait_ge(h3_ready[2], b * PAIRS + m + 1)
                        nc.vector.tensor_tensor(hid[:, m, :], src, h3[w], ALU.mult).then_inc(hid_ready[2], 1)
                    residual_on_vector(dve, 2, b, 2)
                    norm_on_vector(dve, 2, b, steps)
                    steps.close()

        with ExitStack() as three:
            mix = {q: sb(f"mix_{q}", [P, S], ctx=three) for q in "kvr"}
            mtmp = sb("mtmp", [P, S], ctx=three)
            wtab = sb("wtab", [P, CT, S], ctx=three)
            ubk = sb("ubk", [P, CT], ctx=three)
            wneg = sb("wneg", [P, CT], ctx=three)
            brh = sb("brh", [P, CT], ctx=three)
            ones = sb("ones", [P, S], ctx=three)
            w_half = w_out
            karg = [sb(f"karg{u}", [P, S], ctx=three) for u in range(2)]
            e_wu = [sb(f"e_wu{u}", [P, 2, S], ctx=three) for u in range(2)]
            e_w, e_u = [t[:, 0, :] for t in e_wu], [t[:, 1, :] for t in e_wu]
            val = [sb(f"val{u}", [P, S], ctx=three) for u in range(2)]
            ev = [sb(f"ev{u}", [P, S], ctx=three) for u in range(2)]
            euv = [sb(f"euv{u}", [P, S], ctx=three) for u in range(2)]
            sum_e = [sb(f"sum_e{u}", [P, S], ctx=three) for u in range(2)]
            sum_ev = [sb(f"sum_ev{u}", [P, S], ctx=three) for u in range(2)]
            th = [sb(f"th{u}", [P, S], ctx=three) for u in range(2)]
            num = sb("num", [P, CT, S], ctx=three)
            den = sb("den", [P, CT, S], ctx=three)
            RWKV_STEPS = NORM_STEPS + 1
            HALF = CT // 2
            kb_, vb_, rb_ = (bank[0], bank[1]), (bank[2], bank[3]), (bank[4], bank[5])
            COLS = {"bk": 0, "bv": 1, "br": 2, "td": 3, "u": 4}

            def first(b, c, back):
                return isinstance(b, int) and b * CT + c < back

            def col(name, c):
                return cols[:, COLS[name], c:c + 1]

            block = three.enter_context(nc.Block())

            @block.sync
            def _(sp):
                sp.wait_ge(const_ready, 4)
                rows = x_sorted.rearrange("(p n) d -> p (n d)", p=P)
                for k in range(0, SLOTS // P * D, ZW):
                    sp.dma_start(rows[:, k:k + ZW], zeros[:, :]).then_inc(cleared, 16)

            @block.gpsimd
            def _(pool):
                def tile(b, c):
                    w, n = c % 2, b * CT + c
                    pool.wait_ge(vb_ready, n + 1)
                    pool.wait_ge(e_ready, n + 1)
                    if not first(b, c, 2):
                        pool.wait_ge(num_ready, n - 1)
                    nc.gpsimd.tensor_tensor(euv[w][:, :], e_u[w], val[w][:, :], ALU.mult).then_inc(euv_ready, 1)
                    pool.wait_ge(sb_ready, n + 1)
                    if not first(b, c, CT):
                        pool.wait_ge(y_ready, n + 1 - CT)
                    nc.gpsimd.tensor_tensor(den[:, c % CT, :], sum_e[w][:, :], e_u[w], ALU.add).then_inc(den_ready, 1)
                    pool.wait_ge(sum_ev_ready, n + 1)
                    pool.wait_ge(euv_ready, n + 1)
                    if c % CT == 0 and not first(b, c, CT):
                        pool.wait_ge(half_out, b + 1)
                    if c % CT == HALF and not first(b, c, CT):
                        pool.wait_ge(tail_full[3], b * TAIL_USES[3])
                    nc.gpsimd.tensor_tensor(num[:, c % CT, :], sum_ev[w][:, :], euv[w][:, :], ALU.add).then_inc(num_ready, 1)

                for c in range(CT + HALF):
                    tile(0, c)
                norm_on_pool(pool, 3, 0)
                with pool.Fori(1, B - 1) as b:
                    for c in range(HALF, CT + HALF):
                        tile(b, c)
                    norm_on_pool(pool, 3, b)
                for c in range(HALF, CT):
                    tile(B - 1, c)
                norm_on_pool(pool, 3, B - 1)

            @block.tensor
            def _(pe):
                pe.wait_ge(ld_rwkv, 7 * 16)
                pe.wait_ge(wout_ready, 1)
                def project(b, c):
                    w, n = c % 2, b * CT + c
                    cs = slice(c % CT * P, (c % CT + 1) * P)
                    if not first(b, c, 2):
                        pe.wait_ge(karg_ready, n - 1)
                        pe.wait_ge(eu0_ready, n - 1)
                    if c % CT == 0:
                        pe.wait_ge(mixed, (b + c // CT) * 2 + 1)
                    pe.matmul(kb_[w], w_rwkv["k"][:, cs], mix["k"][:, :], start=True, stop=True).then_inc(k_ready, 1)
                    if not first(b, c, 2):
                        pe.wait_ge(vb_ready, n - 1)
                    if c % CT == 0:
                        pe.wait_ge(mixed, (b + c // CT) * 2 + 2)
                    pe.matmul(vb_[w], w_rwkv["v"][:, cs], mix["v"][:, :], start=True, stop=True).then_inc(v_ready, 1)
                    if not first(b, c, 2):
                        pe.wait_ge(th_ready, n - 1)
                    if c % CT == 0:
                        pe.wait_ge(mix_ready, b + c // CT + 1)
                    pe.matmul(rb_[w], w_rwkv["r"][:, cs], mix["r"][:, :], start=True, stop=True).then_inc(r_ready, 1)

                def output(b, c):
                    if c == 0:
                        pe.wait_ge(tail_read[3], b * TAIL_USES[3])
                    pe.wait_ge(y_ready, b * CT + c + 1)
                    for t in range(TB):
                        ins = pe.matmul(tail[:, t * P:(t + 1) * P], num[:, c, t * P:(t + 1) * P], w_half[:, c, :],
                                        start=(c == 0 and t == 0), stop=(c == CT - 1), skip_group_check=True)
                    if c == HALF - 1:
                        ins.then_inc(half_out, 1)
                    if c == CT - 1:
                        ins.then_inc(tail_full[3], 1)

                def body(b, last):
                    output(b, 0)
                    project(b, CT - 1)
                    for c in range(1, HALF):
                        output(b, c)
                    if last:
                        for c in range(HALF, CT):
                            output(b, c)
                    else:
                        project(b, CT)
                        project(b, CT + 1)
                        for c in range(HALF, CT):
                            project(b, c + HALF + 2)
                            output(b, c)
                        project(b, CT + HALF + 2)
                    turn_norm_on_tensor(pe, 3, b, 1)

                for c in range(HALF + 3):
                    project(0, c)
                body(0, False)
                with pe.Fori(1, B - 1) as b:
                    body(b, False)
                body(B - 1, True)

            @block.scalar
            def _(act):
                act.wait_ge(ld_rwkv, 7 * 16)
                nc.scalar.mul(w_half[:, :, :], w_out[:, :, :], 0.5).then_inc(wout_ready, 1)
                act.wait_ge(wtab_ready, 1)
                def tile(b, c):
                    w, n, cc = c % 2, b * CT + c, c % CT
                    act.wait_ge(karg_ready, n + 1)
                    if not first(b, c, 2):
                        act.wait_ge(sb_ready, n - 1)
                        act.wait_ge(ev_ready, n - 1)
                        act.wait_ge(den_ready, n - 1)
                    nc.scalar.activation(e_w[w], karg[w][:, :], ACT.Exp).then_inc(e0_ready, 1)
                    nc.scalar.activation(e_u[w], kb_[w], ACT.Exp, bias=ubk[:, cc:cc + 1]).then_inc(eu0_ready, 1)
                    act.wait_ge(v_ready, n + 1)
                    if not first(b, c, 2):
                        act.wait_ge(euv_ready, n - 1)
                    nc.scalar.activation(val[w][:, :], vb_[w], ACT.Identity, bias=col("bv", cc)).then_inc(vb_ready, 1)
                    act.wait_ge(r_ready, n + 1)
                    if not first(b, c, 2):
                        act.wait_ge(gated_ready, n - 1)
                    nc.scalar.activation(th[w][:, :], rb_[w], ACT.Tanh, bias=brh[:, cc:cc + 1], scale=0.5)\
                        .then_inc(th_ready, 1)

                def invert(b, k):
                    hs = slice(k % 2 * HALF, (k % 2 + 1) * HALF)
                    act.wait_ge(den_ready, b * CT + (k + 1) * HALF)
                    nc.scalar.activation(den[:, hs, :], den[:, hs, :], ACT.Ln).then_inc(lnb_ready, 1)
                    act.wait_ge(lnb_ready, b * 2 + k + 1)
                    nc.scalar.activation(den[:, hs, :], den[:, hs, :], ACT.Exp, scale=-1.0).then_inc(inv_ready, 1)

                def body(b, last):
                    for c in range(HALF + 1, CT):
                        tile(b, c)
                    invert(b, 1)
                    if not last:
                        for c in range(CT, CT + HALF):
                            tile(b, c)
                        invert(b, 2)
                        tile(b, CT + HALF)
                    act.wait_ge(tail_full[3], b * TAIL_USES[3] + 2)
                    nc.scalar.copy(x_feat[:, bass.ds(b * S, S)], tail[:, :]).then_inc(tail_read[3], 1)

                for c in range(HALF):
                    tile(0, c)
                invert(0, 0)
                tile(0, HALF)
                body(0, False)
                with act.Fori(1, B - 1) as b:
                    body(b, False)
                body(B - 1, True)

            @block.vector
            def _(dve):
                dve.wait_ge(ld_rwkv, 7 * 16)
                dve.wait_ge(const_ready, 4)
                nc.vector.memset(ones[:, :], 1.0).then_inc(setup, 1)
                for w in range(2):
                    nc.vector.memset(sum_e[w][:, 0:1], 0.0).then_inc(setup, 1)
                    nc.vector.memset(sum_ev[w][:, 0:1], 0.0).then_inc(setup, 1)
                nc.vector.tensor_scalar(wneg[:, :], cols[:, COLS["td"], :], 0.0, -1.0, ALU.max, ALU.mult).then_inc(setup, 1)
                nc.vector.tensor_tensor(ubk[:, :], cols[:, COLS["u"], :], cols[:, COLS["bk"], :], ALU.add).then_inc(setup, 1)
                nc.vector.tensor_scalar(brh[:, :], cols[:, COLS["br"], :], 0.5, None, ALU.mult).then_inc(setup, 1)
                dve.wait_ge(setup, 8)
                for c in range(CT):
                    ins = nc.vector.tensor_scalar(wtab[:, c, :], trem[:, :], wneg[:, c:c + 1], col("bk", c), ALU.mult, ALU.add)
                ins.then_inc(wtab_ready, 1)
                dve.wait_ge(wtab_ready, 1)

                def interpolate(b):
                    if not isinstance(b, int) or b:
                        dve.wait_ge(r_ready, b * CT)
                    for k, q in enumerate("kvr"):
                        eps = MIX[q]
                        nc.vector.tensor_scalar(mtmp[:, :], x_pad[:, bass.ds(b, 1), 2:S + 2].rearrange("p o s -> p (o s)"),
                                                1.0 - eps, None, ALU.mult).then_inc(after_scaled, 1)
                        dve.wait_ge(after_scaled, b * 3 + k + 1)
                        ins = nc.vector.scalar_tensor_tensor(mix[q][:, :], x_pad[:, bass.ds(b, 1), 0:S].rearrange("p o s -> p (o s)"),
                                                             eps, mtmp[:, :], ALU.mult, ALU.add)
                        if q == "r":
                            ins.then_inc(mix_ready, 1)
                        else:
                            ins.then_inc(mixed, 1)
                            dve.wait_ge(mixed, b * 2 + k + 1)

                def key_arg(b, c):
                    w, n = c % 2, b * CT + c
                    dve.wait_ge(k_ready, n + 1)
                    if not first(b, c, 2):
                        dve.wait_ge(e0_ready, n - 1)
                    nc.vector.tensor_tensor(karg[w][:, :], kb_[w], wtab[:, c % CT, :], ALU.add).then_inc(karg_ready, 1)

                def sums(b, c):
                    w, n = c % 2, b * CT + c
                    dve.wait_ge(eu0_ready, n + 1)
                    nc.vector.tensor_scalar(e_wu[w][:, :, :], e_wu[w][:, :, :], E_MAX, E_MIN, ALU.min, ALU.max).then_inc(e_ready, 1)
                    if c % HALF < HALF - 1:
                        key_arg(b, c + 1)
                    dve.wait_ge(e_ready, n + 1)
                    if not first(b, c, 2):
                        dve.wait_ge(den_ready, n - 1)
                    nc.vector.tensor_tensor_scan(sum_e[w][:, 1:S], ones[:, 0:S - 1], e_w[w][:, 0:S - 1], 0.0,
                                                 ALU.mult, ALU.add).then_inc(sb_ready, 1)
                    if not first(b, c, HALF):
                        divide(b, c - HALF)
                    dve.wait_ge(vb_ready, n + 1)
                    nc.vector.tensor_tensor(ev[w][:, :], e_w[w], val[w][:, :], ALU.mult).then_inc(ev_ready, 1)
                    if c % HALF:
                        gate_sum(b, c - 1)
                    dve.wait_ge(ev_ready, n + 1)
                    if not first(b, c, 2):
                        dve.wait_ge(num_ready, n - 1)
                    nc.vector.tensor_tensor_scan(sum_ev[w][:, 1:S], ones[:, 0:S - 1], ev[w][:, 0:S - 1], 0.0,
                                                 ALU.mult, ALU.add).then_inc(sum_ev_ready, 1)

                def gate_sum(b, c):
                    n, cc = b * CT + c, c % CT
                    dve.wait_ge(num_ready, n + 1)
                    dve.wait_ge(th_ready, n + 1)
                    nc.vector.scalar_tensor_tensor(num[:, cc, :], th[c % 2][:, :], 1.0, num[:, cc, :], ALU.add, ALU.mult)\
                        .then_inc(gated_ready, 1)

                def divide(b, c):
                    dve.wait_ge(gated_ready, b * CT + c + 1)
                    dve.wait_ge(inv_ready, b * 2 + c // HALF + 1)
                    nc.vector.tensor_tensor(num[:, c, :], num[:, c, :], den[:, c, :], ALU.mult).then_inc(y_ready, 1)

                def body(b, last):
                    steps = Steps(dve, step[3], b * RWKV_STEPS, RWKV_STEPS)
                    for c in range(HALF, CT):
                        sums(b, c)
                    if last:
                        gate_sum(b, CT - 1)
                        for c in range(HALF, CT):
                            divide(b, c)
                    else:
                        interpolate(b + 1)
                        gate_sum(b, CT - 1)
                        key_arg(b, CT)
                        for c in range(CT, CT + HALF):
                            sums(b, c)
                        gate_sum(b, CT + HALF - 1)
                        key_arg(b, CT + HALF)
                    residual_on_vector(dve, 3, b, 0)
                    steps.did(nc.vector.tensor_tensor(x_sum[:, :, :], x_sum[:, :, :], bo[:, :, :], ALU.add))
                    steps.settle()
                    norm_on_vector(dve, 3, b, steps)
                    steps.close()

                interpolate(0)
                key_arg(0, 0)
                for c in range(HALF):
                    sums(0, c)
                key_arg(0, HALF)
                gate_sum(0, HALF - 1)
                body(0, False)
                with dve.Fori(1, B - 1) as b:
                    body(b, False)
                body(B - 1, True)

        NT = B * TB
        with ExitStack() as four:
            w_all = sb("w_all", [P, E8, 3 * HID1], ctx=four)
            lgA = sb("lgA", [P, NT, E8], ctx=four)
            mxA = sb("mxA", [P, NT, 8], ctx=four)
            miA = sb("miA", [P, NT, 8], U32, ctx=four)
            mifA = sb("mifA", [P, 2, NT], ctx=four)
            diffA = sb("diffA", [P, NT], ctx=four)
            tgA = sb("tgA", [P, NT], ctx=four)
            gate = sb("gate", [P, 2, NT], ctx=four)
            ohA = sb("ohA", [P, 2, NT, E8], ctx=four)
            chosen = sb("chosen", [P, NT, E8], ctx=four)
            tot = sb("tot", [P, E8, NT], ctx=four)
            cum = sb("cum", [P, E8, NT], ctx=four)
            one_row = sb("one_row", [P, P], ctx=four)
            cpad = sb("cpad", [P, E8 + 1], ctx=four)
            tpad = sb("tpad", [P, E8 + 1], ctx=four)
            cnt = sb("cnt", [P, E8], ctx=four)
            over = sb("over", [P, E8, NT], ctx=four)
            tiles = sb("tiles", [P, E8], ctx=four)
            off = sb("off", [P, E8], ctx=four)
            pos = sb("pos", [P, NT, E8], ctx=four)
            posk = sb("posk", [P, 2, NT, E8], ctx=four)
            slotf = sb("slotf", [P, 2, NT], ctx=four)
            slot = sb("slot", [P, 2, NT], U32, ctx=four)
            later = sb("later", [1, TILES, E8], ctx=four)
            owner_f = sb("owner_f", [1, TILES], ctx=four)
            owner = sb("owner", [1, TILES], I32, ctx=four)
            before_tri = sb("before_tri", [P, P], ctx=four)
            tile_no = sb("tile_no", [P, TILES], ctx=four)
            thr = sb("thr", [P, NT], ctx=four)
            iota_nt = sb("iota_nt", [P, NT, E8], ctx=four)
            x_in = [sb(f"x_in{w}", [P, D], ctx=four) for w in range(2)]
            xe = [sb(f"xe{w}", [P, P], ctx=four) for w in range(2)]
            sil = [sb(f"sil1{w}", [P, HID1], ctx=four) for w in range(2)]
            hid = [sb(f"hid1{w}", [P, HID1], ctx=four) for w in range(2)]
            hid_t = [sb(f"hid_t{w}", [P, HID1], ctx=four) for w in range(2)]
            y_out = [sb(f"y_out{w}", [P, D], ctx=four) for w in range(2)]
            y_got = [sb(f"y_got{k}", [P, NT, D], ctx=four) for k in range(2)]
            h1, h3, down = (bank[0], bank[1]), (bank[2], bank[3]), (bank[4], bank[5])
            COMBINE_STEPS = NORM_STEPS + TB

            def two_back(s):
                return max(s - 1, 0) if isinstance(s, int) else s - 1

            def in_steps(eng, lo, hi, body):
                turns = (hi - lo) // UNROLL
                with eng.Fori(0, turns) as turn:
                    for j in range(lo, lo + UNROLL):
                        body(turn * UNROLL + j, turn * (UNROLL // 2) + j // 2, j % 2)
                for s in range(lo + turns * UNROLL, hi):
                    body(s, s // 2, s % 2)

            block = four.enter_context(nc.Block())

            @block.sync
            def _(sp):
                for dst, src in ((before_tri, "before_tri"), (tile_no, "tile_no"), (thr, "thr")):
                    sp.dma_start(dst[:, :], a[src]).then_inc(ld_route, 16)
                sp.dma_start(iota_nt[:, :, :], a["iota_nt"]).then_inc(ld_route, 16)
                sp.dma_start(w_all[:, :, 0:HID1], a["w1_1"].rearrange("e d h -> d e h")).then_inc(ld_ffn1, 16)
                sp.dma_start(w_all[:, :, HID1:2 * HID1], a["w3_1"].rearrange("e d h -> d e h")).then_inc(ld_ffn1, 16)
                for e in range(E8):
                    sp.dma_start(w_all[:, e, 2 * HID1:].rearrange("p (f d) -> p f d", f=FT),
                                 a["w2_1"][e].rearrange("(f p) d -> p f d", p=P)).then_inc(ld_ffn1, 16)
                sp.wait_ge(scattered, 2 * NT * 16)

                def load(s, w, wait):
                    if wait:
                        sp.wait_ge(xt_full, s - 1)
                    sp.dma_start(x_in[w][:, :], x_sorted[bass.ds(s * P, P), :]).then_inc(x_loaded[w], 16)

                def store(s, w):
                    sp.wait_ge(y_done, s + 1)
                    sp.dma_start(y_sorted[bass.ds(s * P, P), :], y_out[w][:, :]).then_inc(y_stored[w], 16)

                for s in range(6):
                    load(s, s % 2, s >= 2)
                store(0, 0)

                def both(s, half, w):
                    load(s + 2, w, True)
                    store(s - 3, 1 - w)

                in_steps(sp, 4, TILES - 2, both)
                for s in range(TILES - 5, TILES):
                    store(s, s % 2)
                with sp.Fori(0, B) as b:
                    sp.wait_ge(xn_ready[4], b + 1)
                    sp.dma_start(out.rearrange("b (t p) d -> b p t d", p=P)[bass.ds(b, 1)].rearrange("o p t d -> (o p) t d"),
                                 xn[:, :, :]).then_inc(out_stored, 16)
                sp.wait_ge(out_stored, B * 16)

            @block.gpsimd
            def _(pool):
                pool.wait_ge(slot_ready, 1)
                pool.wait_ge(cleared, (SLOTS // P * D // ZW) * 16)
                for t in range(NT):
                    for k in range(2):
                        nc.gpsimd.indirect_dma_start(
                            out=x_sorted[:, :], out_offset=bass.IndirectOffsetOnAxis(ap=slot[:, k, t:t + 1], axis=0),
                            in_=x_tok[:, t, :], in_offset=None).then_inc(scattered, 16)
                for w in range(2):
                    pool.wait_ge(y_stored[w], TILES // 2 * 16)
                for b in range(B):
                    for t in range(b * TB, (b + 1) * TB):
                        for k in range(2):
                            nc.gpsimd.indirect_dma_start(
                                out=y_got[k][:, t, :], out_offset=None, in_=y_sorted[:, :],
                                in_offset=bass.IndirectOffsetOnAxis(ap=slot[:, k, t:t + 1], axis=0))\
                                .then_inc(gathered[b], 16)
                    if b:
                        norm_on_pool(pool, 4, b - 1)
                norm_on_pool(pool, 4, B - 1)

            @block.tensor
            def _(pe):
                pe.wait_ge(ld_gate, 2 * 16)
                for t in range(NT):
                    ins = pe.matmul(tail[:, t * E8:(t + 1) * E8], x_feat[:, t * P:(t + 1) * P], g_w[:, :],
                                    start=True, stop=True)
                ins.then_inc(logits_ready, 1)
                pe.wait_ge(ld_route, 4 * 16)
                pe.wait_ge(chosen_ready, 1)
                picks = chosen[:, :, :].rearrange("p t e -> p (t e)")
                pe.matmul(bank[0][:, 0:NT * E8], before_tri[:, :], picks, start=True, stop=True).then_inc(ranks_ready, 1)
                pe.matmul(bank[3][:, 0:NT * E8], one_row[:, :], picks, start=True, stop=True).then_inc(ranks_ready, 1)
                pe.wait_ge(owner_ready, 1)
                pe.wait_ge(ld_ffn1, (2 + E8) * 16)

                def expert_of(s):
                    return pe.value_load(owner[0:1, bass.ds(s, 1)], min_val=0, max_val=E8 - 1)

                def weights(e, lo, n):
                    return w_all[:, bass.ds(e, 1), lo:lo + n].rearrange("p o n -> p (o n)")

                def turn_in(s, half, w):
                    pe.wait_ge(x_loaded[w], (half + 1) * 16)
                    pe.wait_ge(xe_ready, s)
                    pe.transpose(tail[:, 0:P], x_in[w][:, :], ident[:, :]).then_inc(xt_full, 1)

                def up(s, w):
                    e = expert_of(s)
                    pe.wait_ge(xe_ready, s + 1)
                    pe.wait_ge(hid_ready[4], two_back(s))
                    pe.matmul(h1[w], xe[w][:, :], weights(e, 0, HID1), start=True, stop=True).then_inc(h1_ready[4], 1)
                    pe.matmul(h3[w], xe[w][:, :], weights(e, HID1, HID1), start=True, stop=True).then_inc(h3_ready[4], 1)

                def turn_hidden(s, w):
                    pe.wait_ge(hid_ready[4], s + 1)
                    pe.wait_ge(ht_done, s)
                    for f in range(FT):
                        ins = pe.transpose(pv[:, f * P:(f + 1) * P], hid[w][:, f * P:(f + 1) * P], ident[:, :])
                    ins.then_inc(ht_full, 1)

                def go_down(s, w):
                    e = expert_of(s)
                    pe.wait_ge(ht_done, s + 1)
                    pe.wait_ge(y_done, s)
                    for f in range(FT):
                        ins = pe.matmul(down[w][:, 0:D], hid_t[w][:, f * P:(f + 1) * P], weights(e, 2 * HID1 + f * D, D),
                                        start=(f == 0), stop=(f == FT - 1))
                    ins.then_inc(down_ready[4], 1)

                turn_in(0, 0, 0)
                up(0, 0)
                turn_in(1, 0, 1)
                up(1, 1)
                turn_hidden(0, 0)
                turn_in(2, 1, 0)

                def body(s, half, w):
                    up(s, w)
                    turn_in(s + 1, half + w, 1 - w)
                    turn_hidden(s - 1, 1 - w)
                    go_down(s - 2, w)

                in_steps(pe, 2, TILES - 2, body)
                up(TILES - 2, 0)
                turn_in(TILES - 1, TILES // 2 - 1, 1)
                turn_hidden(TILES - 3, 1)
                go_down(TILES - 4, 0)
                up(TILES - 1, 1)
                turn_hidden(TILES - 2, 0)
                go_down(TILES - 3, 1)
                turn_hidden(TILES - 1, 1)
                go_down(TILES - 2, 0)
                go_down(TILES - 1, 1)

            @block.scalar
            def _(act):
                act.wait_ge(diff_ready[4], 1)
                nc.scalar.activation(tgA[:, :], diffA[:, :], ACT.Tanh, scale=0.5).then_inc(tanh_ready[4], 1)

                def silu(s, w):
                    act.wait_ge(h1_ready[4], s + 1)
                    act.wait_ge(hid_ready[4], two_back(s))
                    nc.scalar.activation(sil[w][:, :], h1[w], ACT.Silu).then_inc(silu_ready[4], 1)

                def copy_turned(s, w):
                    act.wait_ge(ht_full, s + 1)
                    act.wait_ge(down_ready[4], two_back(s))
                    nc.scalar.copy(hid_t[w][:, :], pv[:, :]).then_inc(ht_done, 1)

                silu(0, 0)
                silu(1, 1)
                copy_turned(0, 0)

                def body(s, half, w):
                    silu(s, w)
                    copy_turned(s - 1, 1 - w)

                in_steps(act, 2, TILES, body)
                copy_turned(TILES - 1, 1)

            @block.vector
            def _(dve):
                n = [0]

                def did(ins):
                    ins.then_inc(route_step, 1)
                    n[0] += 1

                def settle():
                    dve.wait_ge(route_step, n[0])

                def flat(t):
                    return t.rearrange("p a b -> p (a b)")

                def over_experts(ap):
                    return ap.unsqueeze(2).to_broadcast([P, NT, E8])

                did(nc.vector.memset(one_row[:, :], 1.0))
                did(nc.vector.memset(cpad[:, 0:1], 0.0))
                did(nc.vector.memset(tpad[:, 0:1], 0.0))
                dve.wait_ge(logits_ready, 1)
                did(nc.vector.tensor_copy(flat(lgA[:, :, :]), tail[:, 0:NT * E8]))
                settle()
                for t in range(NT):
                    did(nc.vector.max(mxA[:, t, :], lgA[:, t, :]))
                settle()
                nc.vector.tensor_tensor(diffA[:, :], mxA[:, :, 0], mxA[:, :, 1], ALU.subtract).then_inc(diff_ready[4], 1)
                for t in range(NT):
                    did(nc.vector.max_index(miA[:, t, :], mxA[:, t, :], lgA[:, t, :]))
                settle()
                did(nc.vector.tensor_copy(mifA[:, :, :].rearrange("p k t -> p t k"), miA[:, :, 0:2]))
                dve.wait_ge(ld_route, 4 * 16)
                settle()
                for k in range(2):
                    did(nc.vector.tensor_tensor(ohA[:, k, :, :], iota_nt[:, :, :], over_experts(mifA[:, k, :]), ALU.is_equal))
                settle()
                nc.vector.tensor_tensor(chosen[:, :, :], ohA[:, 0, :, :], ohA[:, 1, :, :], ALU.add).then_inc(chosen_ready, 1)
                dve.wait_ge(tanh_ready[4], 1)
                for k, sign in enumerate((0.5, -0.5)):
                    did(nc.vector.tensor_scalar(gate[:, k, :], tgA[:, :], sign, 0.5, ALU.mult, ALU.add))
                dve.wait_ge(ranks_ready, 2)
                did(nc.vector.tensor_copy(tot[:, :, :].rearrange("p e t -> p t e"),
                                          bank[3][:, 0:NT * E8].rearrange("p (t e) -> p t e", e=E8)))
                settle()
                did(nc.vector.tensor_tensor_scan(flat(cum[:, :, :]), one_row[:, :], flat(tot[:, :, :]), 0.0, ALU.mult, ALU.add))
                settle()
                did(nc.vector.tensor_copy(cpad[:, 1:], cum[:, :, NT - 1]))
                settle()
                did(nc.vector.tensor_tensor(cnt[:, :], cpad[:, 1:], cpad[:, 0:E8], ALU.subtract))
                settle()
                did(nc.vector.tensor_tensor(over[:, :, :], cnt[:, :].unsqueeze(2).to_broadcast([P, E8, NT]),
                                            thr[:, :].unsqueeze(1).to_broadcast([P, E8, NT]), ALU.is_gt))
                did(nc.vector.tensor_tensor(cum[:, :, :], cum[:, :, :], tot[:, :, :], ALU.subtract))
                settle()
                did(nc.vector.tensor_reduce(tiles[:, :], over[:, :, :], mybir.AxisListType.X, ALU.add))
                settle()
                did(nc.vector.tensor_tensor_scan(tpad[:, 1:], one_row[:, 0:E8], tiles[:, :], 0.0, ALU.mult, ALU.add))
                settle()
                did(nc.vector.scalar_tensor_tensor(off[:, :], tpad[:, 0:E8], float(P), cpad[:, 0:E8], ALU.mult, ALU.subtract))
                did(nc.vector.tensor_tensor(later[:, :, :], tpad[0:1, 1:].unsqueeze(1).to_broadcast([1, TILES, E8]),
                                            tile_no[0:1, :].unsqueeze(2).to_broadcast([1, TILES, E8]), ALU.is_le))
                settle()
                did(nc.vector.tensor_tensor(cum[:, :, :], cum[:, :, :], off[:, :].unsqueeze(2).to_broadcast([P, E8, NT]), ALU.add))
                did(nc.vector.tensor_reduce(owner_f[:, :], later[:, :, :], mybir.AxisListType.X, ALU.add))
                settle()
                did(nc.vector.tensor_tensor(pos[:, :, :], bank[0][:, 0:NT * E8].rearrange("p (t e) -> p t e", e=E8),
                                            cum[:, :, :].rearrange("p e t -> p t e"), ALU.add))
                settle()
                for k in range(2):
                    did(nc.vector.tensor_tensor(posk[:, k, :, :], ohA[:, k, :, :], pos[:, :, :], ALU.mult))
                settle()
                did(nc.vector.tensor_reduce(slotf[:, :, :].rearrange("p k t -> p (k t)"),
                                            posk[:, :, :, :].rearrange("p k t e -> p (k t) e"), mybir.AxisListType.X, ALU.add))
                settle()
                nc.vector.tensor_copy(slot[:, :, :], slotf[:, :, :]).then_inc(slot_ready, 1)
                nc.vector.tensor_scalar(owner[:, :], owner_f[:, :], float(E8 - 1), None, ALU.min).then_inc(owner_ready, 1)
                dve.wait_ge(owner_ready, 1)
                dve.wait_ge(ld_gate, 2 * 16)
                dve.wait_ge(ld_ffn1, (2 + E8) * 16)

                def shift_in(s, w):
                    e = dve.value_load(owner[0:1, bass.ds(s, 1)], min_val=0, max_val=E8 - 1)
                    dve.wait_ge(xt_full, s + 1)
                    dve.wait_ge(h3_ready[4], two_back(s))
                    nc.vector.tensor_scalar(xe[w][:, :], tail[:, 0:P], dom[:, bass.ds(e, 1)], None, ALU.add)\
                        .then_inc(xe_ready, 1)

                def hidden(s, w):
                    dve.wait_ge(silu_ready[4], s + 1)
                    dve.wait_ge(h3_ready[4], s + 1)
                    dve.wait_ge(ht_full, two_back(s))
                    nc.vector.tensor_tensor(hid[w][:, :], sil[w][:, :], h3[w], ALU.mult).then_inc(hid_ready[4], 1)

                def take_down(s, half, w):
                    dve.wait_ge(down_ready[4], s + 1)
                    dve.wait_ge(y_stored[w], half * 16)
                    nc.vector.tensor_copy(y_out[w][:, :], down[w][:, 0:D]).then_inc(y_done, 1)

                shift_in(0, 0)
                shift_in(1, 1)
                hidden(0, 0)
                shift_in(2, 0)
                hidden(1, 1)

                def body(s, half, w):
                    shift_in(s + 1, 1 - w)
                    take_down(s - 2, half - 1, w)
                    hidden(s, w)

                in_steps(dve, 2, TILES - 2, body)
                shift_in(TILES - 1, 1)
                take_down(TILES - 4, TILES // 2 - 2, 0)
                hidden(TILES - 2, 0)
                take_down(TILES - 3, TILES // 2 - 2, 1)
                hidden(TILES - 1, 1)
                take_down(TILES - 2, TILES // 2 - 1, 0)
                take_down(TILES - 1, TILES // 2 - 1, 1)

                for b in range(B):
                    steps = Steps(dve, step[4], b * COMBINE_STEPS, COMBINE_STEPS)
                    dve.wait_ge(gathered[b], 2 * TB * 16)
                    if b:
                        dve.wait_ge(xn_ready[4], b)
                    for t in range(TB):
                        n_t = b * TB + t
                        steps.did(nc.vector.scalar_tensor_tensor(x_sum[:, t, :], y_got[0][:, n_t, :], gate[:, 0, n_t:n_t + 1],
                                                                 x_tok[:, n_t, :], ALU.mult, ALU.add))
                    steps.settle()
                    for t in range(TB):
                        n_t = b * TB + t
                        nc.vector.scalar_tensor_tensor(x_sum[:, t, :], y_got[1][:, n_t, :], gate[:, 1, n_t:n_t + 1],
                                                       x_sum[:, t, :], ALU.mult, ALU.add).then_inc(acc_ready, 1)
                    dve.wait_ge(acc_ready, (b + 1) * TB)
                    norm_on_vector(dve, 4, b, steps)
                    steps.close()


def _constants():
    inv = np.float32(THETA) ** (-np.arange(0, DR, 2, dtype=np.float32) / np.float32(DR))
    ang = np.arange(S, dtype=np.float32)[:, None] * inv.astype(np.float32)
    row = np.arange(P) // H % DR
    cos = np.cos(ang).astype(np.float32).T[row // 2]
    sin = np.sin(ang).astype(np.float32).T[row // 2] * np.where(row % 2 == 0, -1, 1).astype(np.float32)[:, None]
    tri = np.triu(np.ones((P, P), np.float32))
    pair_sel = np.zeros((E8, RP, P), np.float32)
    for e in range(E8):
        pair_sel[e, e // 2, HID0 * (e % 2):HID0 * (e % 2 + 1)] = 1
    return {
        "cos": cos, "sin": sin, "ident": np.eye(P, dtype=np.float32), "tri": np.tile(tri, (1, 2)),
        "iota8": np.tile(np.arange(E8, dtype=np.float32), (P, TB)), "pair_sel": pair_sel,
        "before_tri": np.triu(np.ones((P, P), np.float32), 1),
        "tile_no": np.tile(np.arange(TILES, dtype=np.float32), (P, 1)),
        "thr": np.tile(np.arange(B * TB, dtype=np.float32) * P, (P, 1)),
        "iota_nt": np.tile(np.arange(E8, dtype=np.float32), (P, B * TB, 1)),
        "trem": np.tile(np.float32(S) - np.arange(1, S + 1, dtype=np.float32), (P, 1)),
    }


def _lay_out(i):
    x = i["L0_attn_x"].reshape(B * S, D)
    swap = np.arange(DR) ^ 1
    qr = i["L0_attn_W_QR"].reshape(DL, H, DR)
    kr = i["L0_attn_W_KR"]

    def feature_major(w, width):
        return w.reshape(w.shape[0], H, width).transpose(0, 2, 1).reshape(w.shape[0], H * width)

    def pairs_up(routed, shared):
        w = np.concatenate([routed, shared])
        return w.transpose(1, 0, 2).reshape(D, PAIRS, P)

    w2 = np.concatenate([i["L0_ffn_routed_w2"], i["L0_ffn_shared_w2"]])
    return {
        "x_tok": x, "x_feat": x.T,
        "wdq": i["L0_attn_W_DQ"].T, "wdkv": i["L0_attn_W_DKV"].T,
        "wuq": np.concatenate([feature_major(i["L0_attn_W_UQ"], DH), feature_major(i["L0_attn_W_QR"], DR),
                               feature_major(qr[:, :, swap].reshape(DL, H * DR), DR)], axis=1),
        "wukv": np.concatenate([feature_major(i["L0_attn_W_UK"], DH), i["L0_attn_W_UV"]], axis=1),
        "wkr_a": np.repeat(kr, H, axis=1), "wkr_b": np.repeat(kr[:, swap], H, axis=1),
        "w_o": i["L0_attn_W_O"],
        "r0_w": i["L0_ffn_router_w"], "r0_b": np.tile(i["L0_ffn_router_b"], (P, TB)),
        "w1_0": pairs_up(i["L0_ffn_routed_w1"], i["L0_ffn_shared_w1"]),
        "w3_0": pairs_up(i["L0_ffn_routed_w3"], i["L0_ffn_shared_w3"]),
        "w2_0": w2.reshape(PAIRS, P, D).transpose(1, 0, 2),
        "wk": i["L1_attn_Wk"].T, "wv": i["L1_attn_Wv"].T, "wr": i["L1_attn_Wr"].T,
        "w_out": i["L1_attn_Wo"].T.reshape(CT, P, D).transpose(1, 0, 2),
        "cols": np.stack([i[n].reshape(CT, P).T for n in
                          ("L1_attn_bk", "L1_attn_bv", "L1_attn_br", "L1_attn_time_decay", "L1_attn_U")], axis=1),
        "bo": np.tile(i["L1_attn_bo"], (P, TB, 1)),
        "g_w": i["L1_ffn_gate_w"], "dom": i["L1_ffn_dom"].T,
        "w1_1": i["L1_ffn_W1"], "w3_1": i["L1_ffn_W3"], "w2_1": i["L1_ffn_W2"],
    }


def kernel(**inputs):
    import concourse.bacc as bacc
    from concourse.bass_utils import run_bass_kernel_spmd as run

    arrays = _lay_out({k: np.asarray(v) for k, v in inputs.items()})
    arrays.update(_constants())
    nc = bacc.Bacc("TRN2", target_bir_lowering=False, num_devices=1)
    feed, aps = {}, {}
    for name, value in arrays.items():
        value = np.ascontiguousarray(value)
        feed["in_" + name] = value
        aps[name] = nc.dram_tensor("in_" + name, value.shape, mybir.dt.from_np(value.dtype), kind="ExternalInput").ap()
    out = nc.dram_tensor("out", (B, S, D), F32, kind="ExternalOutput").ap()
    network(nc, aps, out)
    return run(nc, [feed], core_ids=[0]).results[0]["out"]
```

```python
import math
from contextlib import ExitStack

import numpy as np

import concourse.bass as bass
from concourse import mybir

F32 = mybir.dt.float32
BF16 = mybir.dt.bfloat16
U32 = mybir.dt.uint32
I32 = mybir.dt.int32
ALU = mybir.AluOpType
ACT = mybir.ActivationFunctionType

B, S, D = 4, 512, 128
P = 128
TB = S // P
H, DH, DR, DL = 16, 8, 4, 32
DQK = DH + DR
E8 = 8
HID0, SH0 = 64, 2
PAIRS = (E8 + SH0) * HID0 // P
RP = E8 * HID0 // P
CH = 1024
CT = CH // P
HID1 = 512
TILES = B * S * 2 // P + E8
REGION = B * S + P
SORTED = E8 * REGION + E8 * P
RING = 4
XW = D + 1
FT = HID1 // P
LN_EPS = 1e-5
THETA = 10000.0

LAYER_ID, N_LAYERS = 1, 12
_EPS = math.exp(-LAYER_ID / N_LAYERS)
MIX = {"k": _EPS + 0.3 * LAYER_ID / (N_LAYERS - 1), "v": _EPS, "r": _EPS / 2.0}

QK_SCALE = 1.0 / math.sqrt(DQK)
P_MIN, P_MAX = math.exp(-80.0 * QK_SCALE), math.exp(80.0 * QK_SCALE)
E_MIN, E_MAX = math.exp(-20.0), math.exp(10.0)

Q_PART = (0, 1, 2, 0, 1, 0)
K_PART = (0, 0, 0, 1, 1, 2)
STACK = len(Q_PART) * DQK

def runs(order):
    out, at = [], 0
    while at < len(order):
        n = 1
        while at + n < len(order) and order[at + n] == order[at] + n:
            n += 1
        out.append((at, n))
        at += n
    return out


STACK_DMAS = len(runs(Q_PART)) + len(runs(K_PART))


KB_AT = (0, 512, 1024, 896)
KB_LEN = tuple(S - P * kb for kb in range(TB))
SC = 1280


class Steps:

    def __init__(self, eng, sem, first, total):
        self.eng, self.sem, self.first, self.total, self.n = eng, sem, first, total, 0

    def did(self, ins):
        ins.then_inc(self.sem, 1)
        self.n += 1

    def settle(self):
        self.eng.wait_ge(self.sem, self.first + self.n)

    def close(self):
        assert self.n == self.total, (self.n, self.total)


def network(nc, a, out):
    top = ExitStack()
    with top:
        def sb(name, shape, dt=F32, ctx=top):
            return ctx.enter_context(nc.sbuf_tensor(name, shape, dt))

        def sem(name):
            return top.enter_context(nc.semaphore(name))

        x_tok = sb("x_tok", [P, B * TB, D])
        x_pad = sb("x_pad", [P, B, S + 2])
        xn = sb("xn", [P, TB, D])
        x_sum = sb("x_sum", [P, TB, D])
        stats = sb("stats", [P, TB, 6])
        mv = sb("mv", [P, TB, 2])
        var_e = sb("var_e", [P, TB])
        rstd = sb("rstd", [P, TB])
        m_half = sb("m_half", [P, TB])
        ident = sb("ident", [P, P])
        iota8 = sb("iota8", [P, TB * E8])
        lg = sb("lg", [P, TB, E8])
        mx = sb("mx", [P, TB, 8])
        mi = sb("mi", [P, TB, 8], U32)
        mif = sb("mif", [P, 2, TB])
        mdiff = sb("mdiff", [P, TB])
        tg = sb("tg", [P, TB])
        g1 = sb("g1", [P, TB])
        g2 = sb("g2", [P, TB])
        oh1 = sb("oh1", [P, TB, E8])
        oh2 = sb("oh2", [P, TB, E8])
        gates = sb("gates", [P, TB, E8])
        r0_w = sb("r0_w", [P, E8])
        r0_b = sb("r0_b", [P, TB * E8])
        pair_sel = sb("pair_sel", [3 * E8, RP, P])
        w_rwkv = {q: sb(f"w_{q}", [P, CH]) for q in "kvr"}
        w_out = sb("w_out", [P, CT, D])
        cols = sb("cols", [P, 5, CT])
        bo = sb("bo", [P, TB, D])
        trem = sb("trem", [P, S])
        g_w = sb("g_w", [P, E8])
        dom = sb("dom", [P, E8])

        early = top.enter_context(ExitStack())
        x_feat = sb("x_feat", [P, B * S], ctx=early)
        w_o = sb("w_o", [P, D], ctx=early)
        w1_0 = sb("w1_0", [P, PAIRS, P], ctx=early)
        w3_0 = sb("w3_0", [P, PAIRS, P], ctx=early)
        w2_0 = sb("w2_0", [P, PAIRS, D], ctx=early)

        tail = top.enter_context(nc.psum_tensor("tail", [P, S], F32))
        pv = top.enter_context(nc.psum_tensor("pv", [P, S], F32))
        sc = [top.enter_context(nc.psum_tensor(f"sc{u}", [P, 3 * S], F32)) for u in range(2)]
        bank = [sc[k // 3][:, (k % 3) * S:(k % 3 + 1) * S] for k in range(6)]

        q_split = nc.dram_tensor("q_split", [B, 3, DQK * H, S], BF16).ap()
        k_split = nc.dram_tensor("k_split", [B, 3, DQK * H, S], BF16).ap()
        x_sorted = nc.dram_tensor("x_sorted", [SORTED, XW], F32).ap()
        y_rows = nc.dram_tensor("y_rows", [2 * B * S + 2 * E8 * P, D], F32).ap()

        ld_attn, ld_rope, ld_x = sem("ld_attn"), sem("ld_rope"), sem("ld_x")
        ld_xf = [sem(f"ld_xf{b}") for b in range(B)]
        ld_ffn0, ld_rwkv, ld_ffn1 = sem("ld_ffn0"), sem("ld_rwkv"), sem("ld_ffn1")
        split_stored = [sem(f"split_stored{b}") for b in range(B)]
        stack_loaded = [[sem(f"stack_loaded{u}{g}") for g in range(H // 4)] for u in range(2)]
        const_ready = sem("const_ready")
        v_const = sem("v_const")
        fold_mm, fold_ready = sem("fold_mm"), sem("fold_ready")
        qc_mm, kc_mm, rope_mm, v_mm = sem("qc_mm"), sem("kc_mm"), sem("rope_mm"), sem("v_mm")
        rope_ready, rot_ready = sem("rope_ready"), sem("rot_ready")
        part0_ready, res_ready = sem("part0_ready"), sem("res_ready")
        part1_ready, part2_ready = sem("part1_ready"), sem("part2_ready")
        v_stored, rden_ready, clipped, masked = (sem(n) for n in ("v_stored", "rden_ready", "clipped", "masked"))
        v_cur_ready = sem("v_cur_ready")
        scores_ready, exp_ready, probs_ready, pv_ready = (sem(n) for n in ("scores_ready", "exp_ready", "probs_ready", "pv_ready"))
        pv_read = sem("pv_read")
        tail_full = {n: sem(f"tail_full{n}") for n in range(1, 4)}
        tail_read = {n: sem(f"tail_read{n}") for n in range(1, 4)}
        step = {n: sem(f"dve_step{n}") for n in range(1, 5)}
        var_ready = {n: sem(f"var_ready{n}") for n in range(1, 5)}
        rstd_ready = {n: sem(f"rstd_ready{n}") for n in range(1, 5)}
        xn_ready = {n: sem(f"xn_ready{n}") for n in range(1, 5)}
        tok_stored = {n: sem(f"tok_stored{n}") for n in range(1, 4)}
        diff_ready = {n: sem(f"diff_ready{n}") for n in (2, 4)}
        tanh_ready = {n: sem(f"tanh_ready{n}") for n in (2, 4)}
        parts_ready, sel_ready = sem("parts_ready"), sem("sel_ready")
        h1_ready = {n: sem(f"h1_ready{n}") for n in (2, 4)}
        h3_ready = {n: sem(f"h3_ready{n}") for n in (2, 4)}
        silu_ready = {n: sem(f"silu_ready{n}") for n in (2, 4)}
        hid_ready = {n: sem(f"hid_ready{n}") for n in (2, 4)}
        logits_ready2, gates_turned, g12_ready, router_step, weigh_step = (
            sem(n) for n in ("logits_ready2", "gates_turned", "g12_ready", "router_step", "weigh_step"))
        gt_ready, gb_ready, gs_ready = sem("gt_ready"), sem("gb_ready"), sem("gs_ready")
        down_ready = sem("down_ready")
        mix_ready, k_ready, v_ready, r_ready = (sem(n) for n in ("mix_ready", "k_ready", "v_ready", "r_ready"))
        karg_ready, eu0_ready, vb_ready, th_ready, e0_ready = (sem(n) for n in ("karg_ready", "eu0_ready", "vb_ready", "th_ready", "e0_ready"))
        euv_ready, den_ready, e_ready, ev_ready, sb_ready = (sem(n) for n in ("euv_ready", "den_ready", "e_ready", "ev_ready", "sb_ready"))
        lnb_ready, inv_ready, y_ready, wtab_ready, wout_ready, num_ready, mixed, setup, gated_ready = (
            sem(n) for n in ("lnb_ready", "inv_ready", "y_ready", "wtab_ready", "wout_ready", "num_ready", "mixed", "setup", "gated_ready"))
        after_scaled, sum_ev_ready, half_out = sem("after_scaled"), sem("sum_ev_ready"), sem("half_out")
        xe_ready = sem("xe_ready")
        ld_gate = sem("ld_gate")
        cleared, scattered, logits_ready, chosen_ready, slot_ready, owner_ready, route_step = (
            sem(n) for n in ("cleared", "scattered", "logits_ready", "chosen_ready", "slot_ready", "owner_ready", "route_step"))
        x_loaded, y_stored = [sem(f"x_loaded{w}") for w in range(RING)], [sem(f"y_stored{w}") for w in range(RING)]
        ld_ids, ids_set, row_copied, place_ready = sem("ld_ids"), sem("ids_set"), sem("row_copied"), sem("place_ready")
        counts_ready, counts_read, gate_set, table_step, table_ready, pad_ready = (
            sem(n) for n in ("counts_ready", "counts_read", "gate_set", "table_step", "table_ready", "pad_ready"))
        xt_full, ht_full, ht_done, y_done = (sem(n) for n in ("xt_full", "ht_full", "ht_done", "y_done"))
        gathered = [sem(f"gathered{b}") for b in range(B)]
        out_stored = sem("out_stored")

        def wait_apart(eng, semaphore, count):
            if not isinstance(count, int):
                count = eng.to_reg(count)
                eng.wait_ge(const_ready, 3)
            eng.wait_ge(semaphore, count)

        def residual_on_vector(dve, n, b, use):
            dve.wait_ge(tail_full[n], b * TAIL_USES[n] + use + 1)
            nc.vector.tensor_tensor(x_sum[:, :, :], tail[:, :].rearrange("p (t d) -> p t d", t=TB),
                                    x_tok[:, bass.ds(b * TB, TB), :], ALU.add).then_inc(tail_read[n], 1)
            dve.wait_ge(tail_read[n], b * TAIL_USES[n] + use + 1)

        def norm_on_vector(dve, n, b, steps):
            norm_stats(dve, n, steps)
            norm_apply(dve, n, b, steps)

        def norm_stats(dve, n, steps):
            for t in range(TB):
                steps.did(nc.vector.bn_stats(stats[:, t, :], x_sum[:, t, :]))
            wait_apart(dve, steps.sem, steps.first + steps.n)
            for t in range(TB):
                steps.did(nc.vector.bn_aggr(mv[:, t, :], stats[:, t, :]))
            steps.settle()
            nc.vector.tensor_scalar(var_e[:, :], mv[:, :, 1], LN_EPS, None, ALU.add).then_inc(var_ready[n], 1)

        def norm_apply(dve, n, b, steps):
            dve.wait_ge(rstd_ready[n], b + 1)
            dve.wait_ge(tail_full[n], b * TAIL_USES[n])
            dve.wait_ge(tok_stored[n], b)
            for t in range(TB):
                ins = nc.vector.tensor_scalar(xn[:, t, :], x_sum[:, t, :], mv[:, t, 0:1], rstd[:, t:t + 1],
                                              ALU.subtract, ALU.mult)
                if t < TB - 1:
                    steps.did(ins)
            ins.then_inc(xn_ready[n], 1)
        NORM_STEPS = 2 * TB + (TB - 1)
        TAIL_USES = {1: H // 4 + 3, 2: 2, 3: 2}

        def norm_on_pool(pool, n, b):
            pool.wait_ge(var_ready[n], b + 1)
            nc.gpsimd.tensor_tensor(rstd[:, :], var_e[:, :], m_half[:, :], ALU.pow).then_inc(rstd_ready[n], 1)
            if n < 3:
                pool.wait_ge(xn_ready[n], b + 1)
                nc.gpsimd.tensor_copy(x_tok[:, bass.ds(b * TB, TB), :], xn[:, :, :]).then_inc(tok_stored[n], 1)

        def turn_norm_on_tensor(pe, n, b, use):
            pe.wait_ge(xn_ready[n], b + 1)
            pe.wait_ge(tail_read[n], b * TAIL_USES[n] + use)
            for t in range(TB):
                ins = pe.transpose(tail[:, t * P:(t + 1) * P], xn[:, t, :], ident[:, :])
            ins.then_inc(tail_full[n], 1)

        with ExitStack() as one:
            wdq = sb("wdq", [DL, D], ctx=one)
            wdkv = sb("wdkv", [DL, D], ctx=one)
            wuq = sb("wuq", [DL, 2 * P], ctx=one)
            wukv = sb("wukv", [DL, 2 * P], ctx=one)
            f_q = sb("f_q", [P, P], ctx=one)
            f_k = sb("f_k", [P, P], ctx=one)
            f_v = sb("f_v", [P, P], ctx=one)
            f_ra = sb("f_ra", [P, P], ctx=one)
            f_rb = sb("f_rb", [P, P], ctx=one)
            cos = sb("cos", [P, S], ctx=one)
            sin = sb("sin", [P, S], ctx=one)
            tri = sb("tri", [P, 2 * P], ctx=one)
            ra = sb("ra", [P, S], ctx=one)
            rb = sb("rb", [P, S], ctx=one)
            rot = sb("rot", [P, S], ctx=one)
            res = [sb(f"res{k}", [P, S], ctx=one) for k in range(3)]
            part = [[sb(f"part{u}{k}", [P, 3, S], BF16, ctx=one) for k in range(3)] for u in range(2)]
            v_all = sb("v_all", [P, B * TB, D], ctx=one)
            DV = DH + 1
            v_cur = [sb(f"v_cur{u}", [P, TB, H * DV + 32 - DV], ctx=one) for u in range(2)]
            q_st = [sb(f"q_st{u}", [STACK, H, S], BF16, ctx=one) for u in range(2)]
            k_st = [sb(f"k_st{u}", [STACK, H, S], BF16, ctx=one) for u in range(2)]
            probs = [sb(f"probs{u}", [P, SC], ctx=one) for u in range(4)]
            o_feat = sb("o_feat", [P, S], ctx=one)
            rden = sb("rden", [P, TB, 4], ctx=one)
            o_tok = sb("o_tok", [P, TB, D], ctx=one)
            o_t = sb("o_t", [P, S], ctx=one)
            HH, GROUPS = 2 * H, 2 * H // 4
            TURN_OUT, PROJECT, TURN_NORM = H + 5, H + 6, H + 9

            TAIL_ORDER = [("group", g) for g in range(4)] + [("out", 0), ("project", 0), ("group", 4), ("norm", 0)] \
                + [("group", g) for g in range(5, 8)] + [("out", 1), ("project", 1), ("norm", 1)]

            def tails_before(pair, what, k):
                return pair * len(TAIL_ORDER) + TAIL_ORDER.index((what, k))

            def use_of_batch(what, u):
                return TAIL_ORDER.index((what, u)) - u * TAIL_USES[1]

            plain = ((bank[0], bank[1]), (tail[:, :], pv[:, :]))

            block = one.enter_context(nc.Block())

            @block.sync
            def _(sp):
                attn_loads = ((wdq[:, :], a["wdq"]), (wdkv[:, :], a["wdkv"]), (wuq[:, :], a["wuq"]),
                              (wukv[:, :], a["wukv"]), (f_ra[:, P // 2:], a["wkr_a"]), (f_rb[:, P // 2:], a["wkr_b"]))
                for dst, src in attn_loads:
                    sp.dma_start(dst, src).then_inc(ld_attn, 16)
                for b in range(B):
                    sp.dma_start(x_feat[:, b * S:(b + 1) * S], a["x_feat"][:, b * S:(b + 1) * S]).then_inc(ld_xf[b], 16)
                    if b == 0:
                        sp.dma_start(cos[:, :], a["cos"]).then_inc(ld_rope, 16)
                        sp.dma_start(sin[:, :], a["sin"]).then_inc(ld_rope, 16)
                for dst, src in ((w_o[:, :], a["w_o"]), (ident[:, :], a["ident"]), (tri[:, :], a["tri"]),
                                 (iota8[:, :], a["iota8"])):
                    sp.dma_start(dst, src).then_inc(ld_x, 16)
                sp.dma_start(x_tok[:, :, :], a["x_tok"].rearrange("(n p) d -> p n d", p=P)).then_inc(ld_x, 16)
                def store_split(b):
                    u = b % 2
                    sp.wait_ge(part2_ready, 3 * b + 3)
                    sp.wait_ge(part1_ready, 3 * b + 3)
                    sp.wait_ge(part0_ready, 3 * b + 3)
                    c = DH * H
                    for dram, k, lo in ((q_split, 0, 0), (k_split, 1, P // 2)):
                        rows = dram[b].rearrange("s r c -> r s c")
                        sp.dma_start(rows[0:c], part[u][k][:, :, :]).then_inc(split_stored[b], 16)
                        sp.dma_start(rows[c:], part[u][2][lo:lo + P // 2, :, :]).then_inc(split_stored[b], 16)

                def load_stacks(b):
                    u = b % 2
                    sp.wait_ge(split_stored[b], 4 * 16)
                    if b >= 2:
                        sp.wait_ge(scores_ready, H * (b - 1))
                    for g in range(H // 4):
                        hs = slice(4 * g, 4 * g + 4)
                        for dst, dram, order in ((q_st[u], q_split, Q_PART), (k_st[u], k_split, K_PART)):
                            rows = dram[b].rearrange("s (k h) c -> (s k) h c", h=H)
                            for at, n in runs(order):
                                sp.dma_start(dst[at * DQK:(at + n) * DQK, hs, :],
                                             rows[order[at] * DQK:(order[at] + n) * DQK, hs]).then_inc(stack_loaded[u][g], 16)

                store_split(0)
                store_split(1)
                load_stacks(0)
                store_split(2)
                store_split(3)
                for b in range(1, B):
                    load_stacks(b)
                for dst, src in ((r0_w[:, :], a["r0_w"]), (r0_b[:, :], a["r0_b"]), (w1_0[:, :, :], a["w1_0"]),
                                 (w3_0[:, :, :], a["w3_0"]), (w2_0[:, :, :], a["w2_0"]), (pair_sel[:, :, :], a["pair_sel"])):
                    sp.dma_start(dst, src).then_inc(ld_ffn0, 16)
                for dst, src in ((w_rwkv["k"][:, :], a["wk"]), (w_rwkv["v"][:, :], a["wv"]), (w_rwkv["r"][:, :], a["wr"]),
                                 (w_out[:, :, :], a["w_out"]), (cols[:, :, :], a["cols"]), (bo[:, :, :], a["bo"]),
                                 (trem[:, :], a["trem"])):
                    sp.dma_start(dst, src).then_inc(ld_rwkv, 16)
                for dst, src in ((g_w[:, :], a["g_w"]), (dom[:, :], a["dom"])):
                    sp.dma_start(dst, src).then_inc(ld_gate, 16)

            @block.gpsimd
            def _(pool):
                for u in range(2):
                    nc.gpsimd.memset(v_cur[u][:, :, :], 1.0).then_inc(v_const, 1)
                nc.gpsimd.memset(m_half[:, :], -0.5).then_inc(const_ready, 1)
                nc.gpsimd.memset(x_pad[:, :, 0:1], 0.0).then_inc(const_ready, 1)
                nc.gpsimd.memset(x_pad[:, :, S + 1:S + 2], 0.0).then_inc(const_ready, 1)
                for b in range(B):
                    u = b % 2
                    for k in range(3):
                        pool.wait_ge(part1_ready, 3 * b + k + 1)
                        nc.gpsimd.tensor_tensor(part[u][k][:, 2, :], res[k][:, :], part[u][k][:, 1, :], ALU.subtract)\
                            .then_inc(part2_ready, 1)
                pool.wait_ge(const_ready, 3)
                pool.wait_ge(v_stored, B)
                pool.wait_ge(v_const, 2)
                with pool.Fori(0, B // 2) as pair:
                    pool.wait_ge(pv_ready, pair * HH)
                    for u in range(2):
                        nc.gpsimd.tensor_copy(v_cur[u][:, :, 0:H * DV].rearrange("p t (h d) -> p t h d", d=DV)[:, :, :, 0:DH],
                                              v_all[:, bass.ds((pair * 2 + u) * TB, TB), :].rearrange("p t (h d) -> p t h d", h=H))\
                            .then_inc(v_cur_ready, 1)
                    for u in range(2):
                        norm_on_pool(pool, 1, pair * 2 + u)

            @block.tensor
            def _(pe):
                pe.wait_ge(ld_attn, 6 * 16)
                pe.matmul(bank[0][:, 0:2 * P], wdq[:, :], wuq[:, :], start=True, stop=True).then_inc(fold_mm, 1)
                pe.matmul(bank[1][:, 0:2 * P], wdkv[:, :], wukv[:, :], start=True, stop=True).then_inc(fold_mm, 1)
                pe.wait_ge(fold_ready, 5)
                for b in range(B):
                    x = x_feat[:, b * S:(b + 1) * S]
                    pe.wait_ge(ld_xf[b], 16)
                    if b >= 2:
                        pe.wait_ge(res_ready, 3 * (b - 1))
                    pe.matmul(plain[b % 2][0], f_q[:, :], x, start=True, stop=True).then_inc(qc_mm, 1)
                    pe.matmul(plain[b % 2][1], f_k[:, :], x, start=True, stop=True).then_inc(kc_mm, 1)
                    pe.wait_ge(rope_ready, 2 * b)
                    pe.matmul(bank[2], f_ra[:, :], x, start=True, stop=True).then_inc(rope_mm, 1)
                    pe.matmul(bank[3], f_rb[:, :], x, start=True, stop=True).then_inc(rope_mm, 1)
                    pe.wait_ge(v_stored, b)
                    for t in range(TB):
                        ins = pe.matmul(bank[4][:, t * P:(t + 1) * P], x[:, t * P:(t + 1) * P], f_v[:, :],
                                        start=True, stop=True)
                    ins.then_inc(v_mm, 1)
                pe.wait_ge(part0_ready, 3 * B)
                pe.wait_ge(rope_ready, 2 * B)
                pe.wait_ge(res_ready, 3 * B)
                pe.wait_ge(v_stored, B)
                pe.wait_ge(ld_x, 5 * 16)

                with pe.Fori(0, B // 2) as pair:
                    def scores(m):
                        u, h = m // H, m % H
                        if h % 4 == 0:
                            pe.wait_ge(stack_loaded[u][h // 4], (pair + 1) * (16 * STACK_DMAS))
                        pe.wait_ge(exp_ready, pair * HH + max(m - 1, 0))
                        for kb in range(TB):
                            ins = pe.matmul(sc[m % 2][:, KB_AT[kb]:KB_AT[kb] + KB_LEN[kb]],
                                            k_st[u][:, h, kb * P:(kb + 1) * P], q_st[u][:, h, kb * P:S],
                                            start=True, stop=True)
                        ins.then_inc(scores_ready, 1)

                    def values(m):
                        u, h, j = m // H, m % H, m % 4
                        if h == 0:
                            pe.wait_ge(v_cur_ready, pair * 2 + u + 1)
                        pe.wait_ge(probs_ready, pair * HH + (m + 1))
                        pe.wait_ge(pv_read, pair * HH + max(m - 3, 0))
                        for kb in range(TB):
                            ins = pe.matmul(pv[32 * j:32 * j + 32, kb * P:S], v_cur[u][:, kb, h * DV:h * DV + 32],
                                            probs[j][:, KB_AT[kb]:KB_AT[kb] + KB_LEN[kb]],
                                            start=(kb == 0), stop=(kb == TB - 1))
                        ins.then_inc(pv_ready, 1)

                    def turn_group(g):
                        pe.wait_ge(pv_read, pair * HH + 4 * (g + 1))
                        pe.wait_ge(tail_read[1], tails_before(pair, "group", g))
                        for t in range(TB):
                            ins = pe.transpose(tail[:, t * P:(t + 1) * P], o_feat[:, t * P:(t + 1) * P], ident[:, :])
                        ins.then_inc(tail_full[1], 1)

                    def turn_out(u):
                        pe.wait_ge(tail_read[1], tails_before(pair, "out", u))
                        for t in range(TB):
                            ins = pe.transpose(tail[:, t * P:(t + 1) * P], o_tok[:, t, :], ident[:, :])
                        ins.then_inc(tail_full[1], 1)

                    def project(u):
                        pe.wait_ge(tail_read[1], tails_before(pair, "project", u))
                        for t in range(TB):
                            ins = pe.matmul(tail[:, t * P:(t + 1) * P], o_t[:, t * P:(t + 1) * P], w_o[:, :],
                                            start=True, stop=True)
                        ins.then_inc(tail_full[1], 1)

                    for m in range(HH + 2):
                        if m < HH:
                            scores(m)
                        if m > 4 and m % 4 == 3:
                            turn_group(m // 4 - 1)
                        if m == TURN_OUT:
                            turn_out(0)
                        if m == PROJECT:
                            project(0)
                        if m == TURN_NORM:
                            turn_norm_on_tensor(pe, 1, pair * 2, use_of_batch("norm", 0))
                        if m >= 2:
                            values(m - 2)
                    turn_group(GROUPS - 1)
                    turn_out(1)
                    project(1)
                    turn_norm_on_tensor(pe, 1, pair * 2 + 1, use_of_batch("norm", 1))

            @block.scalar
            def _(act):
                act.wait_ge(fold_mm, 2)
                half = P // 2
                for dst, src in ((f_q[:, :], bank[0][:, 0:P]), (f_ra[:, 0:half], bank[0][:, P:P + half]),
                                 (f_rb[:, 0:half], bank[0][:, P + half:2 * P]), (f_k[:, :], bank[1][:, 0:P]),
                                 (f_v[:, :], bank[1][:, P:2 * P])):
                    nc.scalar.copy(dst, src).then_inc(fold_ready, 1)
                for b in range(B):
                    u = b % 2
                    if b >= 2:
                        act.wait_ge(split_stored[b - 2], 4 * 16)
                    for k, ready, src in ((0, qc_mm, plain[u][0]), (1, kc_mm, plain[u][1]), (2, rot_ready, rot[:, :])):
                        act.wait_ge(ready, b + 1)
                        nc.scalar.copy(part[u][k][:, 0, :], src).then_inc(part0_ready, 1)
                    act.wait_ge(v_mm, b + 1)
                    nc.scalar.copy(v_all[:, b * TB:(b + 1) * TB, :], bank[4].rearrange("p (t d) -> p t d", t=TB))\
                        .then_inc(v_stored, 1)
                    for k in range(3):
                        act.wait_ge(res_ready, 3 * b + k + 1)
                        nc.scalar.copy(part[u][k][:, 1, :], res[k][:, :]).then_inc(part1_ready, 1)

                with act.Fori(0, B // 2) as pair:
                    def keep_sums(m):
                        rows = slice(32 * (m % 4), 32 * (m % 4) + 32)
                        act.wait_ge(pv_ready, pair * HH + (m + 1))
                        act.wait_ge(tail_full[1], tails_before(pair, "group", m // 4 - 1) + 1 if m >= 4 else pair * len(TAIL_ORDER))
                        nc.scalar.copy(o_feat[rows, :], pv[rows, :]).then_inc(pv_read, 1)

                    def keep_turned(u):
                        act.wait_ge(tail_full[1], tails_before(pair, "out", u) + 1)
                        nc.scalar.copy(o_t[:, :], tail[:, :]).then_inc(tail_read[1], 1)

                    def keep_features(u):
                        act.wait_ge(tail_full[1], tails_before(pair, "norm", u) + 1)
                        nc.scalar.copy(x_feat[:, bass.ds((pair * 2 + u) * S, S)], tail[:, :]).then_inc(tail_read[1], 1)

                    for m in range(HH + 3):
                        if m < HH:
                            act.wait_ge(scores_ready, pair * HH + (m + 1))
                            act.wait_ge(pv_ready, pair * HH + max(m - 3, 0))
                            nc.scalar.activation(probs[m % 4][:, :], sc[m % 2][:, 0:SC], ACT.Exp, scale=QK_SCALE)\
                                .then_inc(exp_ready, 1)
                        if m >= 3:
                            keep_sums(m - 3)
                        if m == TURN_OUT:
                            keep_turned(0)
                        if m == TURN_NORM:
                            keep_features(0)
                    keep_turned(1)
                    keep_features(1)

            @block.vector
            def _(dve):
                for b in range(B):
                    u = b % 2
                    dve.wait_ge(rot_ready, b)
                    dve.wait_ge(rope_mm, 2 * b + 1)
                    dve.wait_ge(ld_rope, 2 * 16)
                    nc.vector.tensor_tensor(ra[:, :], bank[2], cos[:, :], ALU.mult).then_inc(rope_ready, 1)
                    dve.wait_ge(rope_mm, 2 * b + 2)
                    nc.vector.tensor_tensor(rb[:, :], bank[3], sin[:, :], ALU.mult).then_inc(rope_ready, 1)
                    dve.wait_ge(rope_ready, 2 * b + 2)
                    dve.wait_ge(part0_ready, 3 * b)
                    dve.wait_ge(res_ready, 3 * b)
                    nc.vector.tensor_tensor(rot[:, :], ra[:, :], rb[:, :], ALU.add).then_inc(rot_ready, 1)
                    for k, src in enumerate((plain[u][0], plain[u][1], rot[:, :])):
                        dve.wait_ge(part0_ready, 3 * b + k + 1)
                        if b:
                            dve.wait_ge(part2_ready, 3 * (b - 1) + k + 1)
                            dve.wait_ge(part1_ready, 3 * (b - 1) + k + 1)
                        nc.vector.tensor_tensor(res[k][:, :], src, part[u][k][:, 0, :], ALU.subtract)\
                            .then_inc(res_ready, 1)
                dve.wait_ge(ld_x, 5 * 16)

                with dve.Fori(0, B // 2) as pair:
                    steps = [Steps(dve, step[1], (pair * 2 + u) * NORM_STEPS, NORM_STEPS) for u in range(2)]

                    def clip_and_mask(m):
                        p = probs[m % 4]
                        dve.wait_ge(exp_ready, pair * HH + (m + 1))
                        nc.vector.tensor_scalar(p[:, :], p[:, :], P_MIN, P_MAX, ALU.max, ALU.min).then_inc(clipped, 1)
                        dve.wait_ge(clipped, pair * HH + (m + 1))
                        diag = p[:, 0:2 * S].rearrange("p (k c) -> p k c", c=S)[:, :, 0:P]
                        nc.vector.tensor_tensor(
                            diag, diag, tri[:, :].rearrange("p (k c) -> p k c", c=P), ALU.mult).then_inc(masked, 1)
                        pair_23 = p[:, KB_AT[3]:KB_AT[2] + P]
                        nc.vector.tensor_tensor(pair_23, pair_23, tri[:, :], ALU.mult).then_inc(probs_ready, 1)

                    def normalise(g):
                        gh = g % (H // 4)
                        dve.wait_ge(tail_full[1], tails_before(pair, "group", g) + 1)
                        t4 = tail[:, :].rearrange("p (t j c) -> p t j c", t=TB, j=4)
                        nc.vector.reciprocal(rden[:, :, :], t4[:, :, :, DH]).then_inc(rden_ready, 1)
                        dve.wait_ge(rden_ready, pair * GROUPS + (g + 1))
                        ov = o_tok[:, :, :].rearrange("p t (h d) -> p t h d", d=DH)[:, :, 4 * gh:4 * gh + 4, :]
                        nc.vector.tensor_tensor(ov, t4[:, :, :, 0:DH],
                                                rden[:, :, :].unsqueeze(3).to_broadcast([P, TB, 4, DH]), ALU.mult)\
                            .then_inc(tail_read[1], 1)

                    def add_and_norm(u):
                        residual_on_vector(dve, 1, pair * 2 + u, use_of_batch("project", u))
                        norm_on_vector(dve, 1, pair * 2 + u, steps[u])
                        steps[u].close()

                    for m in range(HH):
                        clip_and_mask(m)
                        if m > 4 and m % 4 == 3:
                            normalise(m // 4 - 1)
                        if m == PROJECT:
                            add_and_norm(0)
                    normalise(GROUPS - 1)
                    add_and_norm(1)

        with ExitStack() as two:
            sil = [sb(f"sil{u}", [P, S], ctx=two) for u in range(2)]
            sg = [sb(f"sg{u}", [P, S], ctx=two) for u in range(2)]
            hid = [sb(f"hid{u}", [P, PAIRS, S], ctx=two) for u in range(2)]
            sel = sb("sel", [3 * E8, RP, P], BF16, ctx=two)
            g_head = sb("g_head", [P, 2, TB, E8], BF16, ctx=two)
            g_rest = sb("g_rest", [P, TB, E8], ctx=two)
            g_parts = sb("g_parts", [P, TB, 3, E8], ctx=two)
            g_t = sb("g_t", [3 * E8, S], BF16, ctx=two)
            h1, h3, gb = (bank[0], bank[1]), (bank[2], bank[3]), (bank[4], bank[5])
            ORDER = [RP, *range(RP)]
            ROUTER_STEPS = 2 * TB + 4

            block = two.enter_context(nc.Block())

            @block.gpsimd
            def _(pool):
                for b in range(B):
                    norm_on_pool(pool, 2, b)

            @block.tensor
            def _(pe):
                def x_of(b):
                    return x_feat[:, b * S:(b + 1) * S]

                def route(b):
                    if b:
                        pe.wait_ge(gt_ready, b)
                    for t in range(TB):
                        ins = pe.matmul(pv[:, t * E8:(t + 1) * E8], x_of(b)[:, t * P:(t + 1) * P], r0_w[:, :],
                                        start=True, stop=True)
                    ins.then_inc(logits_ready2, 1)

                def turn_gates(b):
                    pe.wait_ge(parts_ready, b + 1)
                    for t in range(TB):
                        ins = pe.transpose(pv[0:3 * E8, t * P:(t + 1) * P], g_parts[:, t, :, :].rearrange("p k e -> p (k e)"), ident[:, :])
                    ins.then_inc(gates_turned, 1)

                def up(b, i):
                    q, m = b * PAIRS + i, ORDER[i]
                    if q >= 2:
                        pe.wait_ge(silu_ready[2], q - 1)
                        pe.wait_ge(hid_ready[2], q - 1)
                    pe.matmul(h1[q % 2], w1_0[:, m, :], x_of(b), start=True, stop=True).then_inc(h1_ready[2], 1)
                    pe.matmul(h3[q % 2], w3_0[:, m, :], x_of(b), start=True, stop=True).then_inc(h3_ready[2], 1)

                def spread_gates(b, m):
                    r = b * RP + m
                    if m == 0:
                        pe.wait_ge(gt_ready, b + 1)
                        pe.wait_ge(sel_ready, 1)
                    if r >= 2:
                        pe.wait_ge(gs_ready, r - 1)
                    pe.matmul(gb[r % 2], sel[:, m, :], g_t[:, :], start=True, stop=True).then_inc(gb_ready, 1)

                def down(b):
                    pe.wait_ge(hid_ready[2], (b + 1) * PAIRS)
                    pe.wait_ge(tail_read[2], b * TAIL_USES[2])
                    for t in range(TB):
                        for m in range(PAIRS):
                            ins = pe.matmul(tail[:, t * P:(t + 1) * P], hid[b % 2][:, m, t * P:(t + 1) * P], w2_0[:, m, :],
                                            start=(m == 0), stop=(m == PAIRS - 1))
                    ins.then_inc(tail_full[2], 1)

                pe.wait_ge(ld_ffn0, 6 * 16)
                route(0)
                for b in range(B):
                    up(b, 0)
                    up(b, 1)
                    turn_gates(b)
                    if b:
                        down(b - 1)
                    spread_gates(b, 0)
                    if b + 1 < B:
                        route(b + 1)
                    for i in range(2, PAIRS):
                        up(b, i)
                        spread_gates(b, ORDER[i])
                        if b and i == PAIRS - 1:
                            turn_norm_on_tensor(pe, 2, b - 1, 1)
                down(B - 1)
                turn_norm_on_tensor(pe, 2, B - 1, 1)

            @block.scalar
            def _(act):
                def silu(b, i):
                    q = b * PAIRS + i
                    act.wait_ge(h1_ready[2], q + 1)
                    if q >= 2:
                        act.wait_ge(hid_ready[2], q - 1)
                    nc.scalar.activation(sil[q % 2][:, :], h1[q % 2], ACT.Silu).then_inc(silu_ready[2], 1)

                def softmax_part(b):
                    act.wait_ge(diff_ready[2], b + 1)
                    if b:
                        act.wait_ge(g12_ready, 2 * b)
                    nc.scalar.activation(tg[:, :], mdiff[:, :], ACT.Tanh, scale=0.5).then_inc(tanh_ready[2], 1)

                def keep_gates(b):
                    act.wait_ge(gates_turned, b + 1)
                    if b:
                        act.wait_ge(gb_ready, b * RP)
                    nc.scalar.copy(g_t[:, :], pv[0:3 * E8, :]).then_inc(gt_ready, 1)

                def keep_features(b):
                    act.wait_ge(tail_full[2], (b + 1) * TAIL_USES[2])
                    nc.scalar.copy(x_pad[:, b, 1:S + 1], tail[:, :]).then_inc(tail_read[2], 1)

                act.wait_ge(ld_ffn0, 6 * 16)
                nc.scalar.copy(sel[:, :, :], pair_sel[:, :, :]).then_inc(sel_ready, 1)
                softmax_part(0)
                for b in range(B):
                    silu(b, 0)
                    silu(b, 1)
                    keep_gates(b)
                    for i in range(2, PAIRS):
                        silu(b, i)
                    if b + 1 < B:
                        softmax_part(b + 1)
                    if b:
                        keep_features(b - 1)
                keep_features(B - 1)

            @block.vector
            def _(dve):
                norms = [Steps(dve, step[2], b * NORM_STEPS, NORM_STEPS) for b in range(B)]

                def route(b):
                    steps = Steps(dve, router_step, b * ROUTER_STEPS, ROUTER_STEPS)
                    dve.wait_ge(logits_ready2, b + 1)
                    steps.did(nc.vector.tensor_tensor(lg[:, :, :].rearrange("p t e -> p (t e)"), pv[:, 0:TB * E8],
                                                      r0_b[:, :], ALU.add))
                    steps.settle()
                    for t in range(TB):
                        steps.did(nc.vector.max(mx[:, t, :], lg[:, t, :]))
                    steps.settle()
                    if b:
                        dve.wait_ge(tanh_ready[2], b)
                    nc.vector.tensor_tensor(mdiff[:, :], mx[:, :, 0], mx[:, :, 1], ALU.subtract).then_inc(diff_ready[2], 1)
                    for t in range(TB):
                        steps.did(nc.vector.max_index(mi[:, t, :], mx[:, t, :], lg[:, t, :]))
                    steps.settle()
                    steps.did(nc.vector.tensor_copy(mif[:, :, :].rearrange("p k t -> p t k"), mi[:, :, 0:2]))
                    steps.settle()
                    io = iota8[:, :].rearrange("p (t e) -> p t e", t=TB)
                    for k, oh in enumerate((oh1, oh2)):
                        steps.did(nc.vector.tensor_tensor(
                            oh[:, :, :], io, mif[:, k, :].unsqueeze(2).to_broadcast([P, TB, E8]), ALU.is_equal))
                    steps.close()

                def weigh(b):
                    steps = Steps(dve, weigh_step, b * 8, 8)
                    dve.wait_ge(tanh_ready[2], b + 1)
                    nc.vector.tensor_scalar(g1[:, :], tg[:, :], 0.5, 0.5, ALU.mult, ALU.add).then_inc(g12_ready, 1)
                    nc.vector.tensor_scalar(g2[:, :], tg[:, :], -0.5, 0.5, ALU.mult, ALU.add).then_inc(g12_ready, 1)
                    dve.wait_ge(g12_ready, 2 * (b + 1))
                    dve.wait_ge(router_step, (b + 1) * ROUTER_STEPS)
                    for oh, g in ((oh1, g1), (oh2, g2)):
                        steps.did(nc.vector.tensor_tensor(oh[:, :, :], oh[:, :, :],
                                                          g[:, :].unsqueeze(2).to_broadcast([P, TB, E8]), ALU.mult))
                    steps.settle()
                    steps.did(nc.vector.tensor_tensor(gates[:, :, :], oh1[:, :, :], oh2[:, :, :], ALU.add))
                    steps.settle()
                    steps.did(nc.vector.tensor_copy(g_head[:, 0, :, :], gates[:, :, :]))
                    steps.settle()
                    if b:
                        dve.wait_ge(gates_turned, b)
                    steps.did(nc.vector.tensor_copy(g_parts[:, :, 0, :], g_head[:, 0, :, :]))
                    steps.did(nc.vector.tensor_tensor(g_rest[:, :, :], gates[:, :, :], g_head[:, 0, :, :], ALU.subtract))
                    steps.settle()
                    steps.did(nc.vector.tensor_copy(g_head[:, 1, :, :], g_rest[:, :, :]))
                    steps.settle()
                    steps.did(nc.vector.tensor_copy(g_parts[:, :, 1, :], g_head[:, 1, :, :]))
                    nc.vector.tensor_tensor(g_parts[:, :, 2, :], g_rest[:, :, :], g_head[:, 1, :, :], ALU.subtract)\
                        .then_inc(parts_ready, 1)
                    steps.close()

                def hidden(b, i):
                    q, m = b * PAIRS + i, ORDER[i]
                    w = q % 2
                    dve.wait_ge(silu_ready[2], q + 1)
                    src = sil[w]
                    if m < RP:
                        r = b * RP + m
                        dve.wait_ge(gb_ready, r + 1)
                        if q >= 2:
                            dve.wait_ge(hid_ready[2], q - 1)
                        nc.vector.tensor_tensor(sg[w][:, :], src[:, :], gb[r % 2], ALU.mult).then_inc(gs_ready, 1)
                        dve.wait_ge(gs_ready, r + 1)
                        src = sg[w]
                    dve.wait_ge(h3_ready[2], q + 1)
                    if i == 0 and b >= 2:
                        dve.wait_ge(tail_full[2], (b - 2) * TAIL_USES[2] + 1)
                    nc.vector.tensor_tensor(hid[b % 2][:, m, :], src[:, :], h3[w], ALU.mult).then_inc(hid_ready[2], 1)

                dve.wait_ge(ld_ffn0, 6 * 16)
                route(0)
                weigh(0)
                for b in range(B):
                    hidden(b, 0)
                    if b:
                        residual_on_vector(dve, 2, b - 1, 0)
                        norm_stats(dve, 2, norms[b - 1])
                    hidden(b, 1)
                    if b:
                        norm_apply(dve, 2, b - 1, norms[b - 1])
                        norms[b - 1].close()
                    hidden(b, 2)
                    if b + 1 < B:
                        route(b + 1)
                    hidden(b, 3)
                    hidden(b, 4)
                    if b + 1 < B:
                        weigh(b + 1)
                residual_on_vector(dve, 2, B - 1, 0)
                norm_on_vector(dve, 2, B - 1, norms[B - 1])
                norms[B - 1].close()

        early.close()
        NT = B * TB
        w_all = sb("w_all", [P, E8, 3 * HID1])
        x_row = [sb(f"x_row{k}", [P, TB, XW]) for k in range(2)]
        cnt = sb("cnt", [1, E8])
        over = sb("over", [1, E8, NT])
        tiles = sb("tiles", [1, E8])
        tiles_to = sb("tiles_to", [1, E8])
        skip = sb("skip", [1, E8])
        later = sb("later", [1, TILES, E8])
        skipped = sb("skipped", [1, TILES, E8])
        owner_f = sb("owner_f", [1, TILES])
        row_f = sb("row_f", [1, TILES])
        owner = sb("owner", [1, TILES], I32)
        first_row = sb("first_row", [1, TILES], I32)
        pad_row = sb("pad_row", [1, E8], I32)
        tile_no = sb("tile_no", [P, TILES])
        thr = sb("thr", [P, NT])
        x_now = sb("x_now", [P, S])
        ids = sb("ids", [P, 2, TB])
        batch_len = sb("batch_len", [P, TB])
        before_tri = sb("before_tri", [P, P])
        one_row = sb("one_row", [P, P])
        region = sb("region", [P, E8])
        chosen = sb("chosen", [P, TB, E8])
        start = sb("start", [P, TB + 1, E8])
        pos = sb("pos", [P, TB, E8])
        posk = sb("posk", [P, 2, TB, E8])
        slotf = sb("slotf", [P, 2, TB])
        slot = sb("slot", [P, 2, TB], U32)
        gate = sb("gate", [P, 2, NT])
        with ExitStack() as three:
            mix = {q: sb(f"mix_{q}", [P, S], ctx=three) for q in "kvr"}
            mtmp = sb("mtmp", [P, S], ctx=three)
            wtab = sb("wtab", [P, CT, S], ctx=three)
            ubk = sb("ubk", [P, CT], ctx=three)
            wneg = sb("wneg", [P, CT], ctx=three)
            brh = sb("brh", [P, CT], ctx=three)
            ones = sb("ones", [P, S], ctx=three)
            w_half = w_out
            karg = [sb(f"karg{u}", [P, S], ctx=three) for u in range(2)]
            e_wu = [sb(f"e_wu{u}", [P, 2, S], ctx=three) for u in range(2)]
            e_w, e_u = [t[:, 0, :] for t in e_wu], [t[:, 1, :] for t in e_wu]
            val = [sb(f"val{u}", [P, S], ctx=three) for u in range(2)]
            ev = [sb(f"ev{u}", [P, S], ctx=three) for u in range(2)]
            euv = [sb(f"euv{u}", [P, S], ctx=three) for u in range(2)]
            sum_e = [sb(f"sum_e{u}", [P, S], ctx=three) for u in range(2)]
            sum_ev = [sb(f"sum_ev{u}", [P, S], ctx=three) for u in range(2)]
            th = [sb(f"th{u}", [P, S], ctx=three) for u in range(2)]
            num = sb("num", [P, CT, S], ctx=three)
            den = sb("den", [P, CT, S], ctx=three)
            RWKV_STEPS = NORM_STEPS + 1
            TABLE_STEPS = 9
            ROUTE_STEPS = 2 * TB + 4 + TB + 4
            HALF = CT // 2
            kb_, vb_, rb_ = (bank[0], bank[1]), (bank[2], bank[3]), (bank[4], bank[5])
            COLS = {"bk": 0, "bv": 1, "br": 2, "td": 3, "u": 4}

            def first(b, c, back):
                return isinstance(b, int) and b * CT + c < back

            def col(name, c):
                return cols[:, COLS[name], c:c + 1]

            block = three.enter_context(nc.Block())

            @block.sync
            def _(sp):
                sp.dma_start(ids[:, :, :], a["ids"]).then_inc(ld_ids, 16)
                sp.dma_start(before_tri[:, :], a["before_tri"]).then_inc(ld_ids, 16)
                sp.dma_start(region[:, :], a["region"]).then_inc(ld_ids, 16)
                for dst, src in ((tile_no, "tile_no"), (thr, "thr")):
                    sp.dma_start(dst[:, :], a[src]).then_inc(ld_ids, 16)
                sp.dma_start(x_sorted[E8 * REGION:, :], a["blank_rows"][E8 * P:, :]).then_inc(cleared, 16)
                sp.dma_start(w_all[:, :, 0:HID1], a["w1_1"].rearrange("e d h -> d e h")).then_inc(ld_ffn1, 16)
                sp.dma_start(w_all[:, :, HID1:2 * HID1], a["w3_1"].rearrange("e d h -> d e h")).then_inc(ld_ffn1, 16)
                for e in range(E8):
                    sp.dma_start(w_all[:, e, 2 * HID1:].rearrange("p (f d) -> p f d", f=FT),
                                 a["w2_1"][e].rearrange("(f p) d -> p f d", p=P)).then_inc(ld_ffn1, 16)
                sp.wait_ge(pad_ready, 1)
                for e in range(E8):
                    row = sp.value_load(pad_row[0:1, e:e + 1], min_val=0, max_val=SORTED - P)
                    sp.dma_start(x_sorted[bass.ds(row, P), :], a["blank_rows"][e * P:(e + 1) * P, :]).then_inc(cleared, 16)

            @block.gpsimd
            def _(pool):
                def tile(b, c):
                    w, n = c % 2, b * CT + c
                    pool.wait_ge(vb_ready, n + 1)
                    pool.wait_ge(e_ready, n + 1)
                    if not first(b, c, 2):
                        pool.wait_ge(num_ready, n - 1)
                    nc.gpsimd.tensor_tensor(euv[w][:, :], e_u[w], val[w][:, :], ALU.mult).then_inc(euv_ready, 1)
                    pool.wait_ge(sb_ready, n + 1)
                    if not first(b, c, CT):
                        pool.wait_ge(y_ready, n + 1 - CT)
                    nc.gpsimd.tensor_tensor(den[:, c % CT, :], sum_e[w][:, :], e_u[w], ALU.add).then_inc(den_ready, 1)
                    pool.wait_ge(sum_ev_ready, n + 1)
                    pool.wait_ge(euv_ready, n + 1)
                    if c % CT == 0 and not first(b, c, CT):
                        pool.wait_ge(half_out, b + 1)
                    if c % CT == HALF and not first(b, c, CT):
                        pool.wait_ge(tail_full[3], b * TAIL_USES[3])
                    nc.gpsimd.tensor_tensor(num[:, c % CT, :], sum_ev[w][:, :], euv[w][:, :], ALU.add).then_inc(num_ready, 1)

                def scatter(b, i):
                    t, k = i // 2, i % 2
                    if i == 0:
                        pool.wait_ge(scattered, b * (2 * TB * 16))
                        for row in x_row:
                            nc.gpsimd.tensor_tensor(row[:, :, D], row[:, :, D], batch_len[:, :], ALU.add)\
                                .then_inc(ids_set, 1)
                        wait_apart(pool, slot_ready, b + 1)
                        wait_apart(pool, row_copied, (b + 1) * 2)
                        wait_apart(pool, ids_set, (b + 2) * 2)
                    nc.gpsimd.indirect_dma_start(
                        out=x_sorted[:, :], out_offset=bass.IndirectOffsetOnAxis(ap=slot[:, k, t:t + 1], axis=0),
                        in_=x_row[k][:, t, :], in_offset=None).then_inc(scattered, 16)

                nc.gpsimd.memset(batch_len[:, :], float(S)).then_inc(v_const, 1)
                pool.wait_ge(v_const, 3)
                pool.wait_ge(ld_ids, 5 * 16)
                for k in range(2):
                    nc.gpsimd.tensor_copy(x_row[k][:, :, D], ids[:, k, :]).then_inc(ids_set, 1)
                for c in range(CT + HALF):
                    tile(0, c)
                norm_on_pool(pool, 3, 0)
                with pool.Fori(1, B - 1) as b:
                    for c in range(HALF, CT + HALF):
                        tile(b, c)
                        if c >= CT:
                            scatter(b - 1, c - CT)
                    norm_on_pool(pool, 3, b)
                    for i in range(HALF, 2 * TB):
                        scatter(b - 1, i)
                for c in range(HALF, CT):
                    tile(B - 1, c)
                for i in range(HALF):
                    scatter(B - 2, i)
                norm_on_pool(pool, 3, B - 1)
                for i in range(HALF, 2 * TB):
                    scatter(B - 2, i)
                for i in range(2 * TB):
                    scatter(B - 1, i)

            @block.tensor
            def _(pe):
                pe.wait_ge(ld_rwkv, 7 * 16)
                pe.wait_ge(wout_ready, 1)
                def project(b, c):
                    w, n = c % 2, b * CT + c
                    cs = slice(c % CT * P, (c % CT + 1) * P)
                    if not first(b, c, 2):
                        pe.wait_ge(karg_ready, n - 1)
                        pe.wait_ge(eu0_ready, n - 1)
                    if c % CT == 0:
                        pe.wait_ge(mixed, (b + c // CT) * 2 + 1)
                    pe.matmul(kb_[w], w_rwkv["k"][:, cs], mix["k"][:, :], start=True, stop=True).then_inc(k_ready, 1)
                    if not first(b, c, 2):
                        pe.wait_ge(vb_ready, n - 1)
                    if c % CT == 0:
                        pe.wait_ge(mixed, (b + c // CT) * 2 + 2)
                    pe.matmul(vb_[w], w_rwkv["v"][:, cs], mix["v"][:, :], start=True, stop=True).then_inc(v_ready, 1)
                    if not first(b, c, 2):
                        pe.wait_ge(th_ready, n - 1)
                    if c % CT == 0:
                        pe.wait_ge(mix_ready, b + c // CT + 1)
                    pe.matmul(rb_[w], w_rwkv["r"][:, cs], mix["r"][:, :], start=True, stop=True).then_inc(r_ready, 1)

                def output(b, c):
                    if c == 0:
                        pe.wait_ge(tail_read[3], b * TAIL_USES[3])
                    pe.wait_ge(y_ready, b * CT + c + 1)
                    for t in range(TB):
                        ins = pe.matmul(tail[:, t * P:(t + 1) * P], num[:, c, t * P:(t + 1) * P], w_half[:, c, :],
                                        start=(c == 0 and t == 0), stop=(c == CT - 1), skip_group_check=True)
                    if c == HALF - 1:
                        ins.then_inc(half_out, 1)
                    if c == CT - 1:
                        ins.then_inc(tail_full[3], 1)

                def logits(b):
                    pe.wait_ge(tail_read[3], (b + 1) * TAIL_USES[3])
                    pe.wait_ge(counts_read, b)
                    for t in range(TB):
                        ins = pe.matmul(pv[:, t * E8:(t + 1) * E8], x_now[:, t * P:(t + 1) * P], g_w[:, :],
                                        start=True, stop=True)
                    ins.then_inc(logits_ready, 1)

                def counts(b):
                    pe.wait_ge(chosen_ready, b + 1)
                    picks = chosen[:, :, :].rearrange("p t e -> p (t e)")
                    n = TB * E8
                    pe.matmul(pv[:, n:2 * n], before_tri[:, :], picks, start=True, stop=True)
                    pe.matmul(pv[:, 2 * n:3 * n], one_row[:, :], picks, start=True, stop=True).then_inc(counts_ready, 1)

                pe.wait_ge(ld_gate, 2 * 16)
                pe.wait_ge(ld_ids, 5 * 16)

                def body(b, last):
                    begun = not isinstance(b, int) or b > 0
                    output(b, 0)
                    if begun:
                        logits(b - 1)
                    project(b, CT - 1)
                    for c in range(1, HALF):
                        if begun and c == HALF - 1:
                            counts(b - 1)
                        output(b, c)
                    if last:
                        for c in range(HALF, CT):
                            output(b, c)
                    else:
                        project(b, CT)
                        project(b, CT + 1)
                        for c in range(HALF, CT):
                            project(b, c + HALF + 2)
                            output(b, c)
                    turn_norm_on_tensor(pe, 3, b, 1)
                    if not last:
                        project(b, CT + HALF + 2)

                for c in range(HALF + 3):
                    project(0, c)
                body(0, False)
                with pe.Fori(1, B - 1) as b:
                    body(b, False)
                body(B - 1, True)
                logits(B - 1)
                counts(B - 1)

            @block.scalar
            def _(act):
                act.wait_ge(ld_rwkv, 7 * 16)
                nc.scalar.mul(w_half[:, :, :], w_out[:, :, :], 0.5).then_inc(wout_ready, 1)
                act.wait_ge(wtab_ready, 1)
                def tile(b, c):
                    w, n, cc = c % 2, b * CT + c, c % CT
                    act.wait_ge(karg_ready, n + 1)
                    if not first(b, c, 2):
                        act.wait_ge(sb_ready, n - 1)
                        act.wait_ge(ev_ready, n - 1)
                        act.wait_ge(den_ready, n - 1)
                    nc.scalar.activation(e_w[w], karg[w][:, :], ACT.Exp).then_inc(e0_ready, 1)
                    nc.scalar.activation(e_u[w], kb_[w], ACT.Exp, bias=ubk[:, cc:cc + 1]).then_inc(eu0_ready, 1)
                    act.wait_ge(v_ready, n + 1)
                    if not first(b, c, 2):
                        act.wait_ge(euv_ready, n - 1)
                    nc.scalar.activation(val[w][:, :], vb_[w], ACT.Identity, bias=col("bv", cc)).then_inc(vb_ready, 1)
                    act.wait_ge(r_ready, n + 1)
                    if not first(b, c, 2):
                        act.wait_ge(gated_ready, n - 1)
                    nc.scalar.activation(th[w][:, :], rb_[w], ACT.Tanh, bias=brh[:, cc:cc + 1], scale=0.5)\
                        .then_inc(th_ready, 1)

                def invert(b, k):
                    hs = slice(k % 2 * HALF, (k % 2 + 1) * HALF)
                    act.wait_ge(den_ready, b * CT + (k + 1) * HALF)
                    nc.scalar.activation(den[:, hs, :], den[:, hs, :], ACT.Ln).then_inc(lnb_ready, 1)
                    act.wait_ge(lnb_ready, b * 2 + k + 1)
                    nc.scalar.activation(den[:, hs, :], den[:, hs, :], ACT.Exp, scale=-1.0).then_inc(inv_ready, 1)

                def weigh(b):
                    act.wait_ge(diff_ready[4], b + 1)
                    act.wait_ge(gate_set, 2 * b)
                    nc.scalar.activation(tg[:, :], mdiff[:, :], ACT.Tanh, scale=0.5).then_inc(tanh_ready[4], 1)

                def copy_rows(b):
                    act.wait_ge(tok_stored[3], b + 1)
                    act.wait_ge(scattered, b * (2 * TB * 16))
                    for k in range(2):
                        nc.scalar.copy(x_row[k][:, :, 0:D], x_tok[:, bass.ds(b * TB, TB), :]).then_inc(row_copied, 1)

                def body(b, last):
                    for c in range(HALF + 1, CT):
                        tile(b, c)
                    if not isinstance(b, int) or b:
                        copy_rows(b - 1)
                    if not isinstance(b, int) or b:
                        weigh(b - 1)
                    invert(b, 1)
                    if not last:
                        for c in range(CT, CT + HALF):
                            tile(b, c)
                        invert(b, 2)
                        tile(b, CT + HALF)
                    act.wait_ge(tail_full[3], b * TAIL_USES[3] + 2)
                    act.wait_ge(logits_ready, b)
                    nc.scalar.copy(x_now[:, :], tail[:, :]).then_inc(tail_read[3], 1)
                    act.wait_ge(xn_ready[3], b + 1)
                    nc.scalar.copy(x_tok[:, bass.ds(b * TB, TB), :], xn[:, :, :]).then_inc(tok_stored[3], 1)

                for c in range(HALF):
                    tile(0, c)
                invert(0, 0)
                tile(0, HALF)
                body(0, False)
                with act.Fori(1, B - 1) as b:
                    body(b, False)
                body(B - 1, True)
                copy_rows(B - 1)
                weigh(B - 1)

            @block.vector
            def _(dve):
                dve.wait_ge(ld_rwkv, 7 * 16)
                dve.wait_ge(const_ready, 3)
                def interpolate(b):
                    if not isinstance(b, int) or b:
                        dve.wait_ge(r_ready, b * CT)
                    for k, q in enumerate("kvr"):
                        eps = MIX[q]
                        nc.vector.tensor_scalar(mtmp[:, :], x_pad[:, bass.ds(b, 1), 2:S + 2].rearrange("p o s -> p (o s)"),
                                                1.0 - eps, None, ALU.mult).then_inc(after_scaled, 1)
                        dve.wait_ge(after_scaled, b * 3 + k + 1)
                        ins = nc.vector.scalar_tensor_tensor(mix[q][:, :], x_pad[:, bass.ds(b, 1), 0:S].rearrange("p o s -> p (o s)"),
                                                             eps, mtmp[:, :], ALU.mult, ALU.add)
                        if q == "r":
                            ins.then_inc(mix_ready, 1)
                        else:
                            ins.then_inc(mixed, 1)
                            dve.wait_ge(mixed, b * 2 + k + 1)

                def key_arg(b, c):
                    w, n = c % 2, b * CT + c
                    dve.wait_ge(k_ready, n + 1)
                    if not first(b, c, 2):
                        dve.wait_ge(e0_ready, n - 1)
                    nc.vector.tensor_tensor(karg[w][:, :], kb_[w], wtab[:, c % CT, :], ALU.add).then_inc(karg_ready, 1)

                def sums(b, c):
                    w, n = c % 2, b * CT + c
                    dve.wait_ge(eu0_ready, n + 1)
                    nc.vector.tensor_scalar(e_wu[w][:, :, :], e_wu[w][:, :, :], E_MAX, E_MIN, ALU.min, ALU.max).then_inc(e_ready, 1)
                    if c % HALF < HALF - 1:
                        key_arg(b, c + 1)
                    dve.wait_ge(e_ready, n + 1)
                    if not first(b, c, 2):
                        dve.wait_ge(den_ready, n - 1)
                    nc.vector.tensor_tensor_scan(sum_e[w][:, 1:S], ones[:, 0:S - 1], e_w[w][:, 0:S - 1], 0.0,
                                                 ALU.mult, ALU.add).then_inc(sb_ready, 1)
                    if not first(b, c, HALF):
                        divide(b, c - HALF)
                    dve.wait_ge(vb_ready, n + 1)
                    nc.vector.tensor_tensor(ev[w][:, :], e_w[w], val[w][:, :], ALU.mult).then_inc(ev_ready, 1)
                    if c % HALF:
                        gate_sum(b, c - 1)
                    dve.wait_ge(ev_ready, n + 1)
                    if not first(b, c, 2):
                        dve.wait_ge(num_ready, n - 1)
                    nc.vector.tensor_tensor_scan(sum_ev[w][:, 1:S], ones[:, 0:S - 1], ev[w][:, 0:S - 1], 0.0,
                                                 ALU.mult, ALU.add).then_inc(sum_ev_ready, 1)

                def gate_sum(b, c):
                    n, cc = b * CT + c, c % CT
                    dve.wait_ge(num_ready, n + 1)
                    dve.wait_ge(th_ready, n + 1)
                    nc.vector.scalar_tensor_tensor(num[:, cc, :], th[c % 2][:, :], 1.0, num[:, cc, :], ALU.add, ALU.mult)\
                        .then_inc(gated_ready, 1)

                def divide(b, c):
                    dve.wait_ge(gated_ready, b * CT + c + 1)
                    dve.wait_ge(inv_ready, b * 2 + c // HALF + 1)
                    nc.vector.tensor_tensor(num[:, c, :], num[:, c, :], den[:, c, :], ALU.mult).then_inc(y_ready, 1)

                def body(b, last):
                    steps = Steps(dve, step[3], b * RWKV_STEPS, RWKV_STEPS)
                    begun = not isinstance(b, int) or b > 0
                    if begun:
                        sorting = sorting_steps(b - 1)
                    for c in range(HALF, CT):
                        sums(b, c)
                        if begun and c == HALF + 1:
                            top_two(b - 1, sorting)
                    if last:
                        find_slots(b - 1, sorting)
                        gate_sum(b, CT - 1)
                        for c in range(HALF, CT):
                            divide(b, c)
                    else:
                        if begun:
                            find_slots(b - 1, sorting)
                        interpolate(b + 1)
                        gate_sum(b, CT - 1)
                        key_arg(b, CT)
                        for c in range(CT, CT + HALF):
                            sums(b, c)
                        key_arg(b, CT + HALF)
                    residual_on_vector(dve, 3, b, 0)
                    steps.did(nc.vector.tensor_tensor(x_sum[:, :, :], x_sum[:, :, :], bo[:, :, :], ALU.add))
                    steps.settle()
                    norm_on_vector(dve, 3, b, steps)
                    steps.close()
                    if not last:
                        gate_sum(b, CT + HALF - 1)

                def top_two(b, steps):
                    dve.wait_ge(logits_ready, b + 1)
                    steps.did(nc.vector.tensor_copy(lg[:, :, :].rearrange("p t e -> p (t e)"), pv[:, 0:TB * E8]))
                    wait_apart(dve, steps.sem, steps.first + steps.n)
                    for t in range(TB):
                        steps.did(nc.vector.max(mx[:, t, :], lg[:, t, :]))
                    wait_apart(dve, steps.sem, steps.first + steps.n)
                    for t in range(TB):
                        steps.did(nc.vector.max_index(mi[:, t, :], mx[:, t, :], lg[:, t, :]))
                    dve.wait_ge(tanh_ready[4], b)
                    nc.vector.tensor_tensor(mdiff[:, :], mx[:, :, 0], mx[:, :, 1], ALU.subtract).then_inc(diff_ready[4], 1)
                    steps.settle()
                    steps.did(nc.vector.tensor_copy(mif[:, :, :].rearrange("p k t -> p t k"), mi[:, :, 0:2]))
                    steps.settle()
                    io = iota8[:, :].rearrange("p (t e) -> p t e", t=TB)
                    for k, oh in enumerate((oh1, oh2)):
                        steps.did(nc.vector.tensor_tensor(
                            oh[:, :, :], io, mif[:, k, :].unsqueeze(2).to_broadcast([P, TB, E8]), ALU.is_equal))
                    steps.settle()
                    dve.wait_ge(counts_ready, b)
                    nc.vector.tensor_tensor(chosen[:, :, :], oh1[:, :, :], oh2[:, :, :], ALU.add).then_inc(chosen_ready, 1)

                def find_slots(b, steps):
                    dve.wait_ge(counts_ready, b + 1)
                    n = TB * E8
                    for t in range(TB):
                        steps.did(nc.vector.tensor_tensor(start[:, t + 1, :], start[:, t, :],
                                                          pv[:, 2 * n + t * E8:2 * n + (t + 1) * E8], ALU.add))
                        steps.settle()
                    nc.vector.tensor_tensor(pos[:, :, :], pv[:, n:2 * n].rearrange("p (t e) -> p t e", e=E8),
                                            start[:, 0:TB, :], ALU.add).then_inc(counts_read, 1)
                    dve.wait_ge(counts_read, b + 1)
                    for k, oh in enumerate((oh1, oh2)):
                        steps.did(nc.vector.tensor_tensor(posk[:, k, :, :], oh[:, :, :], pos[:, :, :], ALU.mult))
                    steps.did(nc.vector.tensor_copy(start[:, 0, :], start[:, TB, :]))
                    steps.settle()
                    steps.did(nc.vector.tensor_reduce(slotf[:, :, :].rearrange("p k t -> p (k t)"),
                                                      posk[:, :, :, :].rearrange("p k t e -> p (k t) e"),
                                                      mybir.AxisListType.X, ALU.add))
                    steps.settle()
                    dve.wait_ge(scattered, b * (2 * TB * 16))
                    nc.vector.tensor_copy(slot[:, :, :], slotf[:, :, :]).then_inc(slot_ready, 1)
                    dve.wait_ge(tanh_ready[4], b + 1)
                    for k, sign in enumerate((0.5, -0.5)):
                        nc.vector.tensor_scalar(gate[:, k, bass.ds(b * TB, TB)], tg[:, :], sign, 0.5, ALU.mult, ALU.add)\
                            .then_inc(gate_set, 1)
                    steps.close()

                def sorting_steps(b):
                    return Steps(dve, route_step, b * ROUTE_STEPS, ROUTE_STEPS)

                interpolate(0)
                nc.vector.memset(ones[:, :], 1.0).then_inc(setup, 1)
                for w in range(2):
                    nc.vector.memset(sum_e[w][:, 0:1], 0.0).then_inc(setup, 1)
                    nc.vector.memset(sum_ev[w][:, 0:1], 0.0).then_inc(setup, 1)
                nc.vector.tensor_scalar(wneg[:, :], cols[:, COLS["td"], :], 0.0, -1.0, ALU.max, ALU.mult).then_inc(setup, 1)
                nc.vector.tensor_tensor(ubk[:, :], cols[:, COLS["u"], :], cols[:, COLS["bk"], :], ALU.add).then_inc(setup, 1)
                nc.vector.tensor_scalar(brh[:, :], cols[:, COLS["br"], :], 0.5, None, ALU.mult).then_inc(setup, 1)
                dve.wait_ge(setup, 8)
                for c in range(CT):
                    ins = nc.vector.tensor_scalar(wtab[:, c, :], trem[:, :], wneg[:, c:c + 1], col("bk", c), ALU.mult, ALU.add)
                ins.then_inc(wtab_ready, 1)
                dve.wait_ge(wtab_ready, 1)
                dve.wait_ge(ld_ids, 5 * 16)
                nc.vector.memset(one_row[:, :], 1.0).then_inc(setup, 1)
                nc.vector.tensor_copy(start[:, 0, :], region[:, :]).then_inc(setup, 1)
                dve.wait_ge(setup, 10)
                key_arg(0, 0)
                for c in range(HALF):
                    sums(0, c)
                key_arg(0, HALF)
                gate_sum(0, HALF - 1)
                body(0, False)
                with dve.Fori(1, B - 1) as b:
                    body(b, False)
                body(B - 1, True)
                sorting = sorting_steps(B - 1)
                top_two(B - 1, sorting)
                find_slots(B - 1, sorting)

                steps = Steps(dve, table_step, 0, TABLE_STEPS)
                did, settle = steps.did, steps.settle
                nc.vector.tensor_copy(pad_row[:, :], start[0:1, 0, :]).then_inc(pad_ready, 1)
                dve.wait_ge(route_step, B * ROUTE_STEPS)
                did(nc.vector.tensor_tensor(cnt[:, :], start[0:1, 0, :], region[0:1, :], ALU.subtract))
                settle()
                did(nc.vector.tensor_tensor(over[:, :, :], cnt[:, :].unsqueeze(2).to_broadcast([1, E8, NT]),
                                            thr[0:1, :].unsqueeze(1).to_broadcast([1, E8, NT]), ALU.is_gt))
                settle()
                did(nc.vector.tensor_reduce(tiles[:, :], over[:, :, :], mybir.AxisListType.X, ALU.add))
                settle()
                did(nc.vector.tensor_tensor_scan(tiles_to[:, :], one_row[0:1, 0:E8], tiles[:, :], 0.0, ALU.mult, ALU.add))
                did(nc.vector.tensor_scalar(skip[:, :], tiles[:, :], float(-P), float(REGION), ALU.mult, ALU.add))
                settle()
                did(nc.vector.tensor_tensor(later[:, :, :], tiles_to[:, :].unsqueeze(1).to_broadcast([1, TILES, E8]),
                                            tile_no[0:1, :].unsqueeze(2).to_broadcast([1, TILES, E8]), ALU.is_le))
                settle()
                did(nc.vector.tensor_reduce(owner_f[:, :], later[:, :, :], mybir.AxisListType.X, ALU.add))
                did(nc.vector.tensor_tensor(skipped[:, :, :], later[:, :, :],
                                            skip[:, :].unsqueeze(1).to_broadcast([1, TILES, E8]), ALU.mult))
                settle()
                did(nc.vector.tensor_reduce(row_f[:, :], skipped[:, :, :], mybir.AxisListType.X, ALU.add))
                settle()
                nc.vector.scalar_tensor_tensor(first_row[:, :], tile_no[0:1, :], float(P), row_f[:, :], ALU.mult, ALU.add)\
                    .then_inc(table_ready, 1)
                nc.vector.tensor_scalar(owner[:, :], owner_f[:, :], float(E8 - 1), None, ALU.min).then_inc(owner_ready, 1)

        with ExitStack() as four:
            x_in = [sb(f"x_in{w}", [P, XW], ctx=four) for w in range(RING)]
            place = [sb(f"place{w}", [P, 1], U32, ctx=four) for w in range(RING)]
            xe = [sb(f"xe{w}", [P, P], ctx=four) for w in range(2)]
            sil = [sb(f"sil1{w}", [P, HID1], ctx=four) for w in range(2)]
            hid = [sb(f"hid1{w}", [P, HID1], ctx=four) for w in range(2)]
            hid_t = [sb(f"hid_t{w}", [P, HID1], ctx=four) for w in range(2)]
            y_out = [sb(f"y_out{w}", [P, D], ctx=four) for w in range(RING)]
            y_got = [sb(f"y_got{k}", [P, NT, D], ctx=four) for k in range(2)]
            h1, h3, down = (bank[0], bank[1]), (bank[2], bank[3]), (bank[4], bank[5])
            stats4 = sb("stats4", [P, B, TB, 6], ctx=four)
            mv4 = sb("mv4", [P, B, TB, 2], ctx=four)
            var4 = sb("var4", [P, B, TB], ctx=four)
            rstd4 = sb("rstd4", [P, B, TB], ctx=four)
            COMBINE_STEPS = 4 * TB

            def two_back(s):
                return max(s - 1, 0) if isinstance(s, int) else s - 1

            def in_steps(eng, lo, hi, body):
                turns = (hi - lo) // RING
                with eng.Fori(0, turns) as turn:
                    for j in range(lo, lo + RING):
                        body(turn * RING + j, turn + j // RING, j % RING)
                for s in range(lo + turns * RING, hi):
                    body(s, s // RING, s % RING)

            block = four.enter_context(nc.Block())

            @block.sync
            def _(sp):
                sp.wait_ge(table_ready, 1)
                sp.wait_ge(cleared, (1 + E8) * 16)
                sp.wait_ge(scattered, 2 * NT * 16)

                def load(s, w, wait):
                    row = sp.value_load(first_row[0:1, bass.ds(s, 1)], min_val=0, max_val=SORTED - P)
                    if wait:
                        sp.wait_ge(xt_full, s - RING + 1)
                        sp.wait_ge(place_ready, s - RING + 1)
                    sp.dma_start(x_in[w][:, :], x_sorted[bass.ds(row, P), :]).then_inc(x_loaded[w], 16)

                for s in range(RING):
                    load(s, s, False)
                in_steps(sp, RING, TILES, lambda s, r, w: load(s, w, True))
                for w in range(RING):
                    sp.wait_ge(y_stored[w], TILES // RING * 16)
                for b in range(B):
                    for k in range(2):
                        lo = (k * B + b) * S
                        sp.dma_start(y_got[k][:, b * TB:(b + 1) * TB, :],
                                     y_rows[lo:lo + S, :].rearrange("(t p) d -> p t d", p=P)).then_inc(gathered[b], 16)
                for b in range(B):
                    sp.wait_ge(xn_ready[4], (b + 1) * TB)
                    sp.dma_start(out[b].rearrange("(t p) d -> p t d", p=P), y_got[0][:, b * TB:(b + 1) * TB, :]).then_inc(out_stored, 16)
                sp.wait_ge(out_stored, B * 16)

            @block.gpsimd
            def _(pool):
                def store(s, r, w):
                    wait_apart(pool, y_done, s + 1)
                    nc.gpsimd.indirect_dma_start(
                        out=y_rows[:, :], out_offset=bass.IndirectOffsetOnAxis(ap=place[w][:, 0:1], axis=0),
                        in_=y_out[w][:, :], in_offset=None).then_inc(y_stored[w], 16)

                in_steps(pool, 0, TILES, store)
                for b in range(B):
                    pool.wait_ge(var_ready[4], b + 1)
                    nc.gpsimd.tensor_tensor(rstd4[:, b, :], var4[:, b, :], m_half[:, :], ALU.pow).then_inc(rstd_ready[4], 1)

            @block.tensor
            def _(pe):
                pe.wait_ge(owner_ready, 1)
                pe.wait_ge(ld_ffn1, (2 + E8) * 16)

                def expert_of(s):
                    return pe.value_load(owner[0:1, bass.ds(s, 1)], min_val=0, max_val=E8 - 1)

                def weights(e, lo, n):
                    return w_all[:, bass.ds(e, 1), lo:lo + n].rearrange("p o n -> p (o n)")

                def turn_in(s, r, w):
                    pe.wait_ge(x_loaded[w], (r + 1) * 16)
                    pe.wait_ge(xe_ready, s)
                    pe.transpose(tail[:, 0:P], x_in[w][:, 0:D], ident[:, :]).then_inc(xt_full, 1)

                held = []

                def up(s, w):
                    e = expert_of(s)
                    held.append(e)
                    pe.wait_ge(xe_ready, s + 1)
                    pe.wait_ge(hid_ready[4], two_back(s))
                    pe.matmul(h1[w], xe[w][:, :], weights(e, 0, HID1), start=True, stop=True).then_inc(h1_ready[4], 1)
                    pe.matmul(h3[w], xe[w][:, :], weights(e, HID1, HID1), start=True, stop=True).then_inc(h3_ready[4], 1)

                def turn_hidden(s, w):
                    pe.wait_ge(hid_ready[4], s + 1)
                    pe.wait_ge(ht_done, s)
                    for f in range(FT):
                        ins = pe.transpose(pv[:, f * P:(f + 1) * P], hid[w][:, f * P:(f + 1) * P], ident[:, :])
                    ins.then_inc(ht_full, 1)

                def go_down(s, w):
                    e = held.pop(0) if len(held) > 2 else expert_of(s)
                    pe.wait_ge(ht_done, s + 1)
                    pe.wait_ge(y_done, s)
                    for f in range(FT):
                        ins = pe.matmul(down[w][:, 0:D], hid_t[w][:, f * P:(f + 1) * P], weights(e, 2 * HID1 + f * D, D),
                                        start=(f == 0), stop=(f == FT - 1))
                    ins.then_inc(down_ready, 1)

                turn_in(0, 0, 0)
                up(0, 0)
                turn_in(1, 0, 1)
                up(1, 1)
                turn_hidden(0, 0)
                turn_in(2, 0, 2)

                def body(s, r, j):
                    w = j % 2
                    if j == 2:
                        held.clear()
                    up(s, w)
                    turn_in(s + 1, r + (j + 1) // RING, (j + 1) % RING)
                    turn_hidden(s - 1, 1 - w)
                    go_down(s - 2, w)

                in_steps(pe, 2, TILES - 2, body)
                body(TILES - 2, TILES // RING - 1, RING - 2)
                up(TILES - 1, 1)
                turn_hidden(TILES - 2, 0)
                go_down(TILES - 3, 1)
                turn_hidden(TILES - 1, 1)
                go_down(TILES - 2, 0)
                go_down(TILES - 1, 1)

            @block.scalar
            def _(act):
                def silu(s, w):
                    act.wait_ge(h1_ready[4], s + 1)
                    act.wait_ge(hid_ready[4], two_back(s))
                    nc.scalar.activation(sil[w][:, :], h1[w], ACT.Silu).then_inc(silu_ready[4], 1)

                def copy_turned(s, w):
                    act.wait_ge(ht_full, s + 1)
                    act.wait_ge(down_ready, two_back(s))
                    nc.scalar.copy(hid_t[w][:, :], pv[:, :]).then_inc(ht_done, 1)

                silu(0, 0)
                silu(1, 1)
                copy_turned(0, 0)

                def body(s, r, j):
                    w = j % 2
                    silu(s, w)
                    copy_turned(s - 1, 1 - w)

                in_steps(act, 2, TILES, body)
                copy_turned(TILES - 1, 1)

            @block.vector
            def _(dve):
                dve.wait_ge(owner_ready, 1)
                dve.wait_ge(ld_gate, 2 * 16)
                dve.wait_ge(ld_ffn1, (2 + E8) * 16)

                def shift_in(s, r, j):
                    w = j % 2
                    e = dve.value_load(owner[0:1, bass.ds(s, 1)], min_val=0, max_val=E8 - 1)
                    dve.wait_ge(xt_full, s + 1)
                    dve.wait_ge(h3_ready[4], two_back(s))
                    nc.vector.tensor_scalar(xe[w][:, :], tail[:, 0:P], dom[:, bass.ds(e, 1)], None, ALU.add)\
                        .then_inc(xe_ready, 1)
                    if not isinstance(r, int) or r:
                        dve.wait_ge(y_stored[j], r * 16)
                    dve.wait_ge(x_loaded[j], (r + 1) * 16)
                    nc.vector.tensor_copy(place[j][:, :], x_in[j][:, D:XW]).then_inc(place_ready, 1)

                def hidden(s, w):
                    dve.wait_ge(silu_ready[4], s + 1)
                    dve.wait_ge(h3_ready[4], s + 1)
                    dve.wait_ge(ht_full, two_back(s))
                    nc.vector.tensor_tensor(hid[w][:, :], sil[w][:, :], h3[w], ALU.mult).then_inc(hid_ready[4], 1)

                def take_down(s, r, j):
                    dve.wait_ge(down_ready, s + 1)
                    if not isinstance(r, int) or r:
                        dve.wait_ge(y_stored[j], r * 16)
                    nc.vector.tensor_copy(y_out[j][:, :], down[j % 2][:, 0:D]).then_inc(y_done, 1)

                shift_in(0, 0, 0)
                shift_in(1, 0, 1)
                hidden(0, 0)
                shift_in(2, 0, 2)
                hidden(1, 1)

                def body(s, r, j):
                    shift_in(s + 1, r + (j + 1) // RING, (j + 1) % RING)
                    take_down(s - 2, r + (j - 2) // RING, (j - 2) % RING)
                    hidden(s, j % 2)

                in_steps(dve, 2, TILES - 2, body)
                last = TILES // RING - 1
                body(TILES - 2, last, RING - 2)
                take_down(TILES - 3, last, RING - 3)
                hidden(TILES - 1, 1)
                take_down(TILES - 2, last, RING - 2)
                take_down(TILES - 1, last, RING - 1)

                def combine(b):
                    total = y_got[0]
                    steps = Steps(dve, step[4], b * COMBINE_STEPS, COMBINE_STEPS)
                    dve.wait_ge(gathered[b], 2 * 16)
                    for n_t in range(b * TB, (b + 1) * TB):
                        steps.did(nc.vector.scalar_tensor_tensor(total[:, n_t, :], total[:, n_t, :], gate[:, 0, n_t:n_t + 1],
                                                                 x_tok[:, n_t, :], ALU.mult, ALU.add))
                    steps.settle()
                    for n_t in range(b * TB, (b + 1) * TB):
                        steps.did(nc.vector.scalar_tensor_tensor(total[:, n_t, :], y_got[1][:, n_t, :], gate[:, 1, n_t:n_t + 1],
                                                                 total[:, n_t, :], ALU.mult, ALU.add))
                    steps.settle()
                    for t in range(TB):
                        steps.did(nc.vector.bn_stats(stats4[:, b, t, :], total[:, b * TB + t, :]))
                    steps.settle()
                    for t in range(TB):
                        steps.did(nc.vector.bn_aggr(mv4[:, b, t, :], stats4[:, b, t, :]))
                    steps.settle()
                    nc.vector.tensor_scalar(var4[:, b, :], mv4[:, b, :, 1], LN_EPS, None, ALU.add).then_inc(var_ready[4], 1)
                    steps.close()

                def scale_rows(b):
                    dve.wait_ge(rstd_ready[4], b + 1)
                    for t in range(TB):
                        row = y_got[0][:, b * TB + t, :]
                        nc.vector.tensor_scalar(row, row, mv4[:, b, t, 0:1], rstd4[:, b, t:t + 1],
                                                ALU.subtract, ALU.mult).then_inc(xn_ready[4], 1)

                for b in range(B):
                    combine(b)
                    if b:
                        scale_rows(b - 1)
                scale_rows(B - 1)


def _constants():
    inv = np.float32(THETA) ** (-np.arange(0, DR, 2, dtype=np.float32) / np.float32(DR))
    ang = np.arange(S, dtype=np.float32)[:, None] * inv.astype(np.float32)
    row = np.arange(P) // H % DR
    cos = np.cos(ang).astype(np.float32).T[row // 2]
    sin = np.sin(ang).astype(np.float32).T[row // 2] * np.where(row % 2 == 0, -1, 1).astype(np.float32)[:, None]
    tri = np.triu(np.ones((P, P), np.float32))
    pair_sel = np.zeros((E8, RP, P), np.float32)
    for e in range(E8):
        pair_sel[e, e // 2, HID0 * (e % 2):HID0 * (e % 2 + 1)] = 1
    blank_rows = np.zeros((2 * E8 * P, XW), np.float32)
    blank_rows[:, D] = 2 * B * S + np.arange(2 * E8 * P)
    ids = np.add.outer(np.arange(P), [[(k * B - 1) * S + t * P for t in range(TB)] for k in range(2)]).astype(np.float32)
    return {
        "blank_rows": blank_rows, "ids": ids,
        "cos": cos, "sin": sin, "ident": np.eye(P, dtype=np.float32), "tri": np.tile(tri, (1, 2)),
        "iota8": np.tile(np.arange(E8, dtype=np.float32), (P, TB)), "pair_sel": np.tile(pair_sel, (3, 1, 1)),
        "before_tri": np.triu(np.ones((P, P), np.float32), 1),
        "tile_no": np.tile(np.arange(TILES, dtype=np.float32), (P, 1)),
        "thr": np.tile(np.arange(B * TB, dtype=np.float32) * P, (P, 1)),
        "region": np.tile(np.arange(E8, dtype=np.float32) * REGION, (P, 1)),
        "trem": np.tile(np.float32(S) - np.arange(1, S + 1, dtype=np.float32), (P, 1)),
    }


def _lay_out(i):
    x = i["L0_attn_x"].reshape(B * S, D)
    swap = np.arange(DR) ^ 1
    qr = i["L0_attn_W_QR"].reshape(DL, H, DR)
    kr = i["L0_attn_W_KR"]

    def feature_major(w, width):
        return w.reshape(w.shape[0], H, width).transpose(0, 2, 1).reshape(w.shape[0], H * width)

    def pairs_up(routed, shared):
        w = np.concatenate([routed, shared])
        return w.transpose(1, 0, 2).reshape(D, PAIRS, P)

    w2 = np.concatenate([i["L0_ffn_routed_w2"], i["L0_ffn_shared_w2"]])
    return {
        "x_tok": x, "x_feat": x.T,
        "wdq": i["L0_attn_W_DQ"].T, "wdkv": i["L0_attn_W_DKV"].T,
        "wuq": np.concatenate([feature_major(i["L0_attn_W_UQ"], DH), feature_major(i["L0_attn_W_QR"], DR),
                               feature_major(qr[:, :, swap].reshape(DL, H * DR), DR)], axis=1),
        "wukv": np.concatenate([feature_major(i["L0_attn_W_UK"], DH), i["L0_attn_W_UV"]], axis=1),
        "wkr_a": np.repeat(kr, H, axis=1), "wkr_b": np.repeat(kr[:, swap], H, axis=1),
        "w_o": i["L0_attn_W_O"],
        "r0_w": i["L0_ffn_router_w"], "r0_b": np.tile(i["L0_ffn_router_b"], (P, TB)),
        "w1_0": pairs_up(i["L0_ffn_routed_w1"], i["L0_ffn_shared_w1"]),
        "w3_0": pairs_up(i["L0_ffn_routed_w3"], i["L0_ffn_shared_w3"]),
        "w2_0": w2.reshape(PAIRS, P, D).transpose(1, 0, 2),
        "wk": i["L1_attn_Wk"].T, "wv": i["L1_attn_Wv"].T, "wr": i["L1_attn_Wr"].T,
        "w_out": i["L1_attn_Wo"].T.reshape(CT, P, D).transpose(1, 0, 2),
        "cols": np.stack([i[n].reshape(CT, P).T for n in
                          ("L1_attn_bk", "L1_attn_bv", "L1_attn_br", "L1_attn_time_decay", "L1_attn_U")], axis=1),
        "bo": np.tile(i["L1_attn_bo"], (P, TB, 1)),
        "g_w": i["L1_ffn_gate_w"], "dom": i["L1_ffn_dom"].T,
        "w1_1": i["L1_ffn_W1"], "w3_1": i["L1_ffn_W3"], "w2_1": i["L1_ffn_W2"],
    }


def kernel(**inputs):
    import concourse.bacc as bacc
    from concourse.bass_utils import run_bass_kernel_spmd as run

    arrays = _lay_out({k: np.asarray(v) for k, v in inputs.items()})
    arrays.update(_constants())
    nc = bacc.Bacc("TRN2", target_bir_lowering=False, num_devices=1)
    feed, aps = {}, {}
    for name, value in arrays.items():
        value = np.ascontiguousarray(value)
        feed["in_" + name] = value
        aps[name] = nc.dram_tensor("in_" + name, value.shape, mybir.dt.from_np(value.dtype), kind="ExternalInput").ap()
    out = nc.dram_tensor("out", (B, S, D), F32, kind="ExternalOutput").ap()
    network(nc, aps, out)
    return run(nc, [feed], core_ids=[0]).results[0]["out"]
```
